# Optimizing a Trainium2 kernel written in Bass

```python
import numpy as np
import jax
import jax.numpy as jnp

def _softmax(x, axis=-1):
    return jax.nn.softmax(x, axis=axis)

def _gelu(x):
    return jax.nn.gelu(x, approximate=True)

def _silu(x):
    return jax.nn.silu(x)

def _sigmoid(x):
    return jax.nn.sigmoid(x)

def _layernorm(x, axis=-1, eps=1e-05):
    m = jnp.mean(x, axis=axis, keepdims=True)
    v = jnp.var(x, axis=axis, keepdims=True)
    return (x - m) / jnp.sqrt(v + eps)

def _scatter_add(tgt, idx, src, axis=0):
    return tgt.at[idx].add(src)

def _segment_sum(src, seg, n):
    return jax.ops.segment_sum(src, seg, n)
kernel_name = 'mk_gps_d1_gnn_r16_1ee476'

def setup_inputs(seed: int=0):
    np.random.seed(seed)
    _w = jnp.asarray

    def _rec_inputs():
        import jax
        import jax.numpy as jnp
        _gk = jax.random.key(seed)
        x = -8.776e-05 + 1 * jax.random.normal(jax.random.fold_in(_gk, 1), (625, 512), jnp.float32)
        src = jax.random.randint(jax.random.fold_in(_gk, 2), (10000,), 0, 625, jnp.int32)
        dst = jax.random.randint(jax.random.fold_in(_gk, 3), (10000,), 0, 625, jnp.int32)
        _o = jnp.argsort(dst, stable=True)
        src = src[_o]
        dst = dst[_o]
        edge_type_2 = jax.random.randint(jax.random.fold_in(_gk, 12), (10000,), 0, 2, jnp.int32)
        return (x, src, dst, edge_type_2)
    x, src, dst, edge_type_2 = _rec_inputs()

    def _L0_gnn_setup():
        import jax, jax.numpy as jnp
        import numpy as np
        NUM_RELATIONS = 2
        NUM_BASES = 30
        HIDDEN = 512
        N_NODES = 625
        N_EDGES = 10000

        def rgcn_gate_layer(x, row, col, edge_type, basis, att, gate_w, root, bias):
            H = x.shape[1]
            w = jnp.einsum('rb,bio->rio', att, basis)
            x_j = x[col]
            msgs = []
            for r in range(NUM_RELATIONS):
                gate = jax.nn.sigmoid(x_j @ gate_w[r, :, 0])
                msgs.append(gate[:, None] * x_j @ w[r])
            msg = jnp.where((edge_type == 0)[:, None], msgs[0], msgs[1])
            agg = jax.ops.segment_sum(msg, row, num_segments=x.shape[0])
            return agg + x @ root + bias
        key = jax.random.key(seed)
        ks = jax.random.split(key, 16)
        H, R, B = (HIDDEN, NUM_RELATIONS, NUM_BASES)
        bound = 1.0 / np.sqrt(B * H)
        u = lambda k, shape: jax.random.uniform(k, shape, jnp.float32, -bound, bound)
        inp = {'x': jax.random.normal(ks[0], (N_NODES, H), jnp.float32), 'edge_index': jax.random.randint(ks[1], (2, N_EDGES), 0, N_NODES, jnp.int32), 'edge_type': jax.random.randint(ks[2], (N_EDGES,), 0, R, jnp.int32), 'basis1': u(ks[3], (B, H, H)), 'att1': u(ks[4], (R, B)), 'gate_w1': u(ks[5], (R, H, 1)), 'root1': u(ks[6], (H, H)), 'bias1': u(ks[7], (H,)), 'basis2': u(ks[8], (B, H, H)), 'att2': u(ks[9], (R, B)), 'gate_w2': u(ks[10], (R, H, 1)), 'root2': u(ks[11], (H, H)), 'bias2': u(ks[12], (H,))}
        return inp
    _L0_gnn_all = _L0_gnn_setup()
    _L0_gnn_in = {k: v for k, v in _L0_gnn_all.items() if k in ('basis1', 'att1', 'gate_w1', 'root1', 'bias1', 'basis2', 'att2', 'gate_w2', 'root2', 'bias2')}
    del _L0_gnn_all

    def _L0_mix_setup():
        import jax, jax.numpy as jnp
        import numpy as np
        BATCH, SEQ, D_MODEL = (16, 196, 512)
        M = 256

        def _ln(x, g, b, eps=1e-05):
            mu = jnp.mean(x, axis=-1, keepdims=True)
            var = jnp.mean(jnp.square(x - mu), axis=-1, keepdims=True)
            return (x - mu) / jnp.sqrt(var + eps) * g + b

        def _prm_exp(x, w):
            m = w.shape[0]
            xd = jnp.sum(x * x, axis=-1, keepdims=True) / 2.0
            wtd = jnp.einsum('btd,md->btm', x, w)
            return jnp.exp(wtd - xd) / np.sqrt(m).astype(np.float32)
        key = jax.random.key(seed)
        ks = jax.random.split(key, 8)
        d, m = (D_MODEL, M)
        x = jax.random.normal(ks[0], (BATCH, SEQ, d), dtype=jnp.float32)
        q_mat, _ = jnp.linalg.qr(jax.random.normal(ks[1], (d, m), dtype=jnp.float32))
        w = q_mat.T * np.sqrt(m).astype(np.float32)
        Wkqv = jax.random.normal(ks[2], (d, 3 * d), dtype=jnp.float32) * 0.02
        bkqv = jnp.zeros((3 * d,), jnp.float32)
        Wo = jax.random.normal(ks[3], (d, d), dtype=jnp.float32) * 0.02
        bo = jnp.zeros((d,), jnp.float32)
        W1 = jax.random.normal(ks[4], (d, d), dtype=jnp.float32) * 0.02
        b1 = jnp.zeros((d,), jnp.float32)
        W2 = jax.random.normal(ks[5], (d, d), dtype=jnp.float32) * 0.02
        b2 = jnp.zeros((d,), jnp.float32)
        g1 = jnp.ones((d,), jnp.float32)
        be1 = jnp.zeros((d,), jnp.float32)
        g2 = jnp.ones((d,), jnp.float32)
        be2 = jnp.zeros((d,), jnp.float32)
        return dict(x=x, w=w, Wkqv=Wkqv, bkqv=bkqv, Wo=Wo, bo=bo, W1=W1, b1=b1, W2=W2, b2=b2, g1=g1, be1=be1, g2=g2, be2=be2)
    _L0_mix_all = _L0_mix_setup()
    _L0_mix_in = {k: v for k, v in _L0_mix_all.items() if k in ('w', 'Wkqv', 'bkqv', 'Wo', 'bo', 'W1', 'b1', 'W2', 'b2', 'g1', 'be1', 'g2', 'be2')}
    del _L0_mix_all

    def _L0_ffn_setup():
        import math
        import jax, jax.numpy as jnp
        import numpy as np
        B, T, D, FF, E = (32, 1024, 512, 128, 8)
        CAPACITY_FACTOR = 1.25
        CAP = int(math.ceil(CAPACITY_FACTOR * B * T / E))

        def _bank_residual(x2, Wr, br, W1, b1, W2, b2):
            N, d = x2.shape
            e = Wr.shape[1]
            logits = x2 @ Wr + br
            probs = jax.nn.softmax(logits, axis=-1)
            expert = jnp.argmax(probs, axis=-1)
            gate = jnp.take_along_axis(probs, expert[:, None], axis=-1)[:, 0]
            oneh = jax.nn.one_hot(expert, e, dtype=x2.dtype)
            pos = (jnp.cumsum(oneh, axis=0) * oneh).sum(-1).astype(jnp.int32) - 1
            keep = pos < CAP
            slot = expert.astype(jnp.int32) * CAP + jnp.minimum(pos, CAP - 1)
            xd = jnp.where(keep[:, None], x2, 0.0)
            buf = jnp.zeros((e * CAP, d), x2.dtype).at[slot].add(xd)
            buf = buf.reshape(e, CAP, d)
            h = jax.nn.gelu(jnp.einsum('ecd,edf->ecf', buf, W1) + b1[:, None, :], approximate=False)
            out = jnp.einsum('ecf,efd->ecd', h, W2) + b2[:, None, :]
            y = out.reshape(e * CAP, d)[slot]
            return y * (gate * keep.astype(x2.dtype))[:, None]
        key = jax.random.key(seed)
        ks = jax.random.split(key, 18)
        s = 0.02
        inp = {'x': jax.random.normal(ks[0], (B, T, D), dtype=jnp.float32), 'Wr_sp': jax.random.normal(ks[1], (D, E)) * s, 'br_sp': jnp.zeros((E,), jnp.float32), 'Wr_fq': jax.random.normal(ks[2], (D, E)) * s, 'br_fq': jnp.zeros((E,), jnp.float32), 'Ws1': jax.random.normal(ks[3], (D, FF)) * s, 'bs1': jnp.zeros((FF,), jnp.float32), 'Ws2': jax.random.normal(ks[4], (FF, D)) * s, 'bs2': jnp.zeros((D,), jnp.float32), 'W1_sp': jax.random.normal(ks[5], (E, D, FF)) * s, 'b1_sp': jnp.zeros((E, FF), jnp.float32), 'W2_sp': jax.random.normal(ks[6], (E, FF, D)) * s, 'b2_sp': jnp.zeros((E, D), jnp.float32), 'W1_fq': jax.random.normal(ks[7], (E, D, FF)) * s, 'b1_fq': jnp.zeros((E, FF), jnp.float32), 'W2_fq': jax.random.normal(ks[8], (E, FF, D)) * s, 'b2_fq': jnp.zeros((E, D), jnp.float32)}
        return inp
    _L0_ffn_all = _L0_ffn_setup()
    _L0_ffn_in = {k: v for k, v in _L0_ffn_all.items() if k in ('Wr_sp', 'br_sp', 'Wr_fq', 'br_fq', 'Ws1', 'bs1', 'Ws2', 'bs2', 'W1_sp', 'b1_sp', 'W2_sp', 'b2_sp', 'W1_fq', 'b1_fq', 'W2_fq', 'b2_fq')}
    del _L0_ffn_all
    return {'x': x, 'src': src, 'dst': dst, 'edge_type_2': edge_type_2, 'L0_gnn_basis1': _L0_gnn_in['basis1'], 'L0_gnn_att1': _L0_gnn_in['att1'], 'L0_gnn_gate_w1': _L0_gnn_in['gate_w1'], 'L0_gnn_root1': _L0_gnn_in['root1'], 'L0_gnn_bias1': _L0_gnn_in['bias1'], 'L0_gnn_basis2': _L0_gnn_in['basis2'], 'L0_gnn_att2': _L0_gnn_in['att2'], 'L0_gnn_gate_w2': _L0_gnn_in['gate_w2'], 'L0_gnn_root2': _L0_gnn_in['root2'], 'L0_gnn_bias2': _L0_gnn_in['bias2'], 'L0_mix_w': _L0_mix_in['w'], 'L0_mix_Wkqv': _L0_mix_in['Wkqv'], 'L0_mix_bkqv': _L0_mix_in['bkqv'], 'L0_mix_Wo': _L0_mix_in['Wo'], 'L0_mix_bo': _L0_mix_in['bo'], 'L0_mix_W1': _L0_mix_in['W1'], 'L0_mix_b1': _L0_mix_in['b1'], 'L0_mix_W2': _L0_mix_in['W2'], 'L0_mix_b2': _L0_mix_in['b2'], 'L0_mix_g1': _L0_mix_in['g1'], 'L0_mix_be1': _L0_mix_in['be1'], 'L0_mix_g2': _L0_mix_in['g2'], 'L0_mix_be2': _L0_mix_in['be2'], 'L0_ffn_Wr_sp': _L0_ffn_in['Wr_sp'], 'L0_ffn_br_sp': _L0_ffn_in['br_sp'], 'L0_ffn_Wr_fq': _L0_ffn_in['Wr_fq'], 'L0_ffn_br_fq': _L0_ffn_in['br_fq'], 'L0_ffn_Ws1': _L0_ffn_in['Ws1'], 'L0_ffn_bs1': _L0_ffn_in['bs1'], 'L0_ffn_Ws2': _L0_ffn_in['Ws2'], 'L0_ffn_bs2': _L0_ffn_in['bs2'], 'L0_ffn_W1_sp': _L0_ffn_in['W1_sp'], 'L0_ffn_b1_sp': _L0_ffn_in['b1_sp'], 'L0_ffn_W2_sp': _L0_ffn_in['W2_sp'], 'L0_ffn_b2_sp': _L0_ffn_in['b2_sp'], 'L0_ffn_W1_fq': _L0_ffn_in['W1_fq'], 'L0_ffn_b1_fq': _L0_ffn_in['b1_fq'], 'L0_ffn_W2_fq': _L0_ffn_in['W2_fq'], 'L0_ffn_b2_fq': _L0_ffn_in['b2_fq']}

def reference(x, src, dst, edge_type_2, L0_gnn_basis1, L0_gnn_att1, L0_gnn_gate_w1, L0_gnn_root1, L0_gnn_bias1, L0_gnn_basis2, L0_gnn_att2, L0_gnn_gate_w2, L0_gnn_root2, L0_gnn_bias2, L0_mix_w, L0_mix_Wkqv, L0_mix_bkqv, L0_mix_Wo, L0_mix_bo, L0_mix_W1, L0_mix_b1, L0_mix_W2, L0_mix_b2, L0_mix_g1, L0_mix_be1, L0_mix_g2, L0_mix_be2, L0_ffn_Wr_sp, L0_ffn_br_sp, L0_ffn_Wr_fq, L0_ffn_br_fq, L0_ffn_Ws1, L0_ffn_bs1, L0_ffn_Ws2, L0_ffn_bs2, L0_ffn_W1_sp, L0_ffn_b1_sp, L0_ffn_W2_sp, L0_ffn_b2_sp, L0_ffn_W1_fq, L0_ffn_b1_fq, L0_ffn_W2_fq, L0_ffn_b2_fq):
    import jax
    import jax.numpy as jnp

    def _L0_gnn_ref(x, edge_index, edge_type, basis1, att1, gate_w1, root1, bias1, basis2, att2, gate_w2, root2, bias2):
        import jax, jax.numpy as jnp
        import numpy as np
        NUM_RELATIONS = 2
        NUM_BASES = 30
        HIDDEN = 512
        N_NODES = 625
        N_EDGES = 10000

        def rgcn_gate_layer(x, row, col, edge_type, basis, att, gate_w, root, bias):
            H = x.shape[1]
            w = jnp.einsum('rb,bio->rio', att, basis)
            x_j = x[col]
            msgs = []
            for r in range(NUM_RELATIONS):
                gate = jax.nn.sigmoid(x_j @ gate_w[r, :, 0])
                msgs.append(gate[:, None] * x_j @ w[r])
            msg = jnp.where((edge_type == 0)[:, None], msgs[0], msgs[1])
            agg = jax.ops.segment_sum(msg, row, num_segments=x.shape[0])
            return agg + x @ root + bias
        row, col = (edge_index[0], edge_index[1])
        h = jax.nn.relu(rgcn_gate_layer(x, row, col, edge_type, basis1, att1, gate_w1, root1, bias1))
        out = rgcn_gate_layer(h, row, col, edge_type, basis2, att2, gate_w2, root2, bias2)
        return out

    def _L0_mix_ref(x, w, Wkqv, bkqv, Wo, bo, W1, b1, W2, b2, g1, be1, g2, be2):
        import jax, jax.numpy as jnp
        import numpy as np
        BATCH, SEQ, D_MODEL = (16, 196, 512)
        M = 256

        def _ln(x, g, b, eps=1e-05):
            mu = jnp.mean(x, axis=-1, keepdims=True)
            var = jnp.mean(jnp.square(x - mu), axis=-1, keepdims=True)
            return (x - mu) / jnp.sqrt(var + eps) * g + b

        def _prm_exp(x, w):
            m = w.shape[0]
            xd = jnp.sum(x * x, axis=-1, keepdims=True) / 2.0
            wtd = jnp.einsum('btd,md->btm', x, w)
            return jnp.exp(wtd - xd) / np.sqrt(m).astype(np.float32)
        eps = 1e-08
        xn = _ln(x, g1, be1)
        kqv = xn @ Wkqv + bkqv
        k, q, v = jnp.split(kqv, 3, axis=-1)
        kp = _prm_exp(k, w)
        qp = _prm_exp(q, w)
        D = jnp.einsum('btm,bm->bt', qp, jnp.sum(kp, axis=1))[..., None]
        kptv = jnp.einsum('btn,btm->bnm', v, kp)
        y = jnp.einsum('btm,bnm->btn', qp, kptv) / (D + eps)
        y = v + (y @ Wo + bo)
        h = _ln(y, g2, be2)
        h = jax.nn.gelu(h @ W1 + b1, approximate=False) @ W2 + b2
        return y + h

    def _L0_ffn_ref(x, Wr_sp, br_sp, Wr_fq, br_fq, Ws1, bs1, Ws2, bs2, W1_sp, b1_sp, W2_sp, b2_sp, W1_fq, b1_fq, W2_fq, b2_fq):
        import math
        import jax, jax.numpy as jnp
        import numpy as np
        B, T, D, FF, E = (32, 1024, 512, 128, 8)
        CAPACITY_FACTOR = 1.25
        CAP = int(math.ceil(CAPACITY_FACTOR * B * T / E))

        def _bank_residual(x2, Wr, br, W1, b1, W2, b2):
            N, d = x2.shape
            e = Wr.shape[1]
            logits = x2 @ Wr + br
            probs = jax.nn.softmax(logits, axis=-1)
            expert = jnp.argmax(probs, axis=-1)
            gate = jnp.take_along_axis(probs, expert[:, None], axis=-1)[:, 0]
            oneh = jax.nn.one_hot(expert, e, dtype=x2.dtype)
            pos = (jnp.cumsum(oneh, axis=0) * oneh).sum(-1).astype(jnp.int32) - 1
            keep = pos < CAP
            slot = expert.astype(jnp.int32) * CAP + jnp.minimum(pos, CAP - 1)
            xd = jnp.where(keep[:, None], x2, 0.0)
            buf = jnp.zeros((e * CAP, d), x2.dtype).at[slot].add(xd)
            buf = buf.reshape(e, CAP, d)
            h = jax.nn.gelu(jnp.einsum('ecd,edf->ecf', buf, W1) + b1[:, None, :], approximate=False)
            out = jnp.einsum('ecf,efd->ecd', h, W2) + b2[:, None, :]
            y = out.reshape(e * CAP, d)[slot]
            return y * (gate * keep.astype(x2.dtype))[:, None]
        b, t, d = x.shape
        x2 = x.reshape(b * t, d)
        shared = jax.nn.gelu(x2 @ Ws1 + bs1, approximate=False) @ Ws2 + bs2
        y = shared
        y = y + _bank_residual(x2, Wr_sp, br_sp, W1_sp, b1_sp, W2_sp, b2_sp)
        y = y + _bank_residual(x2, Wr_fq, br_fq, W1_fq, b1_fq, W2_fq, b2_fq)
        return y.reshape(b, t, d)
    edge_index = jnp.stack([src, dst])
    xn = _layernorm(x, axis=-1)
    x = x + _L0_gnn_ref(xn, edge_index, edge_type_2, L0_gnn_basis1, L0_gnn_att1, L0_gnn_gate_w1, L0_gnn_root1, L0_gnn_bias1, L0_gnn_basis2, L0_gnn_att2, L0_gnn_gate_w2, L0_gnn_root2, L0_gnn_bias2) + _L0_mix_ref(xn[None], L0_mix_w, L0_mix_Wkqv, L0_mix_bkqv, L0_mix_Wo, L0_mix_bo, L0_mix_W1, L0_mix_b1, L0_mix_W2, L0_mix_b2, L0_mix_g1, L0_mix_be1, L0_mix_g2, L0_mix_be2)[0]
    x = x + _L0_ffn_ref(_layernorm(x, axis=-1)[None], L0_ffn_Wr_sp, L0_ffn_br_sp, L0_ffn_Wr_fq, L0_ffn_br_fq, L0_ffn_Ws1, L0_ffn_bs1, L0_ffn_Ws2, L0_ffn_bs2, L0_ffn_W1_sp, L0_ffn_b1_sp, L0_ffn_W2_sp, L0_ffn_b2_sp, L0_ffn_W1_fq, L0_ffn_b1_fq, L0_ffn_W2_fq, L0_ffn_b2_fq)[0]
    return x

_drawn_inputs = setup_inputs


def setup_inputs(seed=0):
    import zlib

    import numpy as np

    out = dict(_drawn_inputs(seed))
    spreads = {'L0_mix_bkqv': (0.0, 0.1),
     'L0_mix_bo': (0.0, 0.1),
     'L0_mix_b1': (0.0, 0.311),
     'L0_mix_b2': (0.0, 0.1),
     'L0_mix_g1': (1.0, 0.2),
     'L0_mix_be1': (0.0, 0.1),
     'L0_mix_g2': (1.0, 0.6),
     'L0_mix_be2': (0.0, 0.697),
     'L0_ffn_br_sp': (0.0, 0.641),
     'L0_ffn_br_fq': (0.0, 0.698),
     'L0_ffn_bs1': (0.0, 0.684),
     'L0_ffn_bs2': (0.0, 0.1),
     'L0_ffn_b1_sp': (0.0, 0.8),
     'L0_ffn_b2_sp': (0.0, 0.389),
     'L0_ffn_b1_fq': (0.0, 0.8),
     'L0_ffn_b2_fq': (0.0, 0.393)}
    factors = {'L0_gnn_basis1': 8.0,
     'L0_gnn_att1': 8.0,
     'L0_gnn_gate_w1': 8.0,
     'L0_gnn_root1': 8.0,
     'L0_gnn_bias1': 8.0,
     'L0_gnn_basis2': 8.0,
     'L0_gnn_att2': 8.0,
     'L0_gnn_gate_w2': 8.0,
     'L0_gnn_root2': 7.801,
     'L0_gnn_bias2': 8.0,
     'L0_ffn_W1_sp': 4.953,
     'L0_ffn_W2_sp': 4.653,
     'L0_ffn_W1_fq': 5.019,
     'L0_ffn_W2_fq': 4.721}
    for name, (base, spread) in spreads.items():
        noise = np.random.default_rng([zlib.crc32(name.encode()), seed]).standard_normal(out[name].shape)
        drawn = base * np.exp(spread * noise) if base else spread * noise
        out[name] = jnp.asarray(drawn.astype(out[name].dtype))
    for name, factor in factors.items():
        out[name] = (out[name] * factor).astype(out[name].dtype)
    return out
```

```python
from contextlib import ExitStack

import concourse.bass as bass
from concourse import mybir

F32, F32R, F16 = mybir.dt.float32, mybir.dt.float32r, mybir.dt.float16
I32, I16 = mybir.dt.int32, mybir.dt.int16
ALU, ACT, AX = mybir.AluOpType, mybir.ActivationFunctionType, mybir.AxisListType
RMAX = bass.bass_isa.ReduceOp.max

NODES, D = 625, 512
NT, TP = 5, 125
NPAD, HALF = 628, 314
KT = D // 128
EDGES, ET, TE = 10000, 80, 125
CW = 626
CB = 418
REL, BASES = 2, 30
GB = 8
NG = (BASES + GB - 1) // GB
QI = 16
CHUNKS = D // QI // 4
M = 256
E, FF = 8, 128
BANK = 512


def gnn_mix_ffn(nc, x, src, dst, edge_type, basis1, att1, gate_w1, root1, bias1, basis2, att2, gate_w2,
                root2, bias2, w, Wkqv, bkqv, Wo, bo, W1, b1, W2, b2, g1, be1, g2, be2, Wr_sp, br_sp,
                Wr_fq, br_fq, Ws1, bs1, Ws2, bs2, W1_sp, b1_sp, W2_sp, b2_sp, W1_fq, b1_fq, W2_fq,
                b2_fq, out):
    with ExitStack() as ctx:
        def sem(name):
            return ctx.enter_context(nc.semaphore(name))

        top = [16512]

        def region(size):
            at = top[0]
            top[0] += -(-size // 32) * 32
            assert top[0] <= 229344, top[0]
            return at

        def place(name, shape, dtype, at):
            return nc.alloc_sbuf_tensor_at(name, shape, dtype, offset=-(-at // 32) * 32)

        def own(name, shape, dtype=F32):
            n = {F32: 4, F32R: 4, I32: 4, F16: 2, I16: 2}[dtype]
            for s in shape[1:]:
                n *= s
            return place(name, shape, dtype, region(n))

        ident = own("ident", [128, 128])
        colv = own("colv", [128, 45])
        bias_row = own("bias_row", [128, 6, D])
        gate_hi = own("gate_hi", [128, 2, KT, REL], F32R)
        gate_lo = own("gate_lo", [128, 2, KT, REL], F32R)
        att_col = own("att_col", [128, 2, NG, REL])
        sel_q = own("sel_q", [128, QI])
        sel_att = own("sel_att", [128, 2, NG, REL, QI])
        gates = own("gates", [TP, NT, REL])
        bn = own("bn", [TP, NT, 6])
        stat = own("stat", [TP, NT, 2])
        veps = own("veps", [TP, NT])
        rstd = own("rstd", [TP, NT])
        neg_half_pow = own("neg_half_pow", [TP, NT])
        neg_half = own("neg_half", [128, 1])
        ones = own("ones", [128, 1])
        xd = own("xd", [TP, NT])
        ksum = own("ksum", [128, 2])
        rec = own("rec", [TP, NT])
        range_i = own("range_i", [1, 2, NT], I32)

        KB628, KB512 = KT * NPAD * 4, NT * D * 4
        counts = own("counts", [TP, NT, REL * CW], I16)
        r_ring = region(4 * 8192)
        r_split = region(4 * 8192)
        stag = own("stag", [128, 2, D])
        r_wraw = region(KT * REL * D * 4)
        r_raw = region(2 * KT * D * 4)
        r_ht = region(2 * KB628)
        r_h1t = region(KB512)
        r_u = region(2 * KB512)
        r_cf = region(NT * CW * 4)
        r_extra = region(18720)

        ring0 = place("ring0", [128, 8, 4 * D], F32, r_ring)
        ring1 = place("ring1", [128, 4, 4 * D], F32, r_ring)
        xa = place("xa", [TP, NT, D], F32, r_u)
        xn = place("xn", [TP, NT, D], F32, r_h1t)
        xn2 = place("xn2", [TP, NT, D], F32, r_extra)
        gate_rows = place("gate_rows", [REL, 2, D], F32, r_wraw)
        att_rep = place("att_rep", [REL, 2, BASES * QI], F32, r_wraw + 8448)
        att_rows = place("att_rows", [REL, 2, BASES], F32, r_wraw + 8192)
        row_vec = place("row_vec", [45, 128], F32, r_wraw + 4096)
        oh_n = place("oh_n", [TE, 4, REL * CW], F16, r_cf)
        oh_m = place("oh_m", [TE, 4, TE], F16, r_cf + 4 * REL * CW * 2)
        zeros = place("zeros", [TE, TE], F16, r_cf + 4 * REL * CW * 2 + 4 * TE * 2)
        o = r_u + KB512
        iota_n = place("iota_n", [TE, REL * CW], F16, o)
        keys = place("keys", [TE, 2, ET], F32, o + 2528)
        key_m = place("key_m", [TE, NT, ET], F32, o + 3200)
        edge_i = place("edge_i", [ET, 3, TE], I32, o + 4800)
        edge_f = place("edge_f", [ET, 3, TE], F32, o + 6304)
        key_n = place("key_n", [ET, TE], F32, o + 7808)
        o += 8320
        mnmx = place("mnmx", [ET, 2], F32, o)
        tile_id = place("tile_id", [ET, 2, NT], F32, o + 32)
        tile_ii = place("tile_ii", [ET, 2, NT], I32, o + 96)
        node_lo = place("node_lo", [ET, NT], F32, o + 160)
        in_lo = place("in_lo", [ET, NT], F32, o + 192)
        in_hi = place("in_hi", [ET, NT], F32, o + 224)
        bound = place("bound", [ET, 2, NT], F32, o + 256)
        bound_all = place("bound_all", [ET, 2, NT], F32, o + 320)
        range_f = place("range_f", [1, 2, NT], F32, o + 384)
        w_raw = place("w_raw", [128, KT, REL, D], F32, r_wraw)
        piece_raw = [place(f"piece_raw{i}", [128, KT, D], F32, r_raw + i * KT * D * 4) for i in range(2)]
        piece_hi = [place(f"piece_hi{i}", [128, KT, D], F32R, r_split + i * 16384) for i in range(2)]
        piece_lo = [place(f"piece_lo{i}", [128, KT, D], F32R, r_split + i * 16384 + 8192) for i in range(2)]
        ht_hi = [place(f"ht_hi{l}", [128, KT, NPAD], F32R, r_ht) for l in range(2)]
        ht_lo = [place(f"ht_lo{l}", [128, KT, NPAD], F32R, r_ht + KB628) for l in range(2)]
        h1t = place("h1t", [128, KT, NPAD], F32, r_h1t)
        u_at = [r_u, r_ring]
        u_hi = [place(f"u_hi{l}", [TP, NT, D], F32R, u_at[l]) for l in range(2)]
        u_lo = [place(f"u_lo{l}", [TP, NT, D], F32R, u_at[l] + KB512) for l in range(2)]
        cf = place("cf", [TP, NT, CW], F32R, r_cf)
        row_tmp = place("row_tmp", [TP, 2, D], F32, r_extra + 14336)
        xt_hi = place("xt_hi", [128, KT, NPAD], F32R, r_ht)
        xt_lo = place("xt_lo", [128, KT, NPAD], F32R, r_ht + KB628)
        kq_hi = place("kq_hi", [128, KT, NPAD], F32R, r_u)
        kq_lo = place("kq_lo", [128, KT, NPAD], F32R, r_u + KB628)
        y = place("y", [TP, NT, D], F32, r_u)
        v = place("v", [TP, NT, D], F32, r_u + KB512)
        kp = place("kp", [TP, NT, M], F32, r_cf)
        qpt = place("qpt", [128, 2, NPAD], F32, r_cf + 5120)
        wt_hi = place("wt_hi", [128, KT, M], F32R, r_extra + 10240)
        wt_lo = place("wt_lo", [128, KT, M], F32R, r_extra + 10240 + 4096)
        w_nat = place("w_nat", [128, 2, D], F32, r_extra + 0)
        feat = place("feat", [TP, 2, M], F32, r_extra + 4096)
        square = place("square", [128, NPAD], F32, r_extra + 6144)
        xt_tmp = place("xt_tmp", [128, KT, TP], F32, r_cf)
        kv = place("kv", [128, 2, D], F32, r_extra + 10240)
        yt_hi = place("yt_hi", [128, KT, NPAD], F32R, r_ht)
        yt_lo = place("yt_lo", [128, KT, NPAD], F32R, r_ht + KB628)
        x_again = place("x_again", [TP, 2, D], F32, r_extra)
        yn = place("yn", [TP, 2, D], F32, r_extra + 4096)
        h2_tmp = place("h2_tmp", [128, KT, TP], F32, r_extra + 8192)
        h2t_hi = place("h2t_hi", [128, KT, NPAD], F32R, r_ht)
        h2t_lo = place("h2t_lo", [128, KT, NPAD], F32R, r_ht + KB628)
        act_tmp = place("act_tmp", [128, 2, NPAD], F32, r_extra + 10240)
        act_hi = place("act_hi", [128, KT, NPAD], F32R, r_u + KB512)
        act_lo = place("act_lo", [128, KT, NPAD], F32R, r_u + KB512 + KB628)
        x1 = place("x1", [TP, NT, D], F32, r_wraw)
        x1n = place("x1n", [TP, 2, D], F32, r_extra)
        x1t_hi = place("x1t_hi", [128, KT, NPAD], F32R, r_ht)
        x1t_lo = place("x1t_lo", [128, KT, NPAD], F32R, r_ht + KB628)
        router_raw = place("router_raw", [128, KT, 2 * E], F32, r_extra + 4096)
        router_hi = place("router_hi", [128, KT, 2 * E], F32R, r_extra + 4096 + 256)
        router_lo = place("router_lo", [128, KT, 2 * E], F32R, r_extra + 4096 + 512)
        router_b = place("router_b", [TP, 2 * E], F32, r_extra + 4096 + 768)
        o = r_extra + 4096 + 1024
        logit = place("logit", [TP, NT, 2, E], F32, o)
        lmax = place("lmax", [TP, NT, 2], F32, o + 320)
        shifted = place("shifted", [TP, NT, 2, E], F32, o + 384)
        expo = place("expo", [TP, NT, 2, E], F32, o + 704)
        denom = place("denom", [TP, NT, 2], F32, o + 1024)
        gate_p = place("gate_p", [TP, NT, 2], F32, o + 1088)
        rank = place("rank", [TP, NT, 2, E], F32, o + 1152)
        score = place("score", [TP, NT, 2, E], F32, o + 1472)
        best = place("best", [TP, NT, 2], F32, o + 1792)
        route = place("route", [TP, NT, 2, E], F32, o + 1856)
        o += 2208
        route_t = place("route_t", [2 * E, NPAD], F32, o)
        route_hi = place("route_hi", [2 * E, NPAD], F32R, o + 2528)
        route_lo = place("route_lo", [2 * E, NPAD], F32R, o + 2 * 2528)
        o += 3 * 2528
        assert o <= r_extra + 18720
        out_bias = place("out_bias", [2 * E, D], F32, r_raw + 4 * 4096 - 2048)
        out_b_hi = place("out_b_hi", [2 * E, D], F32R, r_wraw + KB512)
        out_b_lo = place("out_b_lo", [2 * E, D], F32R, r_wraw + KB512 + 2048)
        route_all = place("route_all", [128, 2 * E, NPAD], F32, r_h1t)
        assert r_h1t + 2 * E * NPAD * 4 <= r_extra
        XR = 3
        ex_raw = place("ex_raw", [128, XR, 2, D], F32, r_raw)
        ex_hi = place("ex_hi", [128, 4, 2, D], F32R, r_split)
        ex_lo = place("ex_lo", [128, 4, 2, D], F32R, r_split + 16384)
        o = r_ring
        hid = place("hid", [128, 4, HALF], F32, o)
        gated = place("gated", [128, 4, HALF], F32, o + 5024)
        hg_hi = place("hg_hi", [128, 2, NPAD], F32R, o + 10048)
        hg_lo = place("hg_lo", [128, 2, NPAD], F32R, o + 15072)
        final = place("final", [TP, 2, D], F32, r_extra)

        ps = ctx.enter_context(nc.psum_tensor("ps", [128, 8, BANK], F32))
        rel_dram = [nc.dram_tensor(f"rel_dram{l}", (KT, REL, CHUNKS, QI, D), F32, kind="Internal").ap()
                    for l in range(2)]
        route_dram = nc.dram_tensor("route_dram", (2 * E, NPAD), F32, kind="Internal").ap()

        edges_in, x_in, rows_in, smalls_in = sem("edges_in"), sem("x_in"), sem("rows_in"), sem("smalls_in")
        basis_in = [sem(f"basis_in{i}") for i in range(8)]
        raw_in = [sem(f"raw_in{i}") for i in range(2)]
        rel_out = [sem(f"rel_out{i}") for i in range(2)]
        rel_back = [sem(f"rel_back{t}") for t in range(KT)]
        w_in, router_in, route_out, route_back = sem("w_in"), sem("router_in"), sem("route_out"), sem("route_back")
        x_again_in = [sem(f"x_again_in{i}") for i in range(2)]
        out_b_in = sem("out_b_in")
        ex_in = [sem(f"ex_in{i}") for i in range(XR)]
        stored = [sem(f"stored{i}") for i in range(2)]
        ident_zero, ident_ready, iotas_ready, consts_ready = (
            sem("ident_zero"), sem("ident_ready"), sem("iotas_ready"), sem("consts_ready"))
        key_ready, bound_ready, bound_max, keys_t, range_ready = (
            sem("key_ready"), sem("bound_ready"), sem("bound_max"), sem("keys_t"), sem("range_ready"))
        one_hot, pair_used, count_ready = sem("one_hot"), sem("pair_used"), sem("count_ready")
        var_ready, rstd_ready, xn_ready, xn2_ready = sem("var_ready"), sem("rstd_ready"), sem("xn_ready"), sem("xn2_ready")
        cols_t, cols_ready, gate_rows_t, gate_w_hi, gate_w_ready = (
            sem("cols_t"), sem("cols_ready"), sem("gate_rows_t"), sem("gate_w_hi"), sem("gate_w_ready"))
        sel_ready, att_ready = sem("sel_ready"), sem("att_ready")
        hT_t, hT_hi, hT_ready = sem("hT_t"), sem("hT_hi"), sem("hT_ready")
        basis_used, rel_sum, rel_evac = sem("basis_used"), sem("rel_sum"), sem("rel_evac")
        split_done, piece_used = sem("split_done"), sem("piece_used")
        gate_mm, gates_ready = sem("gate_mm"), sem("gates_ready")
        u_mm, u_hi_done, u_ready, cf_ready, rel_applied, agg_done = (
            sem("u_mm"), sem("u_hi_done"), sem("u_ready"), sem("cf_ready"), sem("rel_applied"), sem("agg_done"))
        h_added, h_relu, h1_t, h1t_ready = sem("h_added"), sem("h_relu"), sem("h1_t"), sem("h1t_ready")
        xt_t, xt_scaled, xt_hi_done, xt_ready = sem("xt_t"), sem("xt_scaled"), sem("xt_hi_done"), sem("xt_ready")
        wt_t, wt_hi_done, wt_ready = sem("wt_t"), sem("wt_hi_done"), sem("wt_ready")
        kq_mm, kq_hi_done, sq_ready, kq_ready, sq_used, xd_mm, xd_ready = (
            sem("kq_mm"), sem("kq_hi_done"), sem("sq_ready"), sem("kq_ready"), sem("sq_used"), sem("xd_mm"), sem("xd_ready"))
        feat_mm, feat_exp, feat_ready, qp_t, qpt_ready = (
            sem("feat_mm"), sem("feat_exp"), sem("feat_ready"), sem("qp_t"), sem("qpt_ready"))
        v_mm, v_ready, kv_mm, kv_ready, yt_mm, yt_hi_done, yt_ready, d_mm, rec_ready = (
            sem("v_mm"), sem("v_ready"), sem("kv_mm"), sem("kv_ready"), sem("yt_mm"), sem("yt_hi_done"),
            sem("yt_ready"), sem("d_mm"), sem("rec_ready"))
        wo_mm, y_ready, yn_ready, h2_t, h2_scaled, h2_hi_done, h2t_ready = (
            sem("wo_mm"), sem("y_ready"), sem("yn_ready"), sem("h2_t"), sem("h2_scaled"), sem("h2_hi_done"), sem("h2t_ready"))
        y_plus_b, y_plus_x = sem("y_plus_b"), sem("y_plus_x")
        act_mm, act_done, act_ready, w2_mm, xm_ready, xm_plus_b = (
            sem("act_mm"), sem("act_done"), sem("act_ready"), sem("w2_mm"), sem("xm_ready"), sem("xm_plus_b"))
        x1n_ready, x1_t, x1_hi_done, x1t_ready = (
            sem("x1n_ready"), sem("x1_t"), sem("x1_hi_done"), sem("x1t_ready"))
        router_w_ready, logit_mm, shift_ready, expo_ready, route_ready, route_tr, route_t_ready, route_split = (
            sem("router_w_ready"), sem("logit_mm"), sem("shift_ready"), sem("expo_ready"), sem("route_ready"),
            sem("route_tr"), sem("route_t_ready"), sem("route_split"))
        x1_plus_b = sem("x1_plus_b")
        ex_split, ex_used, hid_mm, hid_ready, hg_ready, ffn_mm, final_ready = (
            sem("ex_split"), sem("ex_used"), sem("hid_mm"), sem("hid_ready"), sem("hg_ready"), sem("ffn_mm"), sem("final_ready"))
        dve_own, act_own, pool_own = sem("dve_own"), sem("act_own"), sem("pool_own")

        basis_rows = [b.rearrange("b (c q t) o -> c b q (t o)", q=QI, t=KT) for b in (basis1, basis2)]
        LOADED = {"root1": 0, "k": 1, "q": 2, "v": 3, "Wo": 4, "W1": 5, "W2": 6, "root2": 7}
        ORDER = ["rel1_0", "root1", "rel1_1", "k", "q", "v", "Wo", "W1", "W2", "rel2_0", "root2", "rel2_1"]
        PIECE = {name: n for n, name in enumerate(ORDER)}
        SPLIT_OF_LOAD = [PIECE[name] for name in LOADED]
        perm = "(p t) n -> p t n"
        nat = "(t p) n -> p t n"
        piece_src = {
            "root1": [root1.rearrange(perm, t=KT)], "root2": [root2.rearrange(perm, t=KT)],
            "k": [Wkqv[:, 0:D].rearrange(nat, p=128)], "q": [Wkqv[:, D:2 * D].rearrange(nat, p=128)],
            "v": [Wkqv[:, 2 * D:3 * D].rearrange(nat, p=128)], "Wo": [Wo.rearrange(nat, p=128)],
            "W1": [W1.rearrange(nat, p=128)], "W2": [W2.rearrange(nat, p=128)]}
        NX = 2 * E + 1
        ex_w1 = [Ws1] + [W1_sp[e] for e in range(E)] + [W1_fq[e] for e in range(E)]
        ex_w2 = [Ws2] + [W2_sp[e] for e in range(E)] + [W2_fq[e] for e in range(E)]
        C_G1, C_BE1, C_G2, C_BE2, C_BK, C_B1, C_EXP = 0, 4, 8, 12, 16, 24, 28

        AGG = [0, 1, 2, 5, 6]
        UB = [7, 4, 3]

        def basis_slots(l):
            return 8 if l == 0 else 4

        def basis_turn(l, i):
            slot = i % basis_slots(l)
            before = 0 if l == 0 else NG * CHUNKS // 8
            return slot, before + i // basis_slots(l) + 1

        def rel_bank(l, ch):
            return 3 + (ch % 2 if l == 0 else 0)

        block = ctx.enter_context(nc.Block())

        @block.sync
        def _(sp):
            for k, a in enumerate((src, dst, edge_type)):
                sp.dma_start(edge_i[:, k, :], a.rearrange("(t e) -> t e", e=TE)).then_inc(edges_in, 16)
            xv = x.rearrange("(t p) n -> p t n", p=TP)
            sp.dma_start(xa[0:120, :, :], xv[0:120]).then_inc(x_in, 16)
            sp.dma_start(xa[120:TP, :, :], xv[120:TP]).then_inc(x_in, 16)
            for l, gw in enumerate((gate_w1, gate_w2)):
                sp.dma_start(gate_rows[:, l, :], gw.rearrange("r i o -> r (i o)")).then_inc(rows_in, 16)
            at = 0
            for a in (g1, be1, g2, be2, bkqv[0:2 * D], b1, bs1):
                n = a.shape[0] // 128
                sp.dma_start(row_vec[at:at + n, :], a.rearrange("(t p) -> t p", p=128)).then_inc(rows_in, 16)
                at += n
            for a in (b1_sp, b1_fq):
                sp.dma_start(row_vec[at:at + E, :], a).then_inc(rows_in, 16)
                at += E
            for l, a in enumerate((att1, att2)):
                sp.dma_start(att_rows[:, l, :], a).then_inc(rows_in, 16)
            for n, a in enumerate((bias1, bias2, bkqv[2 * D:3 * D], bo, b2, bs2)):
                sp.dma_start(bias_row[:, n, :], a.partition_broadcast(128)).then_inc(smalls_in, 16)

            def load_basis(l, i):
                ch, g = divmod(i, NG)
                nb = min(GB, BASES - g * GB)
                slot, _ = basis_turn(l, i)
                ring = (ring0, ring1)[l]
                first = NG * CHUNKS * l
                if l == 0 and i >= 8:
                    sp.wait_ge(basis_used, i - 8 + 1)
                if l == 1:
                    sp.wait_ge(basis_used, first + i - 4 + 1)
                sp.dma_start(ring[0:nb * QI, slot, :],
                             basis_rows[l][ch, g * GB:g * GB + nb]
                             ).then_inc(basis_in[slot], 16)

            def rel_roundtrip(l, ch):
                sp.wait_ge(rel_evac, CHUNKS * l + ch + 1)
                sp.dma_start(rel_dram[l][:, :, ch].rearrange("t r q n -> (t r) q n"),
                             stag[:, ch % 2, :]).then_inc(rel_out[ch % 2], 16)
                if ch == CHUNKS - 1:
                    for s in rel_out:
                        sp.wait_ge(s, 16 * (CHUNKS // 2) * (l + 1))
                    if l == 0:
                        sp.wait_ge(cols_ready, 1)
                        sp.wait_ge(gate_w_ready, 1)
                    else:
                        sp.wait_ge(split_done, PIECE["rel1_1"] + 1)
                    for t in range(KT):
                        sp.dma_start(w_raw[:, t, :, :], rel_dram[l][t].rearrange("r c q n -> (c q) r n")
                                     ).then_inc(rel_back[t], 16)

            def load_piece(name):
                n = LOADED[name]
                if n >= 2:
                    sp.wait_ge(split_done, SPLIT_OF_LOAD[n - 2] + 1)
                for s in piece_src[name]:
                    sp.dma_start(piece_raw[n % 2][:, :, :], s).then_inc(raw_in[n % 2], 16)

            PER = NG
            for i in range(8):
                load_basis(0, i)
            load_piece("root1")
            load_piece("k")
            for ch in range(CHUNKS):
                for i in range(PER * (ch + 2), PER * (ch + 3)):
                    if i < PER * CHUNKS:
                        load_basis(0, i)
                rel_roundtrip(0, ch)
            for i in range(4):
                load_basis(1, i)
            load_piece("q")

            sp.wait_ge(xt_t, NT)
            sp.dma_start(w_nat[:, :, :], w.rearrange("(t p) n -> p t n", p=128)).then_inc(w_in, 16)

            def next_chunk(ch):
                for i in range(PER * (ch + 1), min(PER * (ch + 2), PER * CHUNKS)):
                    load_basis(1, i)
                rel_roundtrip(1, ch)
            next_chunk(0)
            next_chunk(1)
            load_piece("v")
            next_chunk(2)
            load_piece("Wo")
            next_chunk(3)
            load_piece("W1")
            next_chunk(4)
            load_piece("W2")
            sp.wait_ge(wt_ready, 2)
            for t in range(NT):
                if t >= 2:
                    sp.wait_ge(y_plus_x, t - 1)
                sp.dma_start(x_again[:, t % 2, :], x[t * TP:(t + 1) * TP, :]).then_inc(x_again_in[t % 2], 16)
            next_chunk(5)
            load_piece("root2")
            next_chunk(6)
            next_chunk(7)
            sp.wait_ge(xm_ready, NT)
            for n, a in enumerate((Wr_sp, Wr_fq)):
                sp.dma_start(router_raw[:, :, n * E:(n + 1) * E], a.rearrange("(p t) e -> p t e", p=128),
                             allow_slow_non_contiguous=True).then_inc(router_in, 16)
            for n, a in enumerate((br_sp, br_fq)):
                sp.dma_start(router_b[:, n * E:(n + 1) * E], a.partition_broadcast(TP),
                             allow_slow_non_contiguous=True).then_inc(router_in, 16)

            def load_expert(e):
                if e == 0:
                    sp.wait_ge(split_done, PIECE["root2"] + 1)
                if e >= XR:
                    sp.wait_ge(ex_split, e - XR + 1)
                sp.dma_start(ex_raw[:, e % XR, 0, :].rearrange("p (t f) -> p t f", t=KT),
                             ex_w1[e].rearrange("(p t) f -> p t f", p=128)).then_inc(ex_in[e % XR], 16)
                sp.dma_start(ex_raw[:, e % XR, 1, :], ex_w2[e]).then_inc(ex_in[e % XR], 16)
            for e in range(XR):
                load_expert(e)
            for n, a in enumerate((b2_sp, b2_fq)):
                sp.dma_start(out_bias[n * E:(n + 1) * E, :], a).then_inc(out_b_in, 16)
            sp.wait_ge(route_t_ready, 1)
            sp.dma_start(route_dram, route_t[:, :]).then_inc(route_out, 16)
            sp.wait_ge(route_out, 16)
            for e in range(2 * E):
                sp.dma_start(route_all[:, e, :], route_dram[e].partition_broadcast(128)).then_inc(route_back, 16)
            for e in range(XR, NX):
                load_expert(e)
            for t in range(NT):
                sp.wait_ge(final_ready, t + 1)
                sp.dma_start(out[t * TP:(t + 1) * TP, :], final[:, t % 2, :]).then_inc(stored[t % 2], 16)
            sp.wait_ge(stored[0], 16 * 3)
            sp.wait_ge(stored[1], 16 * 2)

        @block.gpsimd
        def _(pool):
            n = [0]

            def own_step(ins):
                ins.then_inc(pool_own, 1)
                n[0] += 1
                pool.wait_ge(pool_own, n[0])

            pool.memset(ident[:], 0.0).then_inc(ident_zero, 1)
            pool.iota(iota_n[:], pattern=[[1, REL * CW]], base=0, channel_multiplier=0,
                      allow_small_or_imprecise_dtypes=True).then_inc(iotas_ready, 1)
            pool.iota(tile_id[:], pattern=[[0, 2], [0, NT]], base=0, channel_multiplier=1,
                      allow_small_or_imprecise_dtypes=True).then_inc(iotas_ready, 1)
            pool.iota(node_lo[:], pattern=[[TP, NT]], base=0, channel_multiplier=0,
                      allow_small_or_imprecise_dtypes=True).then_inc(iotas_ready, 1)
            pool.wait_ge(ident_zero, 1)
            pool.affine_select(out=ident[:], in_=ident[:], compare_op=ALU.not_equal, fill=1.0, base=0,
                               pattern=[[-1, 128]], channel_multiplier=1).then_inc(ident_ready, 1)
            pool.memset(zeros[:], 0.0).then_inc(consts_ready, 1)
            pool.memset(neg_half_pow[:], -0.5).then_inc(consts_ready, 1)
            pool.memset(neg_half[:], -0.5).then_inc(consts_ready, 1)
            pool.memset(ones[:], 1.0).then_inc(consts_ready, 1)
            pool.wait_ge(consts_ready, 4)
            pool.wait_ge(bound_ready, 1)
            pool.partition_all_reduce(bound_all[:].rearrange("p a j -> p (a j)"),
                                      bound[:].rearrange("p a j -> p (a j)"), ET, RMAX).then_inc(bound_max, 1)

            def power(k, a, b):
                pool.wait_ge(var_ready, k)
                pool.tensor_tensor(rstd[:, a:b], veps[:, a:b], neg_half_pow[:, a:b], ALU.pow).then_inc(rstd_ready, 1)
            power(1, 0, NT)
            power(2, 0, NT)

            def split(name):
                s = PIECE[name]
                if s >= 2:
                    pool.wait_ge(piece_used, s - 1)
                else:
                    pool.wait_ge(basis_used, NG * CHUNKS)
                for t in range(KT):
                    if name[:3] == "rel":
                        l, r = int(name[3]) - 1, int(name[5])
                        pool.wait_ge(rel_back[t], 16 * (l + 1))
                        raw = w_raw[:, t, r, :]
                    else:
                        k = LOADED[name]
                        if t == 0:
                            pool.wait_ge(raw_in[k % 2], 16 * (k // 2 + 1))
                        raw = piece_raw[k % 2][:, t, :]
                    hi, lo = piece_hi[s % 2][:, t, :], piece_lo[s % 2][:, t, :]
                    own_step(pool.tensor_copy(hi, raw))
                    last = pool.tensor_tensor(lo, raw, hi.bitcast(F32), ALU.subtract)
                    if t < KT - 1:
                        own_step(last)
                last.then_inc(split_done, 1)
                pool.wait_ge(split_done, s + 1)
            pool.wait_ge(smalls_in, 16 * 6)
            for name in ORDER[:7]:
                split(name)
            split("W1")
            for t in range(NT):
                power(3 + t, t, t + 1)
            for t in range(NT):
                pool.wait_ge(yn_ready, t + 1)
                pool.tensor_tensor(y[:, t, :], y[:, t, :], bias_row[0:TP, 4, :], ALU.add).then_inc(y_plus_b, 1)
                pool.wait_ge(y_plus_b, t + 1)
                pool.wait_ge(x_again_in[t % 2], 16 * (t // 2 + 1))
                pool.tensor_tensor(y[:, t, :], y[:, t, :], x_again[:, t % 2, :], ALU.add).then_inc(y_plus_x, 1)
            split("W2")
            for t in range(NT):
                pool.wait_ge(xm_ready, t + 1)
                pool.tensor_tensor(y[:, t, :], y[:, t, :], bias_row[0:TP, 1, :], ALU.add).then_inc(xm_plus_b, 1)
            split("rel2_0")
            split("root2")
            pool.wait_ge(xm_ready, NT)
            pool.iota(rank[:], pattern=[[0, 2 * NT], [-1, E]], base=E, channel_multiplier=0,
                      allow_small_or_imprecise_dtypes=True).then_inc(pool_own, 1)
            n[0] += 1
            split("rel2_1")
            pool.wait_ge(router_in, 16 * 4)
            own_step(pool.tensor_copy(router_hi[:], router_raw[:]))
            pool.tensor_tensor(router_lo[:], router_raw[:], router_hi[:].bitcast(F32), ALU.subtract).then_inc(router_w_ready, 1)

            def split_expert(e):
                pool.wait_ge(ex_in[e % XR], 32 * (e // XR + 1))
                if e < 4:
                    pool.wait_ge(piece_used, len(ORDER))
                else:
                    pool.wait_ge(ex_used, e - 3)
                raw, hi, lo = ex_raw[:, e % XR], ex_hi[:, e % 4], ex_lo[:, e % 4]
                own_step(pool.tensor_copy(hi, raw))
                pool.tensor_tensor(lo, raw, hi.bitcast(F32), ALU.subtract).then_inc(ex_split, 1)
                pool.wait_ge(ex_split, e + 1)
            split_expert(0)
            for t in range(NT):
                power(3 + NT + t, t, t + 1)
            split_expert(1)
            split_expert(2)
            pool.wait_ge(out_b_in, 16 * 2)
            own_step(pool.tensor_copy(out_b_hi[:], out_bias[:]))
            own_step(pool.tensor_tensor(out_b_lo[:], out_bias[:], out_b_hi[:].bitcast(F32), ALU.subtract))
            pool.wait_ge(route_t_ready, 1)
            own_step(pool.tensor_copy(route_hi[:], route_t[:]))
            pool.tensor_tensor(route_lo[:], route_t[:], route_hi[:].bitcast(F32), ALU.subtract).then_inc(route_split, 1)
            split_expert(3)
            for t in range(NT):
                pool.wait_ge(x1n_ready, t + 1)
                pool.tensor_tensor(x1[:, t, :], x1[:, t, :], bias_row[0:TP, 5, :], ALU.add).then_inc(x1_plus_b, 1)
            for e in range(4, NX):
                split_expert(e)

        @block.vector
        def _(dve):
            n = [0]

            def own_step(ins):
                ins.then_inc(dve_own, 1)
                n[0] += 1
                dve.wait_ge(dve_own, n[0])

            norms = [0]

            def stats(source, t):
                own_step(dve.bn_stats(bn[:, t, :], source))
                own_step(dve.bn_aggr(stat[:, t, :], bn[:, t, :]))

            def add_eps(a, b):
                norms[0] += 1
                dve.tensor_scalar(veps[:, a:b], stat[:, a:b, 1], 1e-5, None, ALU.add).then_inc(var_ready, 1)

            def normalise(target, source, t):
                return dve.tensor_scalar(target, source, stat[:, t, 0:1], rstd[:, t:t + 1], ALU.subtract, ALU.mult)

            dve.wait_ge(edges_in, 48)
            dve.wait_ge(iotas_ready, 3)
            own_step(dve.tensor_copy(edge_f[:], edge_i[:]))
            own_step(dve.tensor_scalar(key_n[:], edge_f[:, 2, :], 0.0, float(CW), ALU.not_equal, ALU.mult))
            dve.tensor_tensor(key_n[:], key_n[:], edge_f[:, 0, :], ALU.add).then_inc(key_ready, 1)
            own_step(dve.tensor_reduce(mnmx[:, 0:1], edge_f[:, 1, :], AX.X, ALU.min))
            own_step(dve.tensor_reduce(mnmx[:, 1:2], edge_f[:, 1, :], AX.X, ALU.max))
            own_step(dve.tensor_scalar(mnmx[:, 0:1], mnmx[:, 0:1], -(TP - 1.0), None, ALU.add))
            own_step(dve.tensor_scalar(in_hi[:], node_lo[:], mnmx[:, 1:2], None, ALU.is_le))
            own_step(dve.tensor_scalar(in_lo[:], node_lo[:], mnmx[:, 0:1], None, ALU.is_ge))
            own_step(dve.tensor_tensor(in_lo[:], in_lo[:], in_hi[:], ALU.mult))
            own_step(dve.tensor_scalar(tile_id[:], tile_id[:], 0.5, -0.25, ALU.mult, ALU.add))
            own_step(dve.tensor_copy(tile_ii[:], tile_id[:]))
            own_step(dve.tensor_copy(tile_id[:], tile_ii[:]))
            own_step(dve.tensor_scalar(tile_id[:, 0, :], tile_id[:, 0, :], -1.0, float(ET // 2), ALU.mult, ALU.add))
            own_step(dve.tensor_scalar(tile_id[:, 1, :], tile_id[:, 1, :], 1.0, None, ALU.add))
            own_step(dve.tensor_tensor(bound[:, 0, :], tile_id[:, 0, :], in_lo[:], ALU.mult))
            dve.tensor_tensor(bound[:, 1, :], tile_id[:, 1, :], in_lo[:], ALU.mult).then_inc(bound_ready, 1)
            dve.wait_ge(x_in, 32)
            for t in range(NT):
                stats(xa[:, t, :], t)
            add_eps(0, NT)
            dve.wait_ge(keys_t, 1)
            own_step(dve.tensor_copy(keys[:].rearrange("p a t -> p (a t)"), ps[0:TE, 6, 0:2 * ET]))
            for j in range(NT):
                dve.tensor_scalar(key_m[:, j, :], keys[:, 1, :], float(-TP * j), None, ALU.add).then_inc(dve_own, 1)
                n[0] += 1
            dve.wait_ge(dve_own, n[0])
            dve.wait_ge(bound_max, 1)
            own_step(dve.tensor_scalar(range_f[:, 1, :], bound_all[0:1, 1, :], 1.0, None, ALU.max))
            own_step(dve.tensor_scalar(range_f[:, 0, :], bound_all[0:1, 0, :], -1.0, float(ET // 2), ALU.mult, ALU.add))
            own_step(dve.tensor_scalar(bound_all[0:1, 0, :], range_f[:, 1, :], -1.0, None, ALU.add))
            own_step(dve.tensor_tensor(range_f[:, 0, :], range_f[:, 0, :], bound_all[0:1, 0, :], ALU.min))
            dve.tensor_copy(range_i[:], range_f[:]).then_inc(range_ready, 1)
            dve.wait_ge(rstd_ready, 1)
            for t in range(NT):
                normalise(xn[:, t, :], xa[:, t, :], t).then_inc(xn_ready, 1)
            dve.wait_ge(xn_ready, NT)
            for t in range(NT):
                stats(xn[:, t, :], t)
            add_eps(0, NT)
            dve.wait_ge(ident_ready, 1)
            own_step(dve.tensor_reduce(sel_q[:], ident[:].rearrange("p (b q) -> p q b", b=GB), AX.X, ALU.add))
            dve.wait_ge(gate_w_hi, 1)
            for l in range(2):
                for g in range(NG):
                    k = min(GB, BASES - g * GB) * QI
                    last = dve.tensor_copy(att_col[0:k, l, g, :], ps[0:k, 5, 96 + (l * NG + g) * REL:96 + (l * NG + g + 1) * REL])
            own_step(last)
            for l in range(2):
                for g in range(NG):
                    k = min(GB, BASES - g * GB) * QI
                    for r in range(REL):
                        last = dve.tensor_scalar(sel_att[0:k, l, g, r, :], sel_q[0:k, :], att_col[0:k, l, g, r:r + 1],
                                                 None, ALU.mult)
            last.then_inc(sel_ready, 1)
            dve.wait_ge(cols_t, 1)
            dve.tensor_copy(colv[:], ps[:, 5, 0:45]).then_inc(cols_ready, 1)
            dve.wait_ge(gate_w_hi, 1)
            gate_ps = ps[:, 5, 64:64 + 2 * KT * REL]
            dve.tensor_tensor(gate_lo[:].rearrange("p l t r -> p (l t r)"), gate_ps,
                              gate_hi[:].rearrange("p l t r -> p (l t r)").bitcast(F32), ALU.subtract).then_inc(gate_w_ready, 1)
            dve.wait_ge(rstd_ready, 2)
            for t in range(NT):
                normalise(xn2[:, t, :], xn[:, t, :], t).then_inc(xn2_ready, 1)

            dve.wait_ge(range_ready, 1)
            turn, drained = dve.alloc_register("turn"), dve.alloc_register("drained")
            dve.reg_mov(turn, 0)
            for j in range(NT):
                lo = dve.value_load(range_i[0:1, 0, j:j + 1], min_val=0, max_val=ET // 2 - 1)
                hi = dve.value_load(range_i[0:1, 1, j:j + 1], min_val=1, max_val=ET // 2)
                with dve.Fori(lo, hi) as pair:
                    dve.reg_add(turn, turn, 1)
                    k = dve.snap(turn)
                    dve.wait_ge(pair_used, k)
                    s = k % 2
                    for h in range(2):
                        dve.tensor_scalar(oh_n[:, bass.ds(2 * s + h, 1), :], iota_n[:], keys[:, 0, bass.ds(2 * pair + h, 1)],
                                          None, ALU.is_equal)
                        last = dve.tensor_scalar(oh_m[:, bass.ds(2 * s + h, 1), :], iota_n[:, 0:TP],
                                                 key_m[:, j, bass.ds(2 * pair + h, 1)], None, ALU.is_equal)
                    last.then_inc(one_hot, 1)
                dve.reg_add(drained, turn, 2)
                dve.wait_ge(pair_used, dve.snap(drained))
                for h in range(3):
                    wd = min(CB, REL * CW - CB * h)
                    last = dve.tensor_copy(counts[:, j, CB * h:CB * h + wd], ps[0:TP, h, 0:wd])
                last.then_inc(count_ready, 1)
                dve.wait_ge(hT_hi, j + 1)
                dve.tensor_tensor(ht_lo[0][:, :, j * TP:(j + 1) * TP], ps[:, 5 + j % 2, 0:KT * TP].rearrange("p (t m) -> p t m", t=KT),
                                  ht_hi[0][:, :, j * TP:(j + 1) * TP].bitcast(F32), ALU.subtract).then_inc(hT_ready, 1)

            def messages(l):
                dve.wait_ge(gates_ready, l + 1)
                for r in range(REL):
                    for t in range(NT):
                        i = (2 * l + r) * NT + t
                        dve.wait_ge(u_hi_done, i + 1)
                        dve.scalar_tensor_tensor(out=u_lo[l][:, t, :], in0=ps[0:TP, UB[i % 3], :], scalar=gates[:, t, r:r + 1],
                                                 in1=u_hi[l][:, t, :].bitcast(F32), op0=ALU.mult, op1=ALU.subtract).then_inc(u_ready, 1)

            messages(0)
            dve.wait_ge(smalls_in, 16 * 6)
            for t in range(NT):
                dve.wait_ge(agg_done, t + 1)
                if t >= 2:
                    dve.wait_ge(h1_t, t - 1)
                dve.tensor_tensor(row_tmp[:, t % 2, :], ps[0:TP, AGG[t], :], bias_row[0:TP, 0, :], ALU.add).then_inc(h_added, 1)
            for t in range(NT):
                dve.wait_ge(xt_t, t + 1)
                if t:
                    dve.wait_ge(xt_ready, t)
                    dve.wait_ge(xt_hi_done, t)
                else:
                    dve.wait_ge(rel_applied, 2)
                    dve.wait_ge(agg_done, NT)
                    for a in (xt_hi, xt_lo):
                        own_step(dve.memset(a[:, :, NODES:NPAD].bitcast(F32), 0.0))
                for c in range(KT):
                    last = dve.tensor_scalar(xt_tmp[:, c, :], ps[:, 5 + t % 2, c * TP:(c + 1) * TP], colv[:, C_G1 + c:C_G1 + c + 1],
                                             colv[:, C_BE1 + c:C_BE1 + c + 1], ALU.mult, ALU.add)
                last.then_inc(xt_scaled, 1)
                dve.wait_ge(xt_hi_done, t + 1)
                dve.tensor_tensor(xt_lo[:, :, t * TP:(t + 1) * TP], xt_tmp[:], xt_hi[:, :, t * TP:(t + 1) * TP].bitcast(F32),
                                  ALU.subtract).then_inc(xt_ready, 1)
            for c in range(2):
                dve.wait_ge(wt_hi_done, c + 1)
                dve.tensor_tensor(wt_lo[:, 2 * c:2 * c + 2, :], ps[:, (0, 1)[c], :].rearrange("p (t m) -> p t m", t=2),
                                  wt_hi[:, 2 * c:2 * c + 2, :].bitcast(F32), ALU.subtract).then_inc(wt_ready, 1)

            def halves(b):
                return ps[:, b:b + 2, 0:HALF]

            def in_halves(ap):
                return ap.rearrange("p (h m) -> p h m", h=2)

            def project(z):
                for c in range(KT):
                    i = KT * z + c
                    dve.wait_ge(kq_hi_done, i + 1)
                    dve.scalar_tensor_tensor(out=in_halves(kq_lo[:, c, :]), in0=halves((0, 5)[c % 2]),
                                             scalar=colv[:, C_BK + i:C_BK + i + 1],
                                             in1=in_halves(kq_hi[:, c, :]).bitcast(F32),
                                             op0=ALU.add, op1=ALU.subtract).then_inc(kq_ready, 1)
                dve.wait_ge(xd_mm, z + 1)
                dve.tensor_copy(xd[:], ps[0:TP, 2, 0:NT]).then_inc(xd_ready, 1)
                for t in range(NT):
                    i = NT * z + t
                    dve.wait_ge(feat_exp, i + 1)
                    if z == 0:
                        dve.tensor_scalar(kp[:, t, :], feat[:, i % 2, :], 1.0 / 16, None, ALU.mult).then_inc(feat_ready, 1)
                    else:
                        dve.tensor_scalar(feat[:, i % 2, :], feat[:, i % 2, :], 1.0 / 16, None, ALU.mult).then_inc(feat_ready, 1)
                        if t == 0:
                            own_step(dve.memset(qpt[:, :, NODES:NPAD], 0.0))
                        dve.wait_ge(qp_t, t + 1)
                        dve.tensor_copy(qpt[:, :, t * TP:(t + 1) * TP],
                                        ps[:, (0, 1)[t % 2], 0:2 * TP].rearrange("p (c m) -> p c m", c=2)).then_inc(qpt_ready, 1)
            project(0)
            project(1)
            for t in range(NT):
                dve.wait_ge(v_mm, t + 1)
                dve.tensor_tensor(v[:, t, :], ps[0:TP, (5, 6)[t % 2], :], bias_row[0:TP, 2, :], ALU.add).then_inc(v_ready, 1)
            dve.wait_ge(kv_mm, 1)
            own_step(dve.tensor_copy(ksum[:], ps[:, 2, 8:10]))
            dve.tensor_copy(kv[:], ps[:, 0:2, :]).then_inc(kv_ready, 1)
            dve.wait_ge(d_mm, 1)
            own_step(dve.tensor_scalar(rec[:], ps[0:TP, 2, 16:16 + NT], 1e-8, None, ALU.add))
            dve.reciprocal(rec[:], rec[:]).then_inc(rec_ready, 1)
            for c in range(KT):
                dve.wait_ge(yt_hi_done, c + 1)
                dve.tensor_tensor(in_halves(yt_lo[:, c, :]), halves((5, 0)[c % 2]), in_halves(yt_hi[:, c, :]).bitcast(F32),
                                  ALU.subtract).then_inc(yt_ready, 1)
            dve.wait_ge(rec_ready, 1)
            for t in range(NT):
                dve.wait_ge(wo_mm, t + 1)
                own_step(dve.scalar_tensor_tensor(out=y[:, t, :], in0=ps[0:TP, AGG[t], :], scalar=rec[:, t:t + 1],
                                                  in1=bias_row[0:TP, 3, :], op0=ALU.mult, op1=ALU.add))
                own_step(dve.tensor_tensor(y[:, t, :], y[:, t, :], v[:, t, :], ALU.add))
                stats(y[:, t, :], t)
                add_eps(t, t + 1)
                if t == NT - 1:
                    dve.sem_inc(y_ready, 1)
                if t in (1, 2):
                    dve.wait_ge(rstd_ready, 2 + t)
                    normalise(yn[:, (t - 1) % 2, :], y[:, t - 1, :], t - 1).then_inc(yn_ready, 1)
            for t in range(NT):
                dve.wait_ge(h2_t, t + 1)
                if t + 2 < NT:
                    dve.wait_ge(rstd_ready, 2 + t + 3)
                    normalise(yn[:, t % 2, :], y[:, t + 2, :], t + 2).then_inc(yn_ready, 1)
                if t == 0:
                    for a in (h2t_hi, h2t_lo):
                        own_step(dve.memset(a[:, :, NODES:NPAD].bitcast(F32), 0.0))
                else:
                    dve.wait_ge(h2t_ready, t)
                    dve.wait_ge(h2_hi_done, t)
                for c in range(KT):
                    last = dve.tensor_scalar(h2_tmp[:, c, :], ps[:, (7, 4)[t % 2], c * TP:(c + 1) * TP], colv[:, C_G2 + c:C_G2 + c + 1],
                                             colv[:, C_BE2 + c:C_BE2 + c + 1], ALU.mult, ALU.add)
                last.then_inc(h2_scaled, 1)
                dve.wait_ge(h2_hi_done, t + 1)
                dve.tensor_tensor(h2t_lo[:, :, t * TP:(t + 1) * TP], h2_tmp[:], h2t_hi[:, :, t * TP:(t + 1) * TP].bitcast(F32),
                                  ALU.subtract).then_inc(h2t_ready, 1)
            for c in range(KT):
                dve.wait_ge(act_done, c + 1)
                own_step(dve.tensor_copy(act_hi[:, c, :], act_tmp[:, c % 2, :]))
                dve.tensor_tensor(act_lo[:, c, :], act_tmp[:, c % 2, :], act_hi[:, c, :].bitcast(F32), ALU.subtract).then_inc(act_ready, 1)
            for t in range(NT):
                dve.wait_ge(w2_mm, t + 1)
                dve.wait_ge(y_plus_x, t + 1)
                dve.tensor_tensor(y[:, t, :], ps[0:TP, AGG[t], :], y[:, t, :], ALU.add).then_inc(xm_ready, 1)

            for t in range(KT):
                dve.wait_ge(hT_hi, NT + t + 1)
                dve.tensor_tensor(ht_lo[1][:, t, 0:NODES], h1t[:, t, 0:NODES], ht_hi[1][:, t, 0:NODES].bitcast(F32),
                                  ALU.subtract).then_inc(hT_ready, 1)
            messages(1)
            for t in range(NT):
                dve.wait_ge(agg_done, NT + t + 1)
                dve.wait_ge(xm_plus_b, t + 1)
                if t == 0:
                    dve.wait_ge(split_done, PIECE["rel2_1"] + 1)
                own_step(dve.tensor_tensor(x1[:, t, :], ps[0:TP, AGG[t], :], y[:, t, :], ALU.add))
                stats(x1[:, t, :], t)
                add_eps(t, t + 1)
                dve.wait_ge(rstd_ready, 2 + NT + t + 1)
                if t >= 2:
                    dve.wait_ge(x1_t, t - 1)
                normalise(x1n[:, t % 2, :], x1[:, t, :], t).then_inc(x1n_ready, 1)
            for t in range(NT):
                dve.wait_ge(x1_hi_done, t + 1)
                if t == 0:
                    for a in (x1t_hi, x1t_lo):
                        own_step(dve.memset(a[:, :, NODES:NPAD].bitcast(F32), 0.0))
                dve.tensor_tensor(x1t_lo[:, :, t * TP:(t + 1) * TP], ps[:, UB[t % 3], 0:KT * TP].rearrange("p (t m) -> p t m", t=KT),
                                  x1t_hi[:, :, t * TP:(t + 1) * TP].bitcast(F32), ALU.subtract).then_inc(x1t_ready, 1)
            dve.wait_ge(logit_mm, 1)
            dve.wait_ge(router_in, 16 * 4)
            for t in range(NT):
                last = dve.tensor_tensor(logit[:, t].rearrange("p b e -> p (b e)"), ps[0:TP, 4, t * 2 * E:(t + 1) * 2 * E],
                                         router_b[:], ALU.add)
            own_step(last)
            lg = logit[:].rearrange("p t b e -> p (t b) e")

            def over(ap):
                return ap.rearrange("p t b -> p (t b)").unsqueeze(2).to_broadcast([TP, 2 * NT, E])

            def flat(a):
                return a[:].rearrange("p t b e -> p (t b) e")
            own_step(dve.tensor_reduce(lmax[:].rearrange("p t b -> p (t b)"), lg, AX.X, ALU.max))
            dve.tensor_tensor(flat(shifted), lg, over(lmax[:]), ALU.subtract).then_inc(shift_ready, 1)
            own_step(dve.tensor_tensor(flat(score), lg, over(lmax[:]), ALU.is_equal))
            own_step(dve.tensor_tensor(flat(score), flat(score), flat(rank), ALU.mult))
            own_step(dve.tensor_reduce(best[:].rearrange("p t b -> p (t b)"), flat(score), AX.X, ALU.max))
            own_step(dve.tensor_tensor(flat(route), flat(score), over(best[:]), ALU.is_equal))
            dve.wait_ge(expo_ready, 1)
            own_step(dve.tensor_reduce(denom[:].rearrange("p t b -> p (t b)"), flat(expo), AX.X, ALU.add))
            own_step(dve.reciprocal(gate_p[:], denom[:]))
            dve.tensor_tensor(flat(route), flat(route), over(gate_p[:]), ALU.mult).then_inc(route_ready, 1)
            own_step(dve.memset(route_t[:, NODES:NPAD], 0.0))
            dve.wait_ge(route_tr, 1)
            own_step(dve.tensor_copy(route_t[:, 0:4 * TP], ps[0:2 * E, 4, 0:4 * TP]))
            dve.tensor_copy(route_t[:, 4 * TP:NODES], ps[0:2 * E, 7, 0:TP]).then_inc(route_t_ready, 1)
            for e in range(NX):
                for h in range(2):
                    i = 2 * e + h
                    dve.wait_ge(hid_ready, i + 1)
                    source = hid[:, i % 4, :]
                    if e:
                        if h == 0:
                            dve.wait_ge(route_back, 16 * 2 * E)
                        own_step(dve.tensor_tensor(gated[:, i % 4, :], source, route_all[:, e - 1, h * HALF:(h + 1) * HALF], ALU.mult))
                        source = gated[:, i % 4, :]
                    if e >= 2 and h == 0:
                        dve.wait_ge(ex_used, e - 1)
                    hi, lo = (a[:, e % 2, h * HALF:(h + 1) * HALF] for a in (hg_hi, hg_lo))
                    own_step(dve.tensor_copy(hi, source))
                    dve.tensor_tensor(lo, source, hi.bitcast(F32), ALU.subtract).then_inc(hg_ready, 1)
            for t in range(NT):
                dve.wait_ge(ffn_mm, t + 1)
                dve.wait_ge(x1_plus_b, t + 1)
                if t >= 2:
                    dve.wait_ge(stored[t % 2], 16 * (t // 2))
                dve.tensor_tensor(final[:, t % 2, :], ps[0:TP, AGG[t], :], x1[:, t, :], ALU.add).then_inc(final_ready, 1)

        @block.scalar
        def _(act):
            def halves(b):
                return ps[:, b:b + 2, 0:HALF]

            def in_halves(ap):
                return ap.rearrange("p (h m) -> p h m", h=2)

            def evac_relation(l, ch):
                i = CHUNKS * l + ch
                act.wait_ge(rel_sum, i + 1)
                if i >= 2:
                    act.wait_ge(rel_out[ch % 2], 16 * (i // 2))
                act.activation(stag[:, ch % 2, :], ps[:, rel_bank(l, ch), :], ACT.Copy).then_inc(rel_evac, 1)

            act.wait_ge(rows_in, 16 * 13)
            for l in range(2):
                last = act.activation(att_rep[:, l, :].rearrange("r (b q) -> r b q", q=QI),
                                      att_rows[:, l, :].unsqueeze(2).to_broadcast([REL, BASES, QI]), ACT.Copy)
            last.then_inc(att_ready, 1)
            act.wait_ge(gate_rows_t, 1)
            act.activation(gate_hi[:].rearrange("p l t r -> p (l t r)"), ps[:, 5, 64:64 + 2 * KT * REL], ACT.Copy).then_inc(gate_w_hi, 1)
            for j in range(NT):
                act.wait_ge(hT_t, j + 1)
                act.activation(ht_hi[0][:, :, j * TP:(j + 1) * TP], ps[:, 5 + j % 2, 0:KT * TP].rearrange("p (t m) -> p t m", t=KT),
                               ACT.Copy).then_inc(hT_hi, 1)
                for ch in (2 * j, 2 * j + 1):
                    if ch < CHUNKS:
                        evac_relation(0, ch)

            def expand_counts(k, r):
                act.wait_ge(count_ready, NT)
                if k:
                    act.wait_ge(rel_applied, k)
                for t in range(NT):
                    last = act.activation(cf[:, t, :], counts[:, t, r * CW:(r + 1) * CW], ACT.Copy)
                last.then_inc(cf_ready, 1)

            def messages(l):
                act.wait_ge(gate_mm, l + 1)
                act.activation(gates[:].rearrange("p t r -> p (t r)"), ps[0:TP, 7, 0:NT * REL], ACT.Sigmoid).then_inc(gates_ready, 1)
                act.wait_ge(gates_ready, l + 1)
                for r in range(REL):
                    expand_counts(2 * l + r, r)
                    for t in range(NT):
                        i = (2 * l + r) * NT + t
                        act.wait_ge(u_mm, i + 1)
                        act.activation(u_hi[l][:, t, :], ps[0:TP, UB[i % 3], :], ACT.Copy, scale=gates[:, t, r:r + 1]).then_inc(u_hi_done, 1)

            messages(0)
            for t in range(NT):
                act.wait_ge(h_added, t + 1)
                act.activation(row_tmp[:, t % 2, :], row_tmp[:, t % 2, :], ACT.Relu).then_inc(h_relu, 1)
                if t:
                    act.wait_ge(h1_t, t)
                    act.activation(h1t[:, :, (t - 1) * TP:t * TP], ps[:, UB[(t - 1) % 2], 0:KT * TP].rearrange("p (t m) -> p t m", t=KT),
                                   ACT.Copy).then_inc(h1t_ready, 1)
            t = NT
            act.wait_ge(h1_t, t)
            act.activation(h1t[:, :, (t - 1) * TP:t * TP], ps[:, UB[(t - 1) % 2], 0:KT * TP].rearrange("p (t m) -> p t m", t=KT),
                           ACT.Copy).then_inc(h1t_ready, 1)
            evac_relation(1, 0)
            for t in range(NT):
                act.wait_ge(xt_scaled, t + 1)
                act.activation(xt_hi[:, :, t * TP:(t + 1) * TP], xt_tmp[:], ACT.Copy).then_inc(xt_hi_done, 1)
            for c in range(2):
                act.wait_ge(wt_t, c + 1)
                act.activation(wt_hi[:, 2 * c:2 * c + 2, :], ps[:, (0, 1)[c], :].rearrange("p (t m) -> p t m", t=2),
                               ACT.Copy).then_inc(wt_hi_done, 1)

            def project(z):
                for c in range(KT):
                    i = KT * z + c
                    bias = colv[:, C_BK + i:C_BK + i + 1]
                    act.wait_ge(kq_mm, i + 1)
                    if i:
                        act.wait_ge(sq_used, i)
                    act.activation(in_halves(square[:]), halves((0, 5)[c % 2]), ACT.Square, bias=bias).then_inc(sq_ready, 1)
                    if z and c == 0:
                        act.wait_ge(feat_mm, NT)
                    act.activation(in_halves(kq_hi[:, c, :]), halves((0, 5)[c % 2]), ACT.Identity, bias=bias).then_inc(kq_hi_done, 1)
                evac_relation(1, 1 + z)
                act.wait_ge(xd_ready, z + 1)
                for t in range(NT):
                    i = NT * z + t
                    act.wait_ge(feat_mm, i + 1)
                    if i >= 2:
                        if i >= NT + 2:
                            act.wait_ge(qp_t, i - NT - 1)
                        else:
                            act.wait_ge(feat_ready, i - 1)
                    act.activation(feat[:, i % 2, :], ps[0:TP, (5, 6)[t % 2], 0:M], ACT.Exp, bias=xd[:, t:t + 1]).then_inc(feat_exp, 1)
            project(0)
            project(1)
            evac_relation(1, 3)
            for c in range(KT):
                act.wait_ge(yt_mm, c + 1)
                act.activation(in_halves(yt_hi[:, c, :]), halves((5, 0)[c % 2]), ACT.Copy).then_inc(yt_hi_done, 1)
            evac_relation(1, 4)
            evac_relation(1, 5)
            for t in range(NT):
                act.wait_ge(h2_scaled, t + 1)
                if t == 0:
                    act.wait_ge(wo_mm, NT)
                act.activation(h2t_hi[:, :, t * TP:(t + 1) * TP], h2_tmp[:], ACT.Copy).then_inc(h2_hi_done, 1)
            for c in range(KT):
                act.wait_ge(act_mm, c + 1)
                if c >= 2:
                    act.wait_ge(act_ready, c - 1)
                act.activation(in_halves(act_tmp[:, c % 2, :]), halves((0, 5)[c % 2]), ACT.Gelu,
                               bias=colv[:, C_B1 + c:C_B1 + c + 1]).then_inc(act_done, 1)
            evac_relation(1, 6)
            evac_relation(1, 7)
            for t in range(KT):
                if t == 0:
                    act.wait_ge(act_mm, KT)
                    act.wait_ge(h1t_ready, NT)
                act.activation(ht_hi[1][:, t, 0:NODES], h1t[:, t, 0:NODES], ACT.Copy).then_inc(hT_hi, 1)
            messages(1)
            for t in range(NT):
                act.wait_ge(x1_t, t + 1)
                if t == 0:
                    act.wait_ge(u_mm, 4 * NT)
                act.activation(x1t_hi[:, :, t * TP:(t + 1) * TP], ps[:, UB[t % 3], 0:KT * TP].rearrange("p (t m) -> p t m", t=KT),
                               ACT.Copy).then_inc(x1_hi_done, 1)
            act.wait_ge(shift_ready, 1)
            act.activation(expo[:].rearrange("p t b e -> p (t b e)"), shifted[:].rearrange("p t b e -> p (t b e)"),
                           ACT.Exp).then_inc(expo_ready, 1)
            for e in range(NX):
                for h in range(2):
                    i = 2 * e + h
                    act.wait_ge(hid_mm, i + 1)
                    if i >= 4:
                        act.wait_ge(hg_ready, i - 3)
                    act.activation(hid[:, i % 4, :], ps[:, UB[i % 3], 0:HALF], ACT.Gelu,
                                   bias=colv[:, C_EXP + e:C_EXP + e + 1]).then_inc(hid_ready, 1)

        @block.tensor
        def _(pe):
            def mm3(target, a_hi, a_lo, b_hi, b_lo, first, last, skip=False):
                pe.matmul(target, a_hi, b_hi, start=first, stop=False, skip_group_check=skip)
                pe.matmul(target, a_hi, b_lo, start=False, stop=False, skip_group_check=skip)
                return pe.matmul(target, a_lo, b_hi, start=False, stop=last, skip_group_check=skip)

            def relation_part(l, i):
                ch, g = divmod(i, NG)
                nb = min(GB, BASES - g * GB)
                slot, turn_ = basis_turn(l, i)
                ring = (ring0, ring1)[l]
                pe.wait_ge(basis_in[slot], 16 * turn_)
                if g == 0:
                    if l == 0 and ch >= 2:
                        pe.wait_ge(rel_evac, ch - 1)
                    if l == 1:
                        pe.wait_ge(rel_evac, CHUNKS + ch)
                        pe.wait_ge(u_ready, 2 * NT)
                for c in range(4):
                    last = pe.matmul(ps[32 * c:32 * c + 32, rel_bank(l, ch), :],
                                     sel_att[0:nb * QI, l, g].rearrange("p r q -> p (r q)"),
                                     ring[0:nb * QI, slot, c * D:(c + 1) * D], start=(g == 0), stop=(g == NG - 1))
                last.then_inc(basis_used, 1)
                if g == NG - 1:
                    pe.wait_ge(basis_used, CHUNKS * NG * l + i + 1)
                    pe.sem_inc(rel_sum, 1)

            def relation_chunk(l, ch):
                for g in range(NG):
                    relation_part(l, NG * ch + g)

            pe.wait_ge(ident_ready, 1)
            pe.wait_ge(key_ready, 1)
            pe.transpose(ps[0:TE, 6, 0:ET], key_n[:], ident[0:ET, 0:ET])
            pe.transpose(ps[0:TE, 6, ET:2 * ET], edge_f[:, 1, :], ident[0:ET, 0:ET]).then_inc(keys_t, 1)
            pe.wait_ge(rows_in, 16 * 13)
            pe.wait_ge(att_ready, 1)
            pe.transpose(ps[:, 5, 0:45], row_vec[:], ident[0:45, 0:45]).then_inc(cols_t, 1)
            for l in range(2):
                for t in range(KT):
                    o = 64 + (l * KT + t) * REL
                    last = pe.transpose(ps[:, 5, o:o + REL], gate_rows[:, l, :].rearrange("r (i t) -> r t i", t=KT)[:, t],
                                        ident[0:REL, 0:REL])
                for g in range(NG):
                    nb = min(GB, BASES - g * GB)
                    o = 96 + (l * NG + g) * REL
                    last = pe.transpose(ps[0:nb * QI, 5, o:o + REL],
                                        att_rep[:, l, g * GB * QI:(g * GB + nb) * QI],
                                        ident[0:REL, 0:REL])
            last.then_inc(gate_rows_t, 1)

            pe.wait_ge(range_ready, 1)
            pe.wait_ge(consts_ready, 4)
            pe.wait_ge(sel_ready, 1)
            turn = pe.alloc_register("turn")
            pe.reg_mov(turn, 0)
            pe.sem_inc(pair_used, 2)
            for j in range(NT):
                lo = pe.value_load(range_i[0:1, 0, j:j + 1], min_val=0, max_val=ET // 2 - 1)
                hi = pe.value_load(range_i[0:1, 1, j:j + 1], min_val=1, max_val=ET // 2)
                if j:
                    pe.wait_ge(count_ready, j)
                for h in range(3):
                    pe.matmul(ps[0:TP, h, 0:2], zeros[:], iota_n[:, 0:2], start=True, stop=False, skip_group_check=True)
                with pe.Fori(lo, hi) as _pair:
                    pe.reg_add(turn, turn, 1)
                    k = pe.snap(turn)
                    pe.wait_ge(one_hot, k)
                    s = k % 2
                    for u in range(2):
                        for h in range(3):
                            wd = min(CB, REL * CW - CB * h)
                            last = pe.matmul(ps[0:TP, h, 0:wd], oh_m[:, bass.ds(2 * s + u, 1), :],
                                             oh_n[:, bass.ds(2 * s + u, 1), CB * h:CB * h + wd],
                                             start=False, stop=False, skip_group_check=True)
                    last.then_inc(pair_used, 1)
                pe.wait_ge(xn_ready, NT)
                if j == 0:
                    pe.wait_ge(gate_w_ready, 1)
                    pe.wait_ge(cols_ready, 1)
                if j >= 2:
                    pe.wait_ge(hT_ready, j - 1)
                for t in range(KT):
                    last = pe.transpose(ps[:, 5 + j % 2, t * TP:(t + 1) * TP],
                                        xn[:, j, :].rearrange("p (i t) -> p t i", t=KT)[:, t], ident[0:TP, 0:TP])
                last.then_inc(hT_t, 1)
                for ch in (2 * j, 2 * j + 1):
                    if ch < CHUNKS:
                        relation_chunk(0, ch)

            def layer(l):
                hi, lo = ht_hi[l], ht_lo[l]
                pe.wait_ge(hT_ready, (NT, NT + KT)[l])
                if l == 1:
                    pe.wait_ge(rel_evac, 2 * CHUNKS)
                pe.wait_ge(gate_w_ready, 1)
                for t in range(NT):
                    for c in range(KT):
                        last = mm3(ps[0:TP, 7, t * REL:(t + 1) * REL], hi[:, c, t * TP:(t + 1) * TP], lo[:, c, t * TP:(t + 1) * TP],
                                   gate_hi[:, l, c, :], gate_lo[:, l, c, :], t == 0 and c == 0, t == NT - 1 and c == KT - 1, skip=True)
                last.then_inc(gate_mm, 1)
                pe.wait_ge(gates_ready, l + 1)
                for r in range(REL):
                    s = PIECE[f"rel{l + 1}_{r}"]
                    pe.wait_ge(split_done, s + 1)
                    for t in range(NT):
                        i = (2 * l + r) * NT + t
                        if i >= 3:
                            pe.wait_ge(u_ready, i - 2)
                        for c in range(KT):
                            last = mm3(ps[0:TP, UB[i % 3], :], hi[:, c, t * TP:(t + 1) * TP], lo[:, c, t * TP:(t + 1) * TP],
                                       piece_hi[s % 2][:, c, :], piece_lo[s % 2][:, c, :], c == 0, c == KT - 1)
                        last.then_inc(u_mm, 1)
                    pe.wait_ge(u_mm, (2 * l + r + 1) * NT)
                    pe.sem_inc(piece_used, 1)
                    if r == 0:
                        s = PIECE[f"root{l + 1}"]
                        pe.wait_ge(split_done, s + 1)
                        if l == 0:
                            pe.wait_ge(count_ready, NT)
                        else:
                            pe.wait_ge(xm_ready, NT)
                        for t in range(NT):
                            for c in range(KT):
                                last = mm3(ps[0:TP, AGG[t], :], hi[:, c, t * TP:(t + 1) * TP], lo[:, c, t * TP:(t + 1) * TP],
                                           piece_hi[s % 2][:, c, :], piece_lo[s % 2][:, c, :], c == 0, False)
                        last.then_inc(piece_used, 1)
                    pe.wait_ge(cf_ready, 2 * l + r + 1)
                    pe.wait_ge(u_ready, (2 * l + r + 1) * NT)
                    for t in range(NT):
                        for m in range(NT):
                            for u in (u_hi[l], u_lo[l]):
                                last = pe.matmul(ps[0:TP, AGG[t], :], cf[:, m, t * TP:(t + 1) * TP], u[:, m, :], start=False,
                                                 stop=(r == 1 and m == NT - 1 and u is u_lo[l]))
                        if r == 1:
                            last.then_inc(agg_done, 1)
                    if r == 0:
                        last.then_inc(rel_applied, 1)
                    else:
                        pe.wait_ge(agg_done, (l + 1) * NT)
                        pe.sem_inc(rel_applied, 1)

            layer(0)
            for t in range(NT):
                pe.wait_ge(h_relu, t + 1)
                if t >= 2:
                    pe.wait_ge(h1t_ready, t - 1)
                else:
                    pe.wait_ge(u_ready, 2 * NT)
                for c in range(KT):
                    last = pe.transpose(ps[:, UB[t % 2], c * TP:(c + 1) * TP],
                                        row_tmp[:, t % 2, :].rearrange("p (i t) -> p t i", t=KT)[:, c], ident[0:TP, 0:TP])
                last.then_inc(h1_t, 1)
            relation_chunk(1, 0)
            pe.wait_ge(xn2_ready, NT)
            pe.wait_ge(h_added, NT)
            for t in range(NT):
                if t >= 2:
                    pe.wait_ge(xt_scaled, t - 1)
                for c in range(KT):
                    last = pe.transpose(ps[:, 5 + t % 2, c * TP:(c + 1) * TP], xn2[:, t, c * 128:(c + 1) * 128], ident[0:TP, 0:TP])
                last.then_inc(xt_t, 1)
            pe.wait_ge(w_in, 16)
            for c in range(2):
                for t in range(2):
                    for m in range(2):
                        o = t * M + m * 128
                        last = pe.transpose(ps[:, (0, 1)[c], o:o + 128], w_nat[:, m, (2 * c + t) * 128:(2 * c + t + 1) * 128], ident[:])
                last.then_inc(wt_t, 1)

            def project(z):
                s = PIECE["kq"[z]]
                pe.wait_ge(split_done, s + 1)
                pe.wait_ge(xt_ready, NT)
                for c in range(KT):
                    i = KT * z + c
                    b = (0, 5)[c % 2]
                    if c >= 2:
                        pe.wait_ge(kq_ready, i - 1)
                    elif z == 0:
                        pe.wait_ge(wt_ready, 2)
                        pe.wait_ge(xt_scaled, NT)
                    else:
                        pe.wait_ge(feat_exp, NT)
                        pe.wait_ge(kq_ready, KT)
                    for k in range(KT):
                        for h in range(2):
                            last = mm3(ps[:, b + h, 0:HALF], piece_hi[s % 2][:, k, c * 128:(c + 1) * 128],
                                       piece_lo[s % 2][:, k, c * 128:(c + 1) * 128], xt_hi[:, k, h * HALF:(h + 1) * HALF],
                                       xt_lo[:, k, h * HALF:(h + 1) * HALF], k == 0, k == KT - 1)
                    last.then_inc(kq_mm, 1)
                    if c:
                        half_norm(z, c - 1)
                half_norm(z, KT - 1)
                pe.wait_ge(kq_mm, KT * (z + 1))
                pe.sem_inc(piece_used, 1)
                relation_chunk(1, 1 + z)
                pe.wait_ge(kq_ready, KT * (z + 1))
                for t in range(NT):
                    i = NT * z + t
                    if t >= 2:
                        pe.wait_ge(feat_exp, i - 1)
                    for k in range(KT):
                        last = mm3(ps[0:TP, (5, 6)[t % 2], 0:M], kq_hi[:, k, t * TP:(t + 1) * TP], kq_lo[:, k, t * TP:(t + 1) * TP],
                                   wt_hi[:, k, :], wt_lo[:, k, :], k == 0, k == KT - 1)
                    last.then_inc(feat_mm, 1)
                    if z and t:
                        turn_features(t - 1)
                if z:
                    turn_features(NT - 1)

            def half_norm(z, c):
                pe.wait_ge(sq_ready, KT * z + c + 1)
                if z and c == 0:
                    pe.wait_ge(xd_ready, 1)
                for t in range(NT):
                    last = pe.matmul(ps[0:TP, 2, t:t + 1], square[:, t * TP:(t + 1) * TP], neg_half[:], start=(c == 0 and t == 0),
                                     stop=(c == KT - 1 and t == NT - 1), skip_group_check=True)
                last.then_inc(sq_used, 1)
                if c == KT - 1:
                    pe.wait_ge(sq_used, KT * (z + 1))
                    pe.sem_inc(xd_mm, 1)

            def turn_features(t):
                pe.wait_ge(feat_ready, NT + t + 1)
                if t >= 2:
                    pe.wait_ge(qpt_ready, t - 1)
                for m in range(2):
                    last = pe.transpose(ps[:, (0, 1)[t % 2], m * TP:(m + 1) * TP], feat[:, (NT + t) % 2, m * 128:(m + 1) * 128],
                                        ident[0:TP, 0:TP])
                last.then_inc(qp_t, 1)

            project(0)
            project(1)
            s = PIECE["v"]
            pe.wait_ge(split_done, s + 1)
            pe.wait_ge(feat_exp, 2 * NT)
            for t in range(NT):
                if t >= 2:
                    pe.wait_ge(v_ready, t - 1)
                for k in range(KT):
                    last = mm3(ps[0:TP, (5, 6)[t % 2], :], xt_hi[:, k, t * TP:(t + 1) * TP], xt_lo[:, k, t * TP:(t + 1) * TP],
                               piece_hi[s % 2][:, k, :], piece_lo[s % 2][:, k, :], k == 0, k == KT - 1)
                last.then_inc(v_mm, 1)
            pe.wait_ge(v_mm, NT)
            pe.sem_inc(piece_used, 1)
            relation_chunk(1, 3)
            pe.wait_ge(v_ready, NT)
            pe.wait_ge(qpt_ready, NT)
            pe.wait_ge(feat_ready, NT)
            pe.wait_ge(xd_ready, 2)
            for m in range(2):
                for t in range(NT):
                    pe.matmul(ps[:, m, :], kp[:, t, m * 128:(m + 1) * 128], v[:, t, :], start=(t == 0), stop=(t == NT - 1))
                for t in range(NT):
                    last = pe.matmul(ps[:, 2, 8 + m:9 + m], kp[:, t, m * 128:(m + 1) * 128], ones[0:TP, :],
                                     start=(m == 0 and t == 0), stop=(m == 1 and t == NT - 1), skip_group_check=True)
            last.then_inc(kv_mm, 1)
            relation_chunk(1, 4)
            pe.wait_ge(kv_ready, 1)
            for t in range(NT):
                for m in range(2):
                    last = pe.matmul(ps[0:TP, 2, 16 + t:17 + t], qpt[:, m, t * TP:(t + 1) * TP], ksum[:, m:m + 1],
                                     start=(t == 0 and m == 0), stop=(t == NT - 1 and m == 1), skip_group_check=True)
            last.then_inc(d_mm, 1)
            for c in range(KT):
                b = (5, 0)[c % 2]
                if c >= 2:
                    pe.wait_ge(yt_ready, c - 1)
                for m in range(2):
                    for h in range(2):
                        last = pe.matmul(ps[:, b + h, 0:HALF], kv[:, m, c * 128:(c + 1) * 128], qpt[:, m, h * HALF:(h + 1) * HALF],
                                         start=(m == 0), stop=(m == 1))
                last.then_inc(yt_mm, 1)
            s = PIECE["Wo"]
            pe.wait_ge(split_done, s + 1)
            pe.wait_ge(yt_ready, KT)
            pe.wait_ge(rec_ready, 1)
            for t in range(NT):
                for k in range(KT):
                    last = mm3(ps[0:TP, AGG[t], :], yt_hi[:, k, t * TP:(t + 1) * TP], yt_lo[:, k, t * TP:(t + 1) * TP],
                               piece_hi[s % 2][:, k, :], piece_lo[s % 2][:, k, :], k == 0, k == KT - 1)
                last.then_inc(wo_mm, 1)
            pe.wait_ge(wo_mm, NT)
            pe.sem_inc(piece_used, 1)
            relation_chunk(1, 5)
            pe.wait_ge(h1t_ready, NT)
            for t in range(NT):
                pe.wait_ge(yn_ready, t + 1)
                if t >= 2:
                    pe.wait_ge(h2_scaled, t - 1)
                for c in range(KT):
                    last = pe.transpose(ps[:, (7, 4)[t % 2], c * TP:(c + 1) * TP], yn[:, t % 2, c * 128:(c + 1) * 128], ident[0:TP, 0:TP])
                last.then_inc(h2_t, 1)
            s = PIECE["W1"]
            pe.wait_ge(split_done, s + 1)
            pe.wait_ge(h2t_ready, NT)
            pe.wait_ge(y_ready, 1)
            for c in range(KT):
                b = (0, 5)[c % 2]
                if c >= 2:
                    pe.wait_ge(act_done, c - 1)
                for k in range(KT):
                    for h in range(2):
                        last = mm3(ps[:, b + h, 0:HALF], piece_hi[s % 2][:, k, c * 128:(c + 1) * 128],
                                   piece_lo[s % 2][:, k, c * 128:(c + 1) * 128], h2t_hi[:, k, h * HALF:(h + 1) * HALF],
                                   h2t_lo[:, k, h * HALF:(h + 1) * HALF], k == 0, k == KT - 1)
                last.then_inc(act_mm, 1)
            pe.wait_ge(act_mm, KT)
            pe.sem_inc(piece_used, 1)
            relation_chunk(1, 6)
            s = PIECE["W2"]
            pe.wait_ge(split_done, s + 1)
            pe.wait_ge(act_ready, KT)
            for t in range(NT):
                for k in range(KT):
                    last = mm3(ps[0:TP, AGG[t], :], act_hi[:, k, t * TP:(t + 1) * TP], act_lo[:, k, t * TP:(t + 1) * TP],
                               piece_hi[s % 2][:, k, :], piece_lo[s % 2][:, k, :], k == 0, k == KT - 1)
                last.then_inc(w2_mm, 1)
            pe.wait_ge(w2_mm, NT)
            pe.sem_inc(piece_used, 1)
            relation_chunk(1, 7)
            pe.wait_ge(h2_scaled, NT)
            layer(1)
            pe.wait_ge(u_ready, 4 * NT)
            for t in range(NT):
                pe.wait_ge(x1n_ready, t + 1)
                if t >= 3:
                    pe.wait_ge(x1t_ready, t - 2)
                for c in range(KT):
                    last = pe.transpose(ps[:, UB[t % 3], c * TP:(c + 1) * TP], x1n[:, t % 2, :].rearrange("p (f t) -> p t f", t=KT)[:, c],
                                        ident[0:TP, 0:TP])
                last.then_inc(x1_t, 1)
            pe.wait_ge(router_w_ready, 1)
            pe.wait_ge(x1t_ready, NT)
            for t in range(NT):
                for c in range(KT):
                    last = mm3(ps[0:TP, 4, t * 2 * E:(t + 1) * 2 * E], x1t_hi[:, c, t * TP:(t + 1) * TP], x1t_lo[:, c, t * TP:(t + 1) * TP],
                               router_hi[:, c, :], router_lo[:, c, :], t == 0 and c == 0, t == NT - 1 and c == KT - 1, skip=True)
            last.then_inc(logit_mm, 1)
            pe.wait_ge(route_ready, 1)
            for t in range(4):
                pe.transpose(ps[0:2 * E, 4, t * TP:(t + 1) * TP], route[:, t].rearrange("p b e -> p (b e)"), ident[0:TP, 0:TP])
            pe.transpose(ps[0:2 * E, 7, 0:TP], route[:, 4].rearrange("p b e -> p (b e)"), ident[0:TP, 0:TP]).then_inc(route_tr, 1)

            def hidden(e):
                pe.wait_ge(ex_split, e + 1)
                if e == 0:
                    pe.wait_ge(route_t_ready, 1)
                for h in range(2):
                    i = 2 * e + h
                    if i >= 3:
                        pe.wait_ge(hid_ready, i - 2)
                    for k in range(KT):
                        last = mm3(ps[:, UB[i % 3], 0:HALF], ex_hi[:, e % 4, 0, k * FF:(k + 1) * FF], ex_lo[:, e % 4, 0, k * FF:(k + 1) * FF],
                                   x1t_hi[:, k, h * HALF:(h + 1) * HALF], x1t_lo[:, k, h * HALF:(h + 1) * HALF], k == 0, k == KT - 1)
                    last.then_inc(hid_mm, 1)
            hidden(0)
            for e in range(NX):
                if e + 1 < NX:
                    hidden(e + 1)
                pe.wait_ge(hg_ready, 2 * e + 2)
                for t in range(NT):
                    last = mm3(ps[0:TP, AGG[t], :], hg_hi[:, e % 2, t * TP:(t + 1) * TP], hg_lo[:, e % 2, t * TP:(t + 1) * TP],
                               ex_hi[:, e % 4, 1, :], ex_lo[:, e % 4, 1, :], e == 0, False)
                last.then_inc(ex_used, 1)
            pe.wait_ge(route_split, 1)
            for t in range(NT):
                last = mm3(ps[0:TP, AGG[t], :], route_hi[:, t * TP:(t + 1) * TP], route_lo[:, t * TP:(t + 1) * TP],
                           out_b_hi[:], out_b_lo[:], False, True)
                last.then_inc(ffn_mm, 1)


_INS = ['x', 'src', 'dst', 'edge_type_2', 'L0_gnn_basis1', 'L0_gnn_att1', 'L0_gnn_gate_w1', 'L0_gnn_root1',
        'L0_gnn_bias1', 'L0_gnn_basis2', 'L0_gnn_att2', 'L0_gnn_gate_w2', 'L0_gnn_root2', 'L0_gnn_bias2',
        'L0_mix_w', 'L0_mix_Wkqv', 'L0_mix_bkqv', 'L0_mix_Wo', 'L0_mix_bo', 'L0_mix_W1', 'L0_mix_b1',
        'L0_mix_W2', 'L0_mix_b2', 'L0_mix_g1', 'L0_mix_be1', 'L0_mix_g2', 'L0_mix_be2', 'L0_ffn_Wr_sp',
        'L0_ffn_br_sp', 'L0_ffn_Wr_fq', 'L0_ffn_br_fq', 'L0_ffn_Ws1', 'L0_ffn_bs1', 'L0_ffn_Ws2',
        'L0_ffn_bs2', 'L0_ffn_W1_sp', 'L0_ffn_b1_sp', 'L0_ffn_W2_sp', 'L0_ffn_b2_sp', 'L0_ffn_W1_fq',
        'L0_ffn_b1_fq', 'L0_ffn_W2_fq', 'L0_ffn_b2_fq']
_OUTS = [((NODES, D), 'float32')]


def kernel(**inputs):
    import numpy as _np
    import concourse.bacc as _bacc
    from concourse import mybir as _mybir
    from concourse.bass_utils import run_bass_kernel_spmd as _run

    nc = _bacc.Bacc("TRN2", target_bir_lowering=False, num_devices=1)
    arrays, args = {}, []
    for name in _INS:
        a = _np.ascontiguousarray(inputs[name])
        arrays[f"in_{name}_dram"] = a
        args.append(nc.dram_tensor(f"in_{name}_dram", a.shape, _mybir.dt.from_np(a.dtype), kind="ExternalInput").ap())
    for i, (shape, dtype) in enumerate(_OUTS):
        dt = _mybir.dt.from_np(_np.dtype(dtype))
        args.append(nc.dram_tensor(f"out_{i}_dram", shape, dt, kind="ExternalOutput").ap())
    gnn_mix_ffn(nc, *args)
    r = _run(nc, [arrays], core_ids=[0])
    return r.results[0]["out_0_dram"]
```

```python
from contextlib import ExitStack

import concourse.bass as bass
from concourse import mybir

F32, F32R, F16 = mybir.dt.float32, mybir.dt.float32r, mybir.dt.float16
I32, I16 = mybir.dt.int32, mybir.dt.int16
ALU, ACT, AX = mybir.AluOpType, mybir.ActivationFunctionType, mybir.AxisListType
RMAX = bass.bass_isa.ReduceOp.max

NODES, D = 625, 512
NT, TP = 5, 125
NPAD, HALF = 628, 314
KT = D // 128
EDGES, ET, TE = 10000, 80, 125
CW = 626
CB = CW // 2
REL_KEY = 1000
EXACT = 4096
REL, BASES = 2, 30
GB = 8
NG = (BASES + GB - 1) // GB
QI = 16
CHUNKS = D // QI // 4
PARTS = 2 * CHUNKS * NG
WIDE = 5 * NG
M = 256
E, FF = 8, 128
BANK = 512


def gnn_mix_ffn(nc, x, src, dst, edge_type, basis1, att1, gate_w1, root1, bias1, basis2, att2, gate_w2,
                root2, bias2, w, Wkqv, bkqv, Wo, bo, W1, b1, W2, b2, g1, be1, g2, be2, Wr_sp, br_sp,
                Wr_fq, br_fq, Ws1, bs1, Ws2, bs2, W1_sp, b1_sp, W2_sp, b2_sp, W1_fq, b1_fq, W2_fq,
                b2_fq, out):
    with ExitStack() as ctx:
        def sem(name):
            return ctx.enter_context(nc.semaphore(name))

        top = [16512]

        def region(size):
            at = top[0]
            top[0] += -(-size // 32) * 32
            assert top[0] <= 229344, top[0]
            return at

        def place(name, shape, dtype, at):
            return nc.alloc_sbuf_tensor_at(name, shape, dtype, offset=-(-at // 32) * 32)

        def own(name, shape, dtype=F32):
            n = {F32: 4, F32R: 4, I32: 4, F16: 2, I16: 2}[dtype]
            for s in shape[1:]:
                n *= s
            return place(name, shape, dtype, region(n))

        ident = own("ident", [128, 128])
        colv = own("colv", [128, 45])
        bias_row = own("bias_row", [128, 6, D])
        gate_hi = own("gate_hi", [128, 2, KT, REL], F32R)
        gate_lo = own("gate_lo", [128, 2, KT, REL], F32R)
        att_col = own("att_col", [128, 2, NG, REL])
        sel_q = own("sel_q", [128, QI])
        sel_att = own("sel_att", [128, 2, NG, REL, QI])
        gates = own("gates", [TP, NT, REL])
        bn = own("bn", [TP, NT, 6])
        stat = own("stat", [TP, NT, 2])
        veps = own("veps", [TP, NT])
        rstd = own("rstd", [TP, NT])
        neg_half_pow = own("neg_half_pow", [TP, NT])
        neg_half = own("neg_half", [128, 1])
        ones = own("ones", [128, 1])
        xd = own("xd", [TP, NT])
        ksum = own("ksum", [128, 2])
        rec = own("rec", [TP, NT])
        range_i = own("range_i", [1, 2, NT], I32)
        count_acc = own("count_acc", [TP, NT])
        count_max = own("count_max", [TP, NT])
        many_i = own("many_i", [1, 1], I32)

        KB628, KB512 = KT * NPAD * 4, NT * D * 4
        counts = own("counts", [TP, NT, REL * CW], I16)
        r_ring = region(4 * 8192)
        r_split = region(4 * 8192)
        stag = own("stag", [128, 2, D])
        r_wraw = region(KT * REL * D * 4)
        r_raw = region(2 * KT * D * 4)
        r_ht = region(2 * KB628)
        r_h1t = region(KB512)
        r_u = region(2 * KB512)
        r_cf = region(NT * CW * 4)
        r_extra = region(18720)

        ring = [place(f"ring{i}", [128, 4 * D], F32, r_ring + i * 8192) for i in range(8)]
        xa = place("xa", [TP, NT, D], F32, r_u)
        counts_read = place("counts_read", [TP, REL * CW], F16, r_u)
        xn = place("xn", [TP, NT, D], F32, r_h1t)
        xn2 = place("xn2", [TP, NT, D], F32, r_extra)
        gate_rows = place("gate_rows", [REL, 2, D], F32, r_wraw)
        att_rep = place("att_rep", [REL, 2, BASES * QI], F32, r_wraw + 8448)
        att_rows = place("att_rows", [REL, 2, BASES], F32, r_wraw + 8192)
        row_vec = place("row_vec", [45, 128], F32, r_wraw + 4096)
        oh_n = place("oh_n", [TE, 4, CW], F16, r_cf)
        oh_m = place("oh_m", [TE, 4, REL * TE], F16, r_cf + 4 * CW * 2)
        zeros = place("zeros", [TE, TE], F16, r_cf + 4 * CW * 2 + 4 * REL * TE * 2 + 32)
        xt_tmp = [place(f"xt_tmp{i}", [128, KT, TP], F32, r_cf + 8192 + i * 2016) for i in range(2)]
        o = r_u + KB512
        iota_n = place("iota_n", [TE, CW], F16, o)
        iota_m = place("iota_m", [TE, REL * TE], F16, o + 1280)
        keys = place("keys", [TE, 2, ET], F32, o + 2528)
        key_m = place("key_m", [TE, NT, ET], F32, o + 3200)
        edge_i = place("edge_i", [ET, 3, TE], I32, o + 4800)
        edge_f = place("edge_f", [ET, 3, TE], F32, o + 6304)
        key_r = place("key_r", [ET, TE], F32, o + 7808)
        o += 8320
        mnmx = place("mnmx", [ET, 2], F32, o)
        tile_id = place("tile_id", [ET, 2, NT], F32, o + 32)
        tile_ii = place("tile_ii", [ET, 2, NT], I32, o + 96)
        node_lo = place("node_lo", [ET, NT], F32, o + 160)
        in_lo = place("in_lo", [ET, NT], F32, o + 192)
        in_hi = place("in_hi", [ET, NT], F32, o + 224)
        bound = place("bound", [ET, 2, NT], F32, o + 256)
        bound_all = place("bound_all", [ET, 2, NT], F32, o + 320)
        range_f = place("range_f", [1, 2, NT], F32, o + 384)
        mean_acc = place("mean_acc", [TP, 2, NT], F32, o + 448)
        square_acc = place("square_acc", [TP, 2, NT], F32, o + 512)
        minus_mean = place("minus_mean", [TP, 2, NT], F32, o + 576)
        shift = place("shift", [TP, 2, NT], F32, o + 640)
        rstd_x = place("rstd_x", [TP, 2, NT], F32, o + 704)
        w_raw = place("w_raw", [128, KT, REL, D], F32, r_wraw)
        piece_raw = [place(f"piece_raw{i}", [128, KT, D], F32, r_raw + i * KT * D * 4) for i in range(2)]
        piece_hi = [place(f"piece_hi{i}", [128, KT, D], F32R, a) for i, a in
                    enumerate((r_split, r_split + 16384, r_wraw))]
        piece_lo = [place(f"piece_lo{i}", [128, KT, D], F32R, a + 8192) for i, a in
                    enumerate((r_split, r_split + 16384, r_wraw))]
        ht_hi = place("ht_hi", [128, KT, NPAD], F32R, r_ht)
        ht_lo = place("ht_lo", [128, KT, NPAD], F32R, r_ht + KB628)
        u_hi = [place(f"u_hi{l}", [TP, NT, D], F32R, a) for l, a in enumerate((r_u + KB512, r_ring))]
        u_lo = [place(f"u_lo{l}", [TP, NT, D], F32R, a) for l, a in enumerate((r_extra, r_ring + KB512))]
        cf = place("cf", [TP, NT, CW], F32R, r_cf)
        row_tmp = place("row_tmp", [TP, 2, D], F32, r_extra + 14336)
        xt_hi = place("xt_hi", [128, KT, NPAD], F32R, r_ht)
        xt_lo = place("xt_lo", [128, KT, NPAD], F32R, r_ht + KB628)
        kq_hi = place("kq_hi", [128, KT, NPAD], F32R, r_u)
        kq_lo = place("kq_lo", [128, KT, NPAD], F32R, r_u + KB628)
        y = place("y", [TP, NT, D], F32, r_u)
        v = place("v", [TP, NT, D], F32, r_u + KB512)
        kp = place("kp", [TP, NT, M], F32, r_cf)
        qpt = place("qpt", [128, 2, NPAD], F32, r_cf + 5120)
        wt_hi = place("wt_hi", [128, KT, M], F32R, r_extra + 10240)
        wt_lo = place("wt_lo", [128, KT, M], F32R, r_extra + 10240 + 4096)
        w_nat = place("w_nat", [128, 2, D], F32, r_raw + 8192)
        feat = place("feat", [TP, 2, M], F32, r_extra + 4096)
        square = place("square", [128, NPAD], F32, r_extra + 6144)
        kv = place("kv", [128, 2, D], F32, r_extra + 10240)
        yt_hi = place("yt_hi", [128, KT, NPAD], F32R, r_ht)
        yt_lo = place("yt_lo", [128, KT, NPAD], F32R, r_ht + KB628)
        x_again = place("x_again", [TP, NT, D], F32, r_h1t)
        yn = place("yn", [TP, 2, D], F32, r_extra + 4096)
        h2_tmp = [place(f"h2_tmp{i}", [128, KT, TP], F32, r_extra + i * 2016) for i in range(2)]
        h2t_hi = place("h2t_hi", [128, KT, NPAD], F32R, r_ht)
        h2t_lo = place("h2t_lo", [128, KT, NPAD], F32R, r_ht + KB628)
        act_tmp = place("act_tmp", [128, 2, NPAD], F32, r_extra + 10240)
        act_hi = place("act_hi", [128, KT, NPAD], F32R, r_u + KB512)
        act_lo = place("act_lo", [128, KT, NPAD], F32R, r_u + KB512 + KB628)
        x1 = place("x1", [TP, NT, D], F32, r_wraw)
        x1n = place("x1n", [TP, 2, D], F32, r_extra)
        x1t_hi = place("x1t_hi", [128, KT, NPAD], F32R, r_ht)
        x1t_lo = place("x1t_lo", [128, KT, NPAD], F32R, r_ht + KB628)
        router_raw = place("router_raw", [128, KT, 2 * E], F32, r_extra + 4096)
        router_hi = place("router_hi", [128, KT, 2 * E], F32R, r_extra + 4096 + 256)
        router_lo = place("router_lo", [128, KT, 2 * E], F32R, r_extra + 4096 + 512)
        router_b = place("router_b", [TP, 2 * E], F32, r_extra + 4096 + 768)
        o = r_extra + 4096 + 1024
        logit = place("logit", [TP, NT, 2, E], F32, o)
        lmax = place("lmax", [TP, NT, 2], F32, o + 320)
        shifted = place("shifted", [TP, NT, 2, E], F32, o + 384)
        expo = place("expo", [TP, NT, 2, E], F32, o + 704)
        denom = place("denom", [TP, NT, 2], F32, o + 1024)
        gate_p = place("gate_p", [TP, NT, 2], F32, o + 1088)
        rank = place("rank", [TP, NT, 2, E], F32, o + 1152)
        score = place("score", [TP, NT, 2, E], F32, o + 1472)
        best = place("best", [TP, NT, 2], F32, o + 1792)
        route = place("route", [TP, NT, 2, E], F32, o + 1856)
        o += 2208
        route_t = place("route_t", [2 * E, NPAD], F32, o)
        route_hi = place("route_hi", [2 * E, NPAD], F32R, o + 2528)
        route_lo = place("route_lo", [2 * E, NPAD], F32R, o + 2 * 2528)
        o += 3 * 2528
        assert o <= r_extra + 18720
        out_bias = place("out_bias", [2 * E, D], F32, r_raw + 4 * 4096 - 2048)
        out_b_hi = place("out_b_hi", [2 * E, D], F32R, r_wraw + KB512)
        out_b_lo = place("out_b_lo", [2 * E, D], F32R, r_wraw + KB512 + 2048)
        route_all = place("route_all", [128, 2 * E, NPAD], F32, r_h1t)
        assert r_h1t + 2 * E * NPAD * 4 <= r_extra
        XR = 3
        ex_raw = place("ex_raw", [128, XR, 2, D], F32, r_raw)
        ex_hi = place("ex_hi", [128, 4, 2, D], F32R, r_split)
        ex_lo = place("ex_lo", [128, 4, 2, D], F32R, r_split + 16384)
        o = r_ring
        hid = place("hid", [128, 4, HALF], F32, o)
        gated = place("gated", [128, 4, HALF], F32, o + 5024)
        hg_hi = place("hg_hi", [128, 2, NPAD], F32R, o + 10048)
        hg_lo = place("hg_lo", [128, 2, NPAD], F32R, o + 15072)
        final = place("final", [TP, 2, D], F32, r_extra)

        ps = ctx.enter_context(nc.psum_tensor("ps", [128, 8, BANK], F32))
        rel_dram = [nc.dram_tensor(f"rel_dram{l}", (KT, REL, CHUNKS, QI, D), F32, kind="Internal").ap()
                    for l in range(2)]
        route_dram = nc.dram_tensor("route_dram", (2 * E, NPAD), F32, kind="Internal").ap()

        edges_in, x_in, rows_in, smalls_in = sem("edges_in"), sem("x_in"), sem("rows_in"), sem("smalls_in")
        mean_sum, square_sum, minus_mean_ready = sem("mean_sum"), sem("square_sum"), sem("minus_mean_ready")
        pads_ready, sel_q_ready, att_col_ready = sem("pads_ready"), sem("sel_q_ready"), sem("att_col_ready")
        count_sum, count_bound, many_ready, rest_ready, rest_used = (
            sem("count_sum"), sem("count_bound"), sem("many_ready"), sem("rest_ready"), sem("rest_used"))
        biases_joined = sem("biases_joined")
        basis_in = [sem(f"basis_in{i}") for i in range(8)]
        raw_in = [sem(f"raw_in{i}") for i in range(2)]
        rel_out = [sem(f"rel_out{i}") for i in range(2)]
        rel_back = [sem(f"rel_back{t}") for t in range(KT)]
        w_in, router_in, route_out, route_back = sem("w_in"), sem("router_in"), sem("route_out"), sem("route_back")
        x_again_in = sem("x_again_in")
        out_b_in = sem("out_b_in")
        ex_in = [sem(f"ex_in{i}") for i in range(XR)]
        stored = [sem(f"stored{i}") for i in range(2)]
        ident_zero, ident_ready, iotas_ready, consts_ready = (
            sem("ident_zero"), sem("ident_ready"), sem("iotas_ready"), sem("consts_ready"))
        key_ready, bound_ready, bound_max, keys_t, range_ready = (
            sem("key_ready"), sem("bound_ready"), sem("bound_max"), sem("keys_t"), sem("range_ready"))
        one_hot, pair_used, count_ready = sem("one_hot"), sem("pair_used"), sem("count_ready")
        var_ready, rstd_ready, xn_ready, xn2_ready = sem("var_ready"), sem("rstd_ready"), sem("xn_ready"), sem("xn2_ready")
        cols_t, cols_ready, gate_rows_t, gate_w_hi, gate_w_ready = (
            sem("cols_t"), sem("cols_ready"), sem("gate_rows_t"), sem("gate_w_hi"), sem("gate_w_ready"))
        sel_ready, att_ready = sem("sel_ready"), sem("att_ready")
        hT_t, hT_hi, hT_ready = sem("hT_t"), sem("hT_hi"), sem("hT_ready")
        basis_used, rel_sum, rel_evac = sem("basis_used"), sem("rel_sum"), sem("rel_evac")
        split_done, piece_used = sem("split_done"), sem("piece_used")
        gate_mm, gates_ready = sem("gate_mm"), sem("gates_ready")
        u_mm, u_hi_done, u_ready, cf_ready, rel_applied, agg_done = (
            sem("u_mm"), sem("u_hi_done"), sem("u_ready"), sem("cf_ready"), sem("rel_applied"), sem("agg_done"))
        h_added, h_relu = sem("h_added"), sem("h_relu")
        xt_t, xt_scaled, xt_hi_done, xt_ready = sem("xt_t"), sem("xt_scaled"), sem("xt_hi_done"), sem("xt_ready")
        wt_t, wt_hi_done, wt_ready = sem("wt_t"), sem("wt_hi_done"), sem("wt_ready")
        kq_mm, kq_hi_done, sq_ready, kq_ready, sq_used, xd_mm, xd_ready = (
            sem("kq_mm"), sem("kq_hi_done"), sem("sq_ready"), sem("kq_ready"), sem("sq_used"), sem("xd_mm"), sem("xd_ready"))
        feat_mm, feat_exp, feat_ready, qp_t, qpt_ready = (
            sem("feat_mm"), sem("feat_exp"), sem("feat_ready"), sem("qp_t"), sem("qpt_ready"))
        v_mm, v_ready, kv_mm, kv_ready, yt_mm, yt_hi_done, yt_ready, d_mm, rec_ready = (
            sem("v_mm"), sem("v_ready"), sem("kv_mm"), sem("kv_ready"), sem("yt_mm"), sem("yt_hi_done"),
            sem("yt_ready"), sem("d_mm"), sem("rec_ready"))
        wo_mm, y_ready, yn_ready, h2_t, h2_scaled, h2_hi_done, h2t_ready = (
            sem("wo_mm"), sem("y_ready"), sem("yn_ready"), sem("h2_t"), sem("h2_scaled"), sem("h2_hi_done"), sem("h2t_ready"))
        y_plus_b = sem("y_plus_b")
        act_mm, act_done, act_ready, w2_mm, xm_ready, xm_plus_x = (
            sem("act_mm"), sem("act_done"), sem("act_ready"), sem("w2_mm"), sem("xm_ready"), sem("xm_plus_x"))
        x1n_ready, x1_t, x1_hi_done, x1t_ready = (
            sem("x1n_ready"), sem("x1_t"), sem("x1_hi_done"), sem("x1t_ready"))
        router_w_ready, logit_mm, shift_ready, expo_ready, route_ready, route_tr, route_t_ready, route_split = (
            sem("router_w_ready"), sem("logit_mm"), sem("shift_ready"), sem("expo_ready"), sem("route_ready"),
            sem("route_tr"), sem("route_t_ready"), sem("route_split"))
        x1_plus_b = sem("x1_plus_b")
        ex_split, ex_used, hid_mm, hid_ready, hg_ready, ffn_mm, final_ready = (
            sem("ex_split"), sem("ex_used"), sem("hid_mm"), sem("hid_ready"), sem("hg_ready"), sem("ffn_mm"), sem("final_ready"))
        dve_own, act_own, pool_own = sem("dve_own"), sem("act_own"), sem("pool_own")

        basis_rows = [b.rearrange("b (c q t) o -> c b q (t o)", q=QI, t=KT) for b in (basis1, basis2)]
        LOADED = {"k": 0, "q": 1, "v": 2, "Wo": 3, "W1": 4, "W2": 5, "root1": 6, "root2": 7}
        ORDER = ["k", "q", "v", "Wo", "W1", "W2", "rel1_0", "root1", "rel1_1", "rel2_0", "root2", "rel2_1"]
        PIECE = {name: n for n, name in enumerate(ORDER)}
        SPLIT_OF_LOAD = [PIECE[name] for name in LOADED]

        def piece(name):
            s = PIECE[name]
            return s, piece_hi[s % 2 if s else 2], piece_lo[s % 2 if s else 2]
        perm = "(p t) n -> p t n"
        nat = "(t p) n -> p t n"
        piece_src = {
            "root1": [root1.rearrange(perm, t=KT)], "root2": [root2.rearrange(perm, t=KT)],
            "k": [Wkqv[:, 0:D].rearrange(nat, p=128)], "q": [Wkqv[:, D:2 * D].rearrange(nat, p=128)],
            "v": [Wkqv[:, 2 * D:3 * D].rearrange(nat, p=128)], "Wo": [Wo.rearrange(nat, p=128)],
            "W1": [W1.rearrange(nat, p=128)], "W2": [W2.rearrange(nat, p=128)]}
        NX = 2 * E + 1
        ex_w1 = [Ws1] + [W1_sp[e] for e in range(E)] + [W1_fq[e] for e in range(E)]
        ex_w2 = [Ws2] + [W2_sp[e] for e in range(E)] + [W2_fq[e] for e in range(E)]
        C_G1, C_BE1, C_G2, C_BE2, C_BK, C_B1, C_EXP = 0, 4, 8, 12, 16, 24, 28

        AGG = [0, 1, 2, 5, 6]
        UB = [7, 4, 3]
        LB = [7, 4]
        COUNT_BANK = [[0, 1], [2, 7]]

        def basis_turn(i):
            if i < WIDE:
                return i % 8, i // 8 + 1
            return i % 4, (WIDE - 1 - i % 4) // 8 + 1 + (i - WIDE) // 4 + 1

        def rel_bank(ch):
            return 3 + ch % 2 if ch < 2 * CHUNKS - 2 else 3

        block = ctx.enter_context(nc.Block())

        @block.sync
        def _(sp):
            def load_part(i):
                ch, g = divmod(i, NG)
                nb = min(GB, BASES - g * GB)
                slot, _ = basis_turn(i)
                if i >= WIDE:
                    sp.wait_ge(basis_used, i - 4 + 1)
                elif i >= 8:
                    sp.wait_ge(basis_used, i - 8 + 1)
                sp.dma_start(ring[slot][0:nb * QI, :], basis_rows[ch // CHUNKS][ch % CHUNKS, g * GB:g * GB + nb]
                             ).then_inc(basis_in[slot], 16)

            def store_chunk(ch):
                sp.wait_ge(rel_evac, ch + 1)
                sp.dma_start(rel_dram[ch // CHUNKS][:, :, ch % CHUNKS].rearrange("t r q n -> (t r) q n"),
                             stag[:, ch % 2, :]).then_inc(rel_out[ch % 2], 16)

            def read_relations(l):
                for s in rel_out:
                    sp.wait_ge(s, 16 * (CHUNKS // 2) * (l + 1))
                if l == 0:
                    sp.wait_ge(piece_used, PIECE["k"] + 1)
                else:
                    sp.wait_ge(split_done, PIECE["rel1_1"] + 1)
                for t in range(KT):
                    sp.dma_start(w_raw[:, t, :, :], rel_dram[l][t].rearrange("r c q n -> (c q) r n")
                                 ).then_inc(rel_back[t], 16)

            def load_piece(name):
                n = LOADED[name]
                if n >= 2:
                    sp.wait_ge(split_done, SPLIT_OF_LOAD[n - 2] + 1)
                for s in piece_src[name]:
                    sp.dma_start(piece_raw[n % 2][:, :, :], s).then_inc(raw_in[n % 2], 16)

            for k, a in enumerate((src, dst, edge_type)):
                sp.dma_start(edge_i[:, k, :], a.rearrange("(t e) -> t e", e=TE)).then_inc(edges_in, 16)
            for l, a in enumerate((att1, att2)):
                sp.dma_start(att_rows[:, l, :], a).then_inc(rows_in, 16)
            for l, gw in enumerate((gate_w1, gate_w2)):
                sp.dma_start(gate_rows[:, l, :], gw.rearrange("r i o -> r (i o)")).then_inc(rows_in, 16)
            at = 0
            for a in (g1, be1, g2, be2, bkqv[0:2 * D], b1, bs1):
                n = a.shape[0] // 128
                sp.dma_start(row_vec[at:at + n, :], a.rearrange("(t p) -> t p", p=128)).then_inc(rows_in, 16)
                at += n
            for a in (b1_sp, b1_fq):
                sp.dma_start(row_vec[at:at + E, :], a).then_inc(rows_in, 16)
                at += E
            sp.dma_start(xa[:, :, :], x.rearrange("(t p) n -> p t n", p=TP)).then_inc(x_in, 16)
            for i in range(4):
                load_part(i)
            sp.dma_start(w_nat[:, :, :], w.rearrange("(t p) n -> p t n", p=128)).then_inc(w_in, 16)
            for i in range(4, 8):
                load_part(i)
            load_piece("k")
            for n, a in enumerate((bias1, bias2, bkqv[2 * D:3 * D], bo, b2, bs2)):
                sp.dma_start(bias_row[:, n, :], a.partition_broadcast(128)).then_inc(smalls_in, 16)
            between = {12: [(load_piece, "q")], 22: [(load_piece, "v")], 26: [(load_piece, "Wo")],
                       30: [(load_piece, "W1")], 36: [(load_piece, "W2")], 39: [(read_relations, 0)],
                       47: [(load_piece, "root1")], 60: [(load_piece, "root2")]}
            for ch in range(2 * CHUNKS):
                after = NG * ch + (12 if NG * ch + 12 <= WIDE else 9)
                between.setdefault(min(after, PARTS - 1), []).insert(0, (store_chunk, ch))
            between[PARTS - 1].sort(key=lambda step: step[1])
            for i in range(8, PARTS):
                load_part(i)
                for step, what in between.get(i, []):
                    if step is load_piece and what == "q":
                        sp.wait_ge(wt_t, 2)
                    step(what)
            sp.wait_ge(hT_t, NT)
            sp.dma_start(x_again[:, :, :], x.rearrange("(t p) n -> p t n", p=TP)).then_inc(x_again_in, 16)
            read_relations(1)
            sp.wait_ge(rel_applied, 2)
            for n, a in enumerate((Wr_sp, Wr_fq)):
                sp.dma_start(router_raw[:, :, n * E:(n + 1) * E], a.rearrange("(p t) e -> p t e", p=128),
                             allow_slow_non_contiguous=True).then_inc(router_in, 16)
            for n, a in enumerate((br_sp, br_fq)):
                sp.dma_start(router_b[:, n * E:(n + 1) * E], a.partition_broadcast(TP),
                             allow_slow_non_contiguous=True).then_inc(router_in, 16)

            def load_expert(e):
                if e == 0:
                    sp.wait_ge(split_done, PIECE["root2"] + 1)
                if e >= XR:
                    sp.wait_ge(ex_split, e - XR + 1)
                sp.dma_start(ex_raw[:, e % XR, 0, :].rearrange("p (t f) -> p t f", t=KT),
                             ex_w1[e].rearrange("(p t) f -> p t f", p=128)).then_inc(ex_in[e % XR], 16)
                sp.dma_start(ex_raw[:, e % XR, 1, :], ex_w2[e]).then_inc(ex_in[e % XR], 16)
            for e in range(XR):
                load_expert(e)
            for n, a in enumerate((b2_sp, b2_fq)):
                sp.dma_start(out_bias[n * E:(n + 1) * E, :], a).then_inc(out_b_in, 16)
            sp.wait_ge(route_t_ready, 1)
            sp.dma_start(route_dram, route_t[:, :]).then_inc(route_out, 16)
            sp.wait_ge(route_out, 16)
            for e in range(2 * E):
                sp.dma_start(route_all[:, e, :], route_dram[e].partition_broadcast(128)).then_inc(route_back, 16)
            for e in range(XR, NX):
                load_expert(e)
            for t in range(NT):
                sp.wait_ge(final_ready, t + 1)
                sp.dma_start(out[t * TP:(t + 1) * TP, :], final[:, t % 2, :]).then_inc(stored[t % 2], 16)
            sp.wait_ge(stored[0], 16 * 3)
            sp.wait_ge(stored[1], 16 * 2)

        @block.gpsimd
        def _(pool):
            n = [0]

            def own_step(ins):
                ins.then_inc(pool_own, 1)
                n[0] += 1
                pool.wait_ge(pool_own, n[0])

            pool.memset(ident[:], 0.0).then_inc(ident_zero, 1)
            pool.iota(iota_n[:], pattern=[[1, CW]], base=0, channel_multiplier=0,
                      allow_small_or_imprecise_dtypes=True).then_inc(iotas_ready, 1)
            pool.iota(iota_m[:], pattern=[[REL_KEY, REL], [1, TE]], base=0, channel_multiplier=0,
                      allow_small_or_imprecise_dtypes=True).then_inc(iotas_ready, 1)
            pool.iota(tile_id[:], pattern=[[0, 2], [0, NT]], base=0, channel_multiplier=1,
                      allow_small_or_imprecise_dtypes=True).then_inc(iotas_ready, 1)
            pool.iota(node_lo[:], pattern=[[TP, NT]], base=0, channel_multiplier=0,
                      allow_small_or_imprecise_dtypes=True).then_inc(iotas_ready, 1)
            pool.wait_ge(ident_zero, 1)
            pool.affine_select(out=ident[:], in_=ident[:], compare_op=ALU.not_equal, fill=1.0, base=0,
                               pattern=[[-1, 128]], channel_multiplier=1).then_inc(ident_ready, 1)
            pool.memset(zeros[:], 0.0).then_inc(consts_ready, 1)
            pool.memset(neg_half_pow[:], -0.5).then_inc(consts_ready, 1)
            pool.memset(neg_half[:], -0.5).then_inc(consts_ready, 1)
            pool.memset(ones[:], 1.0).then_inc(consts_ready, 1)
            pool.memset(att_col[:], 0.0).then_inc(consts_ready, 1)
            pool.wait_ge(consts_ready, 5)
            pool.wait_ge(bound_ready, 1)
            pool.partition_all_reduce(bound_all[:].rearrange("p a j -> p (a j)"),
                                      bound[:].rearrange("p a j -> p (a j)"), ET, RMAX).then_inc(bound_max, 1)
            for a in (xt_hi, xt_lo):
                pool.memset(a[:, :, NODES:NPAD].bitcast(F32), 0.0).then_inc(pads_ready, 1)
            for k in range(2):
                pool.wait_ge(mean_sum, k + 1)
                pool.tensor_scalar(minus_mean[:, k, :], mean_acc[:, k, :], -1.0 / D, None, ALU.mult).then_inc(minus_mean_ready, 1)
                pool.wait_ge(square_sum, k + 1)
                own_step(pool.tensor_scalar(rstd_x[:, k, :], square_acc[:, k, :], 1.0 / D, 1e-5, ALU.mult, ALU.add))
                own_step(pool.tensor_tensor(rstd_x[:, k, :], rstd_x[:, k, :], neg_half_pow[:], ALU.pow))
                pool.tensor_tensor(shift[:, k, :], minus_mean[:, k, :], rstd_x[:, k, :], ALU.mult).then_inc(rstd_ready, 1)

            def power(k, t):
                pool.wait_ge(var_ready, k)
                pool.tensor_tensor(rstd[:, t:t + 1], veps[:, t:t + 1], neg_half_pow[:, t:t + 1], ALU.pow).then_inc(rstd_ready, 1)

            def split(name):
                s, p_hi, p_lo = piece(name)
                if s == 0:
                    pool.wait_ge(gate_rows_t, 1)
                elif s <= 2:
                    pool.wait_ge(basis_used, WIDE)
                else:
                    pool.wait_ge(piece_used, s - 1)
                for t in range(KT):
                    if name[:3] == "rel":
                        l, r = int(name[3]) - 1, int(name[5])
                        pool.wait_ge(rel_back[t], 16 * (l + 1))
                        raw = w_raw[:, t, r, :]
                    else:
                        k = LOADED[name]
                        if t == 0:
                            pool.wait_ge(raw_in[k % 2], 16 * (k // 2 + 1))
                        raw = piece_raw[k % 2][:, t, :]
                    hi, lo = p_hi[:, t, :], p_lo[:, t, :]
                    own_step(pool.tensor_copy(hi, raw))
                    last = pool.tensor_tensor(lo, raw, hi.bitcast(F32), ALU.subtract)
                    if t < KT - 1:
                        own_step(last)
                last.then_inc(split_done, 1)
                pool.wait_ge(split_done, s + 1)
            split("k")
            for t in range(NT):
                pool.wait_ge(xt_hi_done, t + 1)
                pool.tensor_tensor(xt_lo[:, :, t * TP:(t + 1) * TP], xt_tmp[t % 2][:], xt_hi[:, :, t * TP:(t + 1) * TP].bitcast(F32),
                                   ALU.subtract).then_inc(xt_ready, 1)
            pool.wait_ge(count_sum, NT)
            pool.partition_all_reduce(count_max[:], count_acc[:], TP, RMAX).then_inc(count_bound, 1)
            pool.wait_ge(smalls_in, 16 * 6)
            pool.tensor_tensor(bias_row[:, 4, :], bias_row[:, 4, :], bias_row[:, 1, :], ALU.add).then_inc(biases_joined, 1)
            for name in ("q", "v", "Wo", "W1"):
                split(name)
            for t in range(NT):
                power(t + 1, t)
            pool.wait_ge(biases_joined, 1)
            for t in range(NT):
                pool.wait_ge(yn_ready, t + 1)
                pool.tensor_tensor(y[:, t, :], y[:, t, :], bias_row[0:TP, 4, :], ALU.add).then_inc(y_plus_b, 1)
            split("W2")
            split("rel1_0")
            split("root1")
            pool.wait_ge(x_again_in, 16)
            for t in range(NT):
                pool.wait_ge(xm_ready, t + 1)
                pool.tensor_tensor(y[:, t, :], y[:, t, :], x_again[:, t, :], ALU.add).then_inc(xm_plus_x, 1)
            split("rel1_1")
            split("rel2_0")
            split("root2")
            pool.wait_ge(rel_applied, 2)
            pool.iota(rank[:], pattern=[[0, 2 * NT], [-1, E]], base=E, channel_multiplier=0,
                      allow_small_or_imprecise_dtypes=True).then_inc(pool_own, 1)
            n[0] += 1
            split("rel2_1")
            pool.wait_ge(router_in, 16 * 4)
            own_step(pool.tensor_copy(router_hi[:], router_raw[:]))
            pool.tensor_tensor(router_lo[:], router_raw[:], router_hi[:].bitcast(F32), ALU.subtract).then_inc(router_w_ready, 1)

            def split_expert(e):
                pool.wait_ge(ex_in[e % XR], 32 * (e // XR + 1))
                if e < 4:
                    pool.wait_ge(piece_used, len(ORDER))
                else:
                    pool.wait_ge(ex_used, e - 3)
                raw, hi, lo = ex_raw[:, e % XR], ex_hi[:, e % 4], ex_lo[:, e % 4]
                own_step(pool.tensor_copy(hi, raw))
                pool.tensor_tensor(lo, raw, hi.bitcast(F32), ALU.subtract).then_inc(ex_split, 1)
                pool.wait_ge(ex_split, e + 1)
            split_expert(0)
            for t in range(NT):
                power(NT + t + 1, t)
            split_expert(1)
            split_expert(2)
            pool.wait_ge(out_b_in, 16 * 2)
            own_step(pool.tensor_copy(out_b_hi[:], out_bias[:]))
            own_step(pool.tensor_tensor(out_b_lo[:], out_bias[:], out_b_hi[:].bitcast(F32), ALU.subtract))
            pool.wait_ge(route_t_ready, 1)
            own_step(pool.tensor_copy(route_hi[:], route_t[:]))
            pool.tensor_tensor(route_lo[:], route_t[:], route_hi[:].bitcast(F32), ALU.subtract).then_inc(route_split, 1)
            split_expert(3)
            for t in range(NT):
                pool.wait_ge(x1n_ready, t + 1)
                pool.tensor_tensor(x1[:, t, :], x1[:, t, :], bias_row[0:TP, 5, :], ALU.add).then_inc(x1_plus_b, 1)
            for e in range(4, NX):
                split_expert(e)

        @block.vector
        def _(dve):
            n = [0]

            def own_step(ins):
                ins.then_inc(dve_own, 1)
                n[0] += 1
                dve.wait_ge(dve_own, n[0])


            def stats(source, t):
                own_step(dve.bn_stats(bn[:, t, :], source))
                own_step(dve.bn_aggr(stat[:, t, :], bn[:, t, :]))

            def add_eps(t):
                dve.tensor_scalar(veps[:, t:t + 1], stat[:, t, 1:2], 1e-5, None, ALU.add).then_inc(var_ready, 1)

            def normalise(target, source, t):
                return dve.tensor_scalar(target, source, stat[:, t, 0:1], rstd[:, t:t + 1], ALU.subtract, ALU.mult)

            dve.wait_ge(iotas_ready, 4)
            dve.wait_ge(edges_in, 48)
            own_step(dve.tensor_copy(edge_f[:], edge_i[:]))
            own_step(dve.tensor_scalar(key_r[:], edge_f[:, 2, :], 0.0, float(REL_KEY), ALU.not_equal, ALU.mult))
            dve.tensor_tensor(key_r[:], key_r[:], edge_f[:, 1, :], ALU.add).then_inc(key_ready, 1)
            dve.tensor_reduce(mnmx[:, 0:1], edge_f[:, 1, :], AX.X, ALU.min).then_inc(dve_own, 1)
            n[0] += 1
            own_step(dve.tensor_reduce(mnmx[:, 1:2], edge_f[:, 1, :], AX.X, ALU.max))
            own_step(dve.tensor_scalar(mnmx[:, 0:1], mnmx[:, 0:1], -(TP - 1.0), None, ALU.add))
            own_step(dve.tensor_scalar(tile_id[:], tile_id[:], 0.5, -0.25, ALU.mult, ALU.add))
            own_step(dve.tensor_copy(tile_ii[:], tile_id[:]))
            own_step(dve.tensor_copy(tile_id[:], tile_ii[:]))
            own_step(dve.tensor_scalar(in_hi[:], node_lo[:], mnmx[:, 1:2], None, ALU.is_le))
            own_step(dve.tensor_scalar(in_lo[:], node_lo[:], mnmx[:, 0:1], None, ALU.is_ge))
            own_step(dve.tensor_tensor(in_lo[:], in_lo[:], in_hi[:], ALU.mult))
            own_step(dve.tensor_scalar(tile_id[:, 0, :], tile_id[:, 0, :], -1.0, float(ET // 2), ALU.mult, ALU.add))
            own_step(dve.tensor_scalar(tile_id[:, 1, :], tile_id[:, 1, :], 1.0, None, ALU.add))
            own_step(dve.tensor_tensor(bound[:, 0, :], tile_id[:, 0, :], in_lo[:], ALU.mult))
            dve.tensor_tensor(bound[:, 1, :], tile_id[:, 1, :], in_lo[:], ALU.mult).then_inc(bound_ready, 1)
            dve.wait_ge(keys_t, 1)
            own_step(dve.tensor_copy(keys[:].rearrange("p a t -> p (a t)"), ps[0:TE, 6, 0:2 * ET]))
            for j in range(NT):
                dve.tensor_scalar(key_m[:, j, :], keys[:, 1, :], float(-TP * j), None, ALU.add).then_inc(dve_own, 1)
                n[0] += 1
            dve.wait_ge(dve_own, n[0])
            dve.wait_ge(ident_ready, 1)
            dve.tensor_reduce(sel_q[:], ident[:].rearrange("p (b q) -> p q b", b=GB), AX.X, ALU.add).then_inc(sel_q_ready, 1)
            dve.wait_ge(bound_max, 1)
            own_step(dve.tensor_scalar(range_f[:, 1, :], bound_all[0:1, 1, :], 1.0, None, ALU.max))
            own_step(dve.tensor_scalar(range_f[:, 0, :], bound_all[0:1, 0, :], -1.0, float(ET // 2), ALU.mult, ALU.add))
            own_step(dve.tensor_scalar(bound_all[0:1, 0, :], range_f[:, 1, :], -1.0, None, ALU.add))
            own_step(dve.tensor_tensor(range_f[:, 0, :], range_f[:, 0, :], bound_all[0:1, 0, :], ALU.min))
            dve.tensor_copy(range_i[:], range_f[:]).then_inc(range_ready, 1)

            dve.wait_ge(range_ready, 1)
            turn, drained = dve.alloc_register("turn"), dve.alloc_register("drained")
            dve.reg_mov(turn, 0)
            for j in range(NT):
                lo = dve.value_load(range_i[0:1, 0, j:j + 1], min_val=0, max_val=ET // 2 - 1)
                hi = dve.value_load(range_i[0:1, 1, j:j + 1], min_val=1, max_val=ET // 2)
                with dve.Fori(lo, hi) as pair:
                    dve.reg_add(turn, turn, 1)
                    k = dve.snap(turn)
                    dve.wait_ge(pair_used, k)
                    s = k % 2
                    for h in range(2):
                        dve.tensor_scalar(oh_n[:, bass.ds(2 * s + h, 1), :], iota_n[:], keys[:, 0, bass.ds(2 * pair + h, 1)],
                                          None, ALU.is_equal)
                        last = dve.tensor_scalar(oh_m[:, bass.ds(2 * s + h, 1), :], iota_m[:],
                                                 key_m[:, j, bass.ds(2 * pair + h, 1)], None, ALU.is_equal)
                    last.then_inc(one_hot, 1)
                if j == 0:
                    dve.wait_ge(sel_q_ready, 1)
                    dve.wait_ge(att_col_ready, 2)
                    a = sel_att[:].rearrange("p l g r q -> p (l g r) q")
                    dve.tensor_tensor(a, att_col[:].rearrange("p l g r -> p (l g r)").unsqueeze(2).to_broadcast([128, 2 * NG * REL, QI]),
                                      sel_q[:].unsqueeze(1).to_broadcast([128, 2 * NG * REL, QI]), ALU.mult).then_inc(sel_ready, 1)
                    dve.wait_ge(gate_w_hi, 1)
                    gate_ps = ps[:, 5, 64:64 + 2 * KT * REL]
                    dve.tensor_tensor(gate_lo[:].rearrange("p l t r -> p (l t r)"), gate_ps,
                                      gate_hi[:].rearrange("p l t r -> p (l t r)").bitcast(F32), ALU.subtract).then_inc(gate_w_ready, 1)
                dve.reg_add(drained, turn, 2)
                dve.wait_ge(pair_used, dve.snap(drained))
                for r in range(REL):
                    for h in range(2):
                        last = dve.tensor_copy(counts[:, j, r * CW + h * CB:r * CW + (h + 1) * CB], ps[0:TP, COUNT_BANK[r][h], 0:CB])
                last.then_inc(count_ready, 1)
                if j == 2:
                    for c in range(2):
                        dve.wait_ge(wt_hi_done, c + 1)
                        dve.tensor_tensor(wt_lo[:, 2 * c:2 * c + 2, :], ps[:, 5 + c, :].rearrange("p (t m) -> p t m", t=2),
                                          wt_hi[:, 2 * c:2 * c + 2, :].bitcast(F32), ALU.subtract).then_inc(wt_ready, 1)

            def halves(b):
                return ps[:, b:b + 2, 0:HALF]

            def in_halves(ap):
                return ap.rearrange("p (h m) -> p h m", h=2)

            def project(z):
                for c in range(KT):
                    i = KT * z + c
                    dve.wait_ge(kq_hi_done, i + 1)
                    dve.scalar_tensor_tensor(out=in_halves(kq_lo[:, c, :]), in0=halves((0, 5)[c % 2]),
                                             scalar=colv[:, C_BK + i:C_BK + i + 1],
                                             in1=in_halves(kq_hi[:, c, :]).bitcast(F32),
                                             op0=ALU.add, op1=ALU.subtract).then_inc(kq_ready, 1)
                dve.wait_ge(xd_mm, z + 1)
                dve.tensor_copy(xd[:], ps[0:TP, 2, 0:NT]).then_inc(xd_ready, 1)
                for t in range(NT):
                    i = NT * z + t
                    dve.wait_ge(feat_exp, i + 1)
                    if z == 0:
                        dve.tensor_scalar(kp[:, t, :], feat[:, i % 2, :], 1.0 / 16, None, ALU.mult).then_inc(feat_ready, 1)
                    else:
                        dve.tensor_scalar(feat[:, i % 2, :], feat[:, i % 2, :], 1.0 / 16, None, ALU.mult).then_inc(feat_ready, 1)
                        if t == 0:
                            own_step(dve.memset(qpt[:, :, NODES:NPAD], 0.0))
                        dve.wait_ge(qp_t, t + 1)
                        dve.tensor_copy(qpt[:, :, t * TP:(t + 1) * TP],
                                        ps[:, (0, 1)[t % 2], 0:2 * TP].rearrange("p (c m) -> p c m", c=2)).then_inc(qpt_ready, 1)
            project(0)
            dve.wait_ge(count_bound, 1)
            own_step(dve.tensor_reduce(count_max[0:1, 0:1], count_max[0:1, :], AX.X, ALU.max))
            own_step(dve.tensor_scalar(count_max[0:1, 1:2], count_max[0:1, 0:1], float(EXACT), None, ALU.is_gt))
            dve.tensor_copy(many_i[:], count_max[0:1, 1:2]).then_inc(many_ready, 1)
            project(1)
            for t in range(NT):
                dve.wait_ge(v_mm, t + 1)
                dve.wait_ge(smalls_in, 16 * 6)
                dve.tensor_tensor(v[:, t, :], ps[0:TP, (5, 6)[t % 2], :], bias_row[0:TP, 2, :], ALU.add).then_inc(v_ready, 1)
            dve.wait_ge(kv_mm, 1)
            own_step(dve.tensor_copy(ksum[:], ps[:, 2, 8:10]))
            dve.tensor_copy(kv[:], ps[:, 0:2, :]).then_inc(kv_ready, 1)
            dve.wait_ge(d_mm, 1)
            own_step(dve.tensor_scalar(rec[:], ps[0:TP, 2, 16:16 + NT], 1e-8, None, ALU.add))
            dve.reciprocal(rec[:], rec[:]).then_inc(rec_ready, 1)
            for c in range(KT):
                dve.wait_ge(yt_hi_done, c + 1)
                dve.tensor_tensor(in_halves(yt_lo[:, c, :]), halves((5, 0)[c % 2]), in_halves(yt_hi[:, c, :]).bitcast(F32),
                                  ALU.subtract).then_inc(yt_ready, 1)
            dve.wait_ge(rec_ready, 1)

            def normalise_y(t):
                dve.wait_ge(rstd_ready, 2 + t + 1)
                if t >= 2:
                    dve.wait_ge(h2_t, t - 1)
                normalise(yn[:, t % 2, :], y[:, t, :], t).then_inc(yn_ready, 1)
            for t in range(NT):
                dve.wait_ge(wo_mm, t + 1)
                own_step(dve.scalar_tensor_tensor(out=y[:, t, :], in0=ps[0:TP, AGG[t], :], scalar=rec[:, t:t + 1],
                                                  in1=bias_row[0:TP, 3, :], op0=ALU.mult, op1=ALU.add))
                own_step(dve.tensor_tensor(y[:, t, :], y[:, t, :], v[:, t, :], ALU.add))
                stats(y[:, t, :], t)
                add_eps(t)
                if t in (1, 2):
                    normalise_y(t - 1)
            for a in (h2t_hi, h2t_lo):
                own_step(dve.memset(a[:, :, NODES:NPAD].bitcast(F32), 0.0))
            normalise_y(2)
            normalise_y(3)
            for t in range(NT):
                dve.wait_ge(h2_hi_done, t + 1)
                dve.tensor_tensor(h2t_lo[:, :, t * TP:(t + 1) * TP], h2_tmp[t % 2][:], h2t_hi[:, :, t * TP:(t + 1) * TP].bitcast(F32),
                                  ALU.subtract).then_inc(h2t_ready, 1)
                if t == 1:
                    normalise_y(4)
            for c in range(KT):
                dve.wait_ge(act_done, c + 1)
                own_step(dve.tensor_copy(act_hi[:, c, :], act_tmp[:, c % 2, :]))
                dve.tensor_tensor(act_lo[:, c, :], act_tmp[:, c % 2, :], act_hi[:, c, :].bitcast(F32), ALU.subtract).then_inc(act_ready, 1)

            def rest_of_transposed(i, t):
                dve.wait_ge(hT_hi, i + 1)
                dve.tensor_tensor(ht_lo[:, :, t * TP:(t + 1) * TP], ps[:, LB[t % 2], 0:KT * TP].rearrange("p (t m) -> p t m", t=KT),
                                  ht_hi[:, :, t * TP:(t + 1) * TP].bitcast(F32), ALU.subtract).then_inc(hT_ready, 1)
            for t in range(NT):
                dve.wait_ge(w2_mm, t + 1)
                dve.wait_ge(y_plus_b, t + 1)
                dve.tensor_tensor(y[:, t, :], ps[0:TP, AGG[t], :], y[:, t, :], ALU.add).then_inc(xm_ready, 1)
                rest_of_transposed(t, t)

            many = dve.value_load(many_i[0:1, 0:1], min_val=0, max_val=1)

            def messages(l):
                dve.wait_ge(gates_ready, l + 1)
                for r in range(REL):
                    a = 2 * l + r
                    for t in range(NT):
                        i = a * NT + t
                        dve.wait_ge(u_hi_done, i + 1)
                        dve.scalar_tensor_tensor(out=u_lo[l][:, t, :], in0=ps[0:TP, LB[i % 2], :], scalar=gates[:, t, r:r + 1],
                                                 in1=u_hi[l][:, t, :].bitcast(F32), op0=ALU.mult, op1=ALU.subtract).then_inc(u_ready, 1)
                    with dve.If(many):
                        dve.wait_ge(cf_ready, (a + 1) * NT)
                        last = dve.tensor_tensor(cf[:], counts[:, :, r * CW:(r + 1) * CW], cf[:].bitcast(F32), ALU.subtract)
                        last.then_inc(rest_ready, 1)
                        dve.wait_ge(rest_used, a + 1)
                        dve.tensor_copy(cf[:], counts[:, :, r * CW:(r + 1) * CW]).then_inc(rest_ready, 1)

            messages(0)
            for t in range(NT):
                dve.wait_ge(agg_done, t + 1)
                if t >= 2:
                    dve.wait_ge(hT_t, NT + t - 1)
                dve.tensor_tensor(row_tmp[:, t % 2, :], ps[0:TP, AGG[t], :], bias_row[0:TP, 0, :], ALU.add).then_inc(h_added, 1)
                if t >= 2:
                    rest_of_transposed(NT + t - 2, t - 2)
            for t in (NT - 2, NT - 1):
                rest_of_transposed(NT + t, t)

            messages(1)

            def x1_of(t):
                dve.wait_ge(agg_done, NT + t + 1)
                dve.wait_ge(xm_plus_x, t + 1)
                if t == 0:
                    dve.wait_ge(split_done, PIECE["rel2_1"] + 1)
                own_step(dve.tensor_tensor(x1[:, t, :], ps[0:TP, AGG[t], :], y[:, t, :], ALU.add))
                stats(x1[:, t, :], t)
                add_eps(t)

            def x1_normalised(t):
                dve.wait_ge(rstd_ready, 2 + NT + t + 1)
                if t >= 2:
                    dve.wait_ge(x1_t, t - 1)
                normalise(x1n[:, t % 2, :], x1[:, t, :], t).then_inc(x1n_ready, 1)

            def x1_rest(t):
                dve.wait_ge(x1_hi_done, t + 1)
                dve.tensor_tensor(x1t_lo[:, :, t * TP:(t + 1) * TP], ps[:, UB[t % 3], 0:KT * TP].rearrange("p (t m) -> p t m", t=KT),
                                  x1t_hi[:, :, t * TP:(t + 1) * TP].bitcast(F32), ALU.subtract).then_inc(x1t_ready, 1)
            for t in range(NT + 2):
                if t < NT:
                    x1_of(t)
                if 1 <= t <= NT:
                    x1_normalised(t - 1)
                if t >= 2:
                    if t == 2:
                        for a in (x1t_hi, x1t_lo):
                            own_step(dve.memset(a[:, :, NODES:NPAD].bitcast(F32), 0.0))
                    x1_rest(t - 2)
            dve.wait_ge(logit_mm, 1)
            dve.wait_ge(router_in, 16 * 4)
            for t in range(NT):
                last = dve.tensor_tensor(logit[:, t].rearrange("p b e -> p (b e)"), ps[0:TP, 4, t * 2 * E:(t + 1) * 2 * E],
                                         router_b[:], ALU.add)
            own_step(last)
            lg = logit[:].rearrange("p t b e -> p (t b) e")

            def over(ap):
                return ap.rearrange("p t b -> p (t b)").unsqueeze(2).to_broadcast([TP, 2 * NT, E])

            def flat(a):
                return a[:].rearrange("p t b e -> p (t b) e")
            own_step(dve.tensor_reduce(lmax[:].rearrange("p t b -> p (t b)"), lg, AX.X, ALU.max))
            dve.tensor_tensor(flat(shifted), lg, over(lmax[:]), ALU.subtract).then_inc(shift_ready, 1)
            own_step(dve.tensor_tensor(flat(score), lg, over(lmax[:]), ALU.is_equal))
            own_step(dve.tensor_tensor(flat(score), flat(score), flat(rank), ALU.mult))
            own_step(dve.tensor_reduce(best[:].rearrange("p t b -> p (t b)"), flat(score), AX.X, ALU.max))
            own_step(dve.tensor_tensor(flat(route), flat(score), over(best[:]), ALU.is_equal))
            dve.wait_ge(expo_ready, 1)
            own_step(dve.tensor_reduce(denom[:].rearrange("p t b -> p (t b)"), flat(expo), AX.X, ALU.add))
            own_step(dve.reciprocal(gate_p[:], denom[:]))
            dve.tensor_tensor(flat(route), flat(route), over(gate_p[:]), ALU.mult).then_inc(route_ready, 1)
            own_step(dve.memset(route_t[:, NODES:NPAD], 0.0))
            dve.wait_ge(route_tr, 1)
            own_step(dve.tensor_copy(route_t[:, 0:4 * TP], ps[0:2 * E, 4, 0:4 * TP]))
            dve.tensor_copy(route_t[:, 4 * TP:NODES], ps[0:2 * E, 7, 0:TP]).then_inc(route_t_ready, 1)
            for e in range(NX):
                for h in range(2):
                    i = 2 * e + h
                    dve.wait_ge(hid_ready, i + 1)
                    source = hid[:, i % 4, :]
                    if e:
                        if h == 0:
                            dve.wait_ge(route_back, 16 * 2 * E)
                        own_step(dve.tensor_tensor(gated[:, i % 4, :], source, route_all[:, e - 1, h * HALF:(h + 1) * HALF], ALU.mult))
                        source = gated[:, i % 4, :]
                    if e >= 2 and h == 0:
                        dve.wait_ge(ex_used, e - 1)
                    hi, lo = (a[:, e % 2, h * HALF:(h + 1) * HALF] for a in (hg_hi, hg_lo))
                    own_step(dve.tensor_copy(hi, source))
                    dve.tensor_tensor(lo, source, hi.bitcast(F32), ALU.subtract).then_inc(hg_ready, 1)
            for t in range(NT):
                dve.wait_ge(ffn_mm, t + 1)
                dve.wait_ge(x1_plus_b, t + 1)
                if t >= 2:
                    dve.wait_ge(stored[t % 2], 16 * (t // 2))
                dve.tensor_tensor(final[:, t % 2, :], ps[0:TP, AGG[t], :], x1[:, t, :], ALU.add).then_inc(final_ready, 1)

        @block.scalar
        def _(act):
            def halves(b):
                return ps[:, b:b + 2, 0:HALF]

            def in_halves(ap):
                return ap.rearrange("p (h m) -> p h m", h=2)

            def evac_relation(ch):
                act.wait_ge(rel_sum, ch + 1)
                if ch >= 2:
                    act.wait_ge(rel_out[ch % 2], 16 * (ch // 2))
                act.activation(stag[:, ch % 2, :], ps[:, rel_bank(ch), :], ACT.Copy).then_inc(rel_evac, 1)

            act.wait_ge(rows_in, 16 * 13)
            for l in range(2):
                last = act.activation(att_rep[:, l, :].rearrange("r (b q) -> r b q", q=QI),
                                      att_rows[:, l, :].unsqueeze(2).to_broadcast([REL, BASES, QI]), ACT.Copy)
            last.then_inc(att_ready, 1)
            act.wait_ge(gate_rows_t, 1)
            act.wait_ge(consts_ready, 5)
            n_all = (BASES - (NG - 1) * GB) * QI
            act.activation(att_col[0:n_all].rearrange("p l g r -> p (l g r)"), ps[0:n_all, 5, 96:96 + 2 * NG * REL],
                           ACT.Copy).then_inc(att_col_ready, 1)
            act.activation(att_col[n_all:128, :, 0:NG - 1, :].rearrange("p l g r -> p l (g r)"),
                           ps[n_all:128, 5, 96:96 + 2 * NG * REL].rearrange("p (l g) -> p l g", l=2)[:, :, 0:(NG - 1) * REL],
                           ACT.Copy).then_inc(att_col_ready, 1)
            act.activation(colv[:], ps[:, 5, 0:45], ACT.Copy).then_inc(cols_ready, 1)
            act.activation(gate_hi[:].rearrange("p l t r -> p (l t r)"), ps[:, 5, 64:64 + 2 * KT * REL], ACT.Copy).then_inc(gate_w_hi, 1)
            act.wait_ge(x_in, 16)
            for k, (source, target, ready) in enumerate(((xa, xn, xn_ready), (xn, xn2, xn2_ready))):
                if k:
                    act.wait_ge(xn_ready, NT)
                for t in range(NT):
                    last = act.activation(xn2[:, t, :], source[:, t, :], ACT.Copy, accum_out=mean_acc[:, k, t:t + 1])
                last.then_inc(mean_sum, 1)
                act.wait_ge(minus_mean_ready, k + 1)
                for t in range(NT):
                    last = act.activation(xn2[:, t, :], source[:, t, :], ACT.Square, bias=minus_mean[:, k, t:t + 1],
                                          accum_out=square_acc[:, k, t:t + 1])
                last.then_inc(square_sum, 1)
                act.wait_ge(rstd_ready, k + 1)
                for t in range(NT):
                    act.activation(target[:, t, :], source[:, t, :], ACT.Identity, bias=shift[:, k, t:t + 1],
                                   scale=rstd_x[:, k, t:t + 1]).then_inc(ready, 1)

            def scaled(target, bank, column_g, column_b):
                for c in range(KT):
                    last = act.activation(target[:, c, :], ps[:, bank, c * TP:(c + 1) * TP], ACT.Identity,
                                          bias=colv[:, column_b + c:column_b + c + 1], scale=colv[:, column_g + c:column_g + c + 1])
                return last

            def count_rows(j):
                act.wait_ge(count_ready, j + 1)
                if j:
                    act.wait_ge(count_sum, j)
                act.activation(counts_read[:], counts[:, j, :], ACT.Copy, accum_out=count_acc[:, j:j + 1]).then_inc(count_sum, 1)

            def scale_xt(t):
                act.wait_ge(xt_t, t + 1)
                if t >= 2:
                    act.wait_ge(xt_ready, t - 1)
                if t == 0:
                    act.wait_ge(cols_ready, 1)
                scaled(xt_tmp[t % 2], 5 + t % 2, C_G1, C_BE1).then_inc(xt_scaled, 1)
                act.wait_ge(xt_scaled, t + 1)
                act.activation(xt_hi[:, :, t * TP:(t + 1) * TP], xt_tmp[t % 2][:], ACT.Copy).then_inc(xt_hi_done, 1)
            count_rows(0)
            evac_relation(0)
            for c in range(2):
                act.wait_ge(wt_t, c + 1)
                act.activation(wt_hi[:, 2 * c:2 * c + 2, :], ps[:, 5 + c, :].rearrange("p (t m) -> p t m", t=2),
                               ACT.Copy).then_inc(wt_hi_done, 1)
            evac_relation(1)
            count_rows(1)
            evac_relation(2)
            count_rows(2)
            for t in range(3):
                scale_xt(t)
            count_rows(3)
            evac_relation(3)
            for t in range(3, NT):
                scale_xt(t)
            count_rows(4)
            evac_relation(4)

            act.wait_ge(count_sum, NT)

            def project(z):
                for c in range(KT):
                    i = KT * z + c
                    bias = colv[:, C_BK + i:C_BK + i + 1]
                    act.wait_ge(kq_mm, i + 1)
                    if i:
                        act.wait_ge(sq_used, i)
                    act.activation(in_halves(square[:]), halves((0, 5)[c % 2]), ACT.Square, bias=bias).then_inc(sq_ready, 1)
                    if z and c == 0:
                        act.wait_ge(feat_mm, NT)
                    act.activation(in_halves(kq_hi[:, c, :]), halves((0, 5)[c % 2]), ACT.Identity, bias=bias).then_inc(kq_hi_done, 1)
                evac_relation(5 + z)
                act.wait_ge(xd_ready, z + 1)
                for t in range(NT):
                    i = NT * z + t
                    act.wait_ge(feat_mm, i + 1)
                    if i >= 2:
                        if i >= NT + 2:
                            act.wait_ge(qp_t, i - NT - 1)
                        else:
                            act.wait_ge(feat_ready, i - 1)
                    act.activation(feat[:, i % 2, :], ps[0:TP, (5, 6)[t % 2], 0:M], ACT.Exp, bias=xd[:, t:t + 1]).then_inc(feat_exp, 1)
            project(0)
            project(1)
            evac_relation(7)
            evac_relation(8)
            evac_relation(9)
            for c in range(KT):
                act.wait_ge(yt_mm, c + 1)
                act.activation(in_halves(yt_hi[:, c, :]), halves((5, 0)[c % 2]), ACT.Copy).then_inc(yt_hi_done, 1)
            evac_relation(10)
            evac_relation(11)
            for t in range(NT):
                act.wait_ge(h2_t, t + 1)
                if t >= 2:
                    act.wait_ge(h2t_ready, t - 1)
                if t == 0:
                    act.wait_ge(wo_mm, NT)
                scaled(h2_tmp[t % 2], (7, 2)[t % 2], C_G2, C_BE2).then_inc(h2_scaled, 1)
                act.wait_ge(h2_scaled, t + 1)
                act.activation(h2t_hi[:, :, t * TP:(t + 1) * TP], h2_tmp[t % 2][:], ACT.Copy).then_inc(h2_hi_done, 1)
            evac_relation(12)
            for c in range(KT):
                act.wait_ge(act_mm, c + 1)
                if c >= 2:
                    act.wait_ge(act_ready, c - 1)
                act.activation(in_halves(act_tmp[:, c % 2, :]), halves((0, 5)[c % 2]), ACT.Gelu,
                               bias=colv[:, C_B1 + c:C_B1 + c + 1]).then_inc(act_done, 1)
            evac_relation(13)

            def split_transposed(i, t):
                act.wait_ge(hT_t, i + 1)
                act.activation(ht_hi[:, :, t * TP:(t + 1) * TP], ps[:, LB[t % 2], 0:KT * TP].rearrange("p (t m) -> p t m", t=KT),
                               ACT.Copy).then_inc(hT_hi, 1)
            for t in range(NT):
                if t == NT - 1:
                    evac_relation(14)
                split_transposed(t, t)

            def messages(l):
                act.wait_ge(gate_mm, l + 1)
                act.activation(gates[:].rearrange("p t r -> p (t r)"), ps[0:TP, 7, 0:NT * REL], ACT.Sigmoid).then_inc(gates_ready, 1)
                act.wait_ge(gates_ready, l + 1)
                for r in range(REL):
                    a = 2 * l + r
                    for t in range(NT):
                        if t == 0 and a == 0:
                            act.wait_ge(w2_mm, NT)
                            act.wait_ge(count_ready, NT)
                        elif t == 0:
                            act.wait_ge(rel_applied, a)
                        i = a * NT + t
                        act.activation(cf[:, t, :], counts[:, t, r * CW:(r + 1) * CW], ACT.Copy).then_inc(cf_ready, 1)
                        act.wait_ge(u_mm, i + 1)
                        act.activation(u_hi[l][:, t, :], ps[0:TP, LB[i % 2], :], ACT.Copy, scale=gates[:, t, r:r + 1]).then_inc(u_hi_done, 1)
                    if a == 0:
                        evac_relation(15)

            messages(0)
            for t in range(NT):
                act.wait_ge(h_added, t + 1)
                act.activation(row_tmp[:, t % 2, :], row_tmp[:, t % 2, :], ACT.Relu).then_inc(h_relu, 1)
                if t >= 2:
                    split_transposed(NT + t - 2, t - 2)
            for t in (NT - 2, NT - 1):
                split_transposed(NT + t, t)
            messages(1)
            for t in range(NT):
                act.wait_ge(x1_t, t + 1)
                if t == 0:
                    act.wait_ge(u_mm, 4 * NT)
                act.activation(x1t_hi[:, :, t * TP:(t + 1) * TP], ps[:, UB[t % 3], 0:KT * TP].rearrange("p (t m) -> p t m", t=KT),
                               ACT.Copy).then_inc(x1_hi_done, 1)
            act.wait_ge(shift_ready, 1)
            act.activation(expo[:].rearrange("p t b e -> p (t b e)"), shifted[:].rearrange("p t b e -> p (t b e)"),
                           ACT.Exp).then_inc(expo_ready, 1)
            for e in range(NX):
                for h in range(2):
                    i = 2 * e + h
                    act.wait_ge(hid_mm, i + 1)
                    if i >= 4:
                        act.wait_ge(hg_ready, i - 3)
                    act.activation(hid[:, i % 4, :], ps[:, UB[i % 3], 0:HALF], ACT.Gelu,
                                   bias=colv[:, C_EXP + e:C_EXP + e + 1]).then_inc(hid_ready, 1)

        @block.tensor
        def _(pe):
            def mm3(target, a_hi, a_lo, b_hi, b_lo, first, last, skip=False):
                pe.matmul(target, a_hi, b_hi, start=first, stop=False, skip_group_check=skip)
                pe.matmul(target, a_hi, b_lo, start=False, stop=False, skip_group_check=skip)
                return pe.matmul(target, a_lo, b_hi, start=False, stop=last, skip_group_check=skip)

            part = [0]

            def relation_parts(count):
                for i in range(part[0], part[0] + count):
                    ch, g = divmod(i, NG)
                    nb = min(GB, BASES - g * GB)
                    slot, turn_ = basis_turn(i)
                    pe.wait_ge(basis_in[slot], 16 * turn_)
                    if g == 0 and ch >= 2:
                        pe.wait_ge(rel_evac, ch - 1 if ch < 2 * CHUNKS - 1 else ch)
                    for c in range(4):
                        last = pe.matmul(ps[32 * c:32 * c + 32, rel_bank(ch), :],
                                         sel_att[0:nb * QI, ch // CHUNKS, g].rearrange("p r q -> p (r q)"),
                                         ring[slot][0:nb * QI, c * D:(c + 1) * D], start=(g == 0), stop=(g == NG - 1))
                    last.then_inc(basis_used, 1)
                    if g == NG - 1:
                        pe.wait_ge(basis_used, i + 1)
                        pe.sem_inc(rel_sum, 1)
                part[0] += count

            pe.wait_ge(ident_ready, 1)
            pe.wait_ge(key_ready, 1)
            pe.transpose(ps[0:TE, 6, 0:ET], edge_f[:, 0, :], ident[0:ET, 0:ET])
            pe.transpose(ps[0:TE, 6, ET:2 * ET], key_r[:], ident[0:ET, 0:ET]).then_inc(keys_t, 1)
            pe.wait_ge(rows_in, 16 * 13)
            pe.wait_ge(att_ready, 1)
            pe.transpose(ps[:, 5, 0:45], row_vec[:], ident[0:45, 0:45])
            for l in range(2):
                for t in range(KT):
                    o = 64 + (l * KT + t) * REL
                    pe.transpose(ps[:, 5, o:o + REL], gate_rows[:, l, :].rearrange("r (i t) -> r t i", t=KT)[:, t],
                                 ident[0:REL, 0:REL])
                for g in range(NG):
                    nb = min(GB, BASES - g * GB)
                    o = 96 + (l * NG + g) * REL
                    last = pe.transpose(ps[0:nb * QI, 5, o:o + REL],
                                        att_rep[:, l, g * GB * QI:(g * GB + nb) * QI],
                                        ident[0:REL, 0:REL])
            last.then_inc(gate_rows_t, 1)

            def turn_xt(t):
                pe.wait_ge(xn2_ready, t + 1)
                if t >= 2:
                    pe.wait_ge(xt_scaled, t - 1)
                else:
                    pe.wait_ge(wt_ready, t + 1)
                for c in range(KT):
                    last = pe.transpose(ps[:, 5 + t % 2, c * TP:(c + 1) * TP], xn2[:, t, c * 128:(c + 1) * 128], ident[0:TP, 0:TP])
                last.then_inc(xt_t, 1)

            pe.wait_ge(range_ready, 1)
            pe.wait_ge(consts_ready, 5)
            turn = pe.alloc_register("turn")
            pe.reg_mov(turn, 0)
            pe.sem_inc(pair_used, 2)
            for j in range(NT):
                lo = pe.value_load(range_i[0:1, 0, j:j + 1], min_val=0, max_val=ET // 2 - 1)
                hi = pe.value_load(range_i[0:1, 1, j:j + 1], min_val=1, max_val=ET // 2)
                if j:
                    pe.wait_ge(count_ready, j)
                for b in COUNT_BANK[0] + COUNT_BANK[1]:
                    pe.matmul(ps[0:TP, b, 0:2], zeros[:], iota_n[:, 0:2], start=True, stop=False, skip_group_check=True)
                with pe.Fori(lo, hi) as _pair:
                    pe.reg_add(turn, turn, 1)
                    k = pe.snap(turn)
                    pe.wait_ge(one_hot, k)
                    s = k % 2
                    for u in range(2):
                        for r in range(REL):
                            for h in range(2):
                                last = pe.matmul(ps[0:TP, COUNT_BANK[r][h], 0:CB],
                                                 oh_m[:, bass.ds(2 * s + u, 1), r * TE:(r + 1) * TE],
                                                 oh_n[:, bass.ds(2 * s + u, 1), CB * h:CB * (h + 1)],
                                                 start=False, stop=False, skip_group_check=True)
                    last.then_inc(pair_used, 1)
                if j == 0:
                    pe.wait_ge(sel_ready, 1)
                if j == 1:
                    pe.wait_ge(w_in, 16)
                    pe.wait_ge(gate_w_ready, 1)
                    pe.wait_ge(cols_ready, 1)
                    for c in range(2):
                        for t in range(2):
                            for m in range(2):
                                o = t * M + m * 128
                                last = pe.transpose(ps[:, 5 + c, o:o + 128], w_nat[:, m, (2 * c + t) * 128:(2 * c + t + 1) * 128], ident[:])
                        last.then_inc(wt_t, 1)
                if j == 3:
                    turn_xt(2)
                relation_parts(NG)
                if j == 2:
                    turn_xt(0)
                    turn_xt(1)
                if j == 3:
                    turn_xt(3)
                if j == 4:
                    turn_xt(4)

            def project(z):
                s, p_hi, p_lo = piece("kq"[z])
                pe.wait_ge(split_done, s + 1)
                pe.wait_ge(xt_ready, NT)
                pe.wait_ge(pads_ready, 2)
                for c in range(KT):
                    i = KT * z + c
                    b = (0, 5)[c % 2]
                    if c >= 2:
                        pe.wait_ge(kq_ready, i - 1)
                    elif z == 0:
                        pe.wait_ge(count_ready, NT)
                        pe.wait_ge(wt_ready, 2)
                        pe.wait_ge(xt_scaled, NT)
                    else:
                        pe.wait_ge(feat_exp, NT)
                        pe.wait_ge(kq_ready, KT)
                    for k in range(KT):
                        for h in range(2):
                            last = mm3(ps[:, b + h, 0:HALF], p_hi[:, k, c * 128:(c + 1) * 128],
                                       p_lo[:, k, c * 128:(c + 1) * 128], xt_hi[:, k, h * HALF:(h + 1) * HALF],
                                       xt_lo[:, k, h * HALF:(h + 1) * HALF], k == 0, k == KT - 1)
                    last.then_inc(kq_mm, 1)
                    relation_parts(1)
                    if c:
                        half_norm(z, c - 1)
                half_norm(z, KT - 1)
                pe.wait_ge(kq_mm, KT * (z + 1))
                pe.sem_inc(piece_used, 1)
                pe.wait_ge(kq_ready, KT * (z + 1))
                for t in range(NT):
                    i = NT * z + t
                    if t >= 2:
                        pe.wait_ge(feat_exp, i - 1)
                    for k in range(KT):
                        last = mm3(ps[0:TP, (5, 6)[t % 2], 0:M], kq_hi[:, k, t * TP:(t + 1) * TP], kq_lo[:, k, t * TP:(t + 1) * TP],
                                   wt_hi[:, k, :], wt_lo[:, k, :], k == 0, k == KT - 1)
                    last.then_inc(feat_mm, 1)
                    if t in ((1, 3), (0, 2, 4))[z]:
                        relation_parts(1)
                    if z and t:
                        turn_features(t - 1)
                if z:
                    turn_features(NT - 1)

            def half_norm(z, c):
                pe.wait_ge(sq_ready, KT * z + c + 1)
                if z and c == 0:
                    pe.wait_ge(xd_ready, 1)
                for t in range(NT):
                    last = pe.matmul(ps[0:TP, 2, t:t + 1], square[:, t * TP:(t + 1) * TP], neg_half[:], start=(c == 0 and t == 0),
                                     stop=(c == KT - 1 and t == NT - 1), skip_group_check=True)
                last.then_inc(sq_used, 1)
                if c == KT - 1:
                    pe.wait_ge(sq_used, KT * (z + 1))
                    pe.sem_inc(xd_mm, 1)

            def turn_features(t):
                pe.wait_ge(feat_ready, NT + t + 1)
                if t >= 2:
                    pe.wait_ge(qpt_ready, t - 1)
                for m in range(2):
                    last = pe.transpose(ps[:, (0, 1)[t % 2], m * TP:(m + 1) * TP], feat[:, (NT + t) % 2, m * 128:(m + 1) * 128],
                                        ident[0:TP, 0:TP])
                last.then_inc(qp_t, 1)

            project(0)
            project(1)
            s, p_hi, p_lo = piece("v")
            pe.wait_ge(split_done, s + 1)
            pe.wait_ge(feat_exp, 2 * NT)
            for t in range(NT):
                if t >= 2:
                    pe.wait_ge(v_ready, t - 1)
                for k in range(KT):
                    last = mm3(ps[0:TP, (5, 6)[t % 2], :], xt_hi[:, k, t * TP:(t + 1) * TP], xt_lo[:, k, t * TP:(t + 1) * TP],
                               p_hi[:, k, :], p_lo[:, k, :], k == 0, k == KT - 1)
                last.then_inc(v_mm, 1)
                if t < 4:
                    relation_parts(1)
            pe.wait_ge(v_mm, NT)
            pe.sem_inc(piece_used, 1)
            pe.wait_ge(v_ready, NT)
            pe.wait_ge(qpt_ready, NT)
            pe.wait_ge(feat_ready, NT)
            pe.wait_ge(xd_ready, 2)
            for m in range(2):
                for t in range(NT):
                    pe.matmul(ps[:, m, :], kp[:, t, m * 128:(m + 1) * 128], v[:, t, :], start=(t == 0), stop=(t == NT - 1))
                for t in range(NT):
                    last = pe.matmul(ps[:, 2, 8 + m:9 + m], kp[:, t, m * 128:(m + 1) * 128], ones[0:TP, :],
                                     start=(m == 0 and t == 0), stop=(m == 1 and t == NT - 1), skip_group_check=True)
                if m == 1:
                    last.then_inc(kv_mm, 1)
                relation_parts((1, 2)[m])
            pe.wait_ge(kv_ready, 1)
            for t in range(NT):
                for m in range(2):
                    last = pe.matmul(ps[0:TP, 2, 16 + t:17 + t], qpt[:, m, t * TP:(t + 1) * TP], ksum[:, m:m + 1],
                                     start=(t == 0 and m == 0), stop=(t == NT - 1 and m == 1), skip_group_check=True)
            last.then_inc(d_mm, 1)
            for c in range(KT):
                b = (5, 0)[c % 2]
                if c >= 2:
                    pe.wait_ge(yt_ready, c - 1)
                for m in range(2):
                    for h in range(2):
                        last = pe.matmul(ps[:, b + h, 0:HALF], kv[:, m, c * 128:(c + 1) * 128], qpt[:, m, h * HALF:(h + 1) * HALF],
                                         start=(m == 0), stop=(m == 1))
                last.then_inc(yt_mm, 1)
                if c:
                    relation_parts(1)
            s, p_hi, p_lo = piece("Wo")
            pe.wait_ge(split_done, s + 1)
            pe.wait_ge(yt_ready, KT)
            pe.wait_ge(rec_ready, 1)
            for t in range(NT):
                for k in range(KT):
                    last = mm3(ps[0:TP, AGG[t], :], yt_hi[:, k, t * TP:(t + 1) * TP], yt_lo[:, k, t * TP:(t + 1) * TP],
                               p_hi[:, k, :], p_lo[:, k, :], k == 0, k == KT - 1)
                last.then_inc(wo_mm, 1)
                if t:
                    relation_parts(1)
            pe.wait_ge(wo_mm, NT)
            pe.sem_inc(piece_used, 1)
            relation_parts(1)
            for t in range(NT):
                pe.wait_ge(yn_ready, t + 1)
                if t == 0:
                    pe.wait_ge(count_ready, NT)
                if t >= 2:
                    pe.wait_ge(h2_scaled, t - 1)
                for c in range(KT):
                    last = pe.transpose(ps[:, (7, 2)[t % 2], c * TP:(c + 1) * TP], yn[:, t % 2, c * 128:(c + 1) * 128], ident[0:TP, 0:TP])
                last.then_inc(h2_t, 1)
                if t:
                    relation_parts(1)
            s, p_hi, p_lo = piece("W1")
            pe.wait_ge(split_done, s + 1)
            pe.wait_ge(h2t_ready, NT)
            for c in range(KT):
                b = (0, 5)[c % 2]
                if c >= 2:
                    pe.wait_ge(act_done, c - 1)
                for k in range(KT):
                    for h in range(2):
                        last = mm3(ps[:, b + h, 0:HALF], p_hi[:, k, c * 128:(c + 1) * 128],
                                   p_lo[:, k, c * 128:(c + 1) * 128], h2t_hi[:, k, h * HALF:(h + 1) * HALF],
                                   h2t_lo[:, k, h * HALF:(h + 1) * HALF], k == 0, k == KT - 1)
                last.then_inc(act_mm, 1)
                relation_parts(1)
            pe.wait_ge(act_mm, KT)
            pe.sem_inc(piece_used, 1)

            def turn_layer_input(t, rows):
                for c in range(KT):
                    last = pe.transpose(ps[:, LB[t % 2], c * TP:(c + 1) * TP], rows.rearrange("p (i t) -> p t i", t=KT)[:, c],
                                        ident[0:TP, 0:TP])
                last.then_inc(hT_t, 1)

            def turn_xn(t):
                if t >= 2:
                    pe.wait_ge(hT_ready, t - 1)
                elif t == 0:
                    pe.wait_ge(xn_ready, NT)
                    pe.wait_ge(h2_scaled, NT)
                else:
                    pe.wait_ge(rel_evac, 2 * CHUNKS - 2)
                turn_layer_input(t, xn[:, t, :])
            turn_xn(0)
            s, p_hi, p_lo = piece("W2")
            pe.wait_ge(split_done, s + 1)
            pe.wait_ge(act_ready, KT)
            for t in range(NT):
                for k in range(KT):
                    last = mm3(ps[0:TP, AGG[t], :], act_hi[:, k, t * TP:(t + 1) * TP], act_lo[:, k, t * TP:(t + 1) * TP],
                               p_hi[:, k, :], p_lo[:, k, :], k == 0, k == KT - 1)
                last.then_inc(w2_mm, 1)
                if t + 1 < NT:
                    turn_xn(t + 1)
                relation_parts(1)
            pe.wait_ge(w2_mm, NT)
            pe.sem_inc(piece_used, 1)
            many = pe.alloc_register("many")

            def layer(l):
                pe.wait_ge(hT_ready, NT * (l + 1))
                for t in range(NT):
                    for c in range(KT):
                        last = mm3(ps[0:TP, 7, t * REL:(t + 1) * REL], ht_hi[:, c, t * TP:(t + 1) * TP], ht_lo[:, c, t * TP:(t + 1) * TP],
                                   gate_hi[:, l, c, :], gate_lo[:, l, c, :], t == 0 and c == 0, t == NT - 1 and c == KT - 1, skip=True)
                last.then_inc(gate_mm, 1)
                if l == 0:
                    relation_parts(PARTS - part[0])
                    pe.wait_ge(rel_evac, 2 * CHUNKS - 2)
                pe.wait_ge(gates_ready, l + 1)
                for r in range(REL):
                    a = 2 * l + r
                    s, p_hi, p_lo = piece(f"rel{l + 1}_{r}")
                    pe.wait_ge(split_done, s + 1)
                    for t in range(NT):
                        i = a * NT + t
                        if i >= 2:
                            pe.wait_ge(u_ready, i - 1)
                        for c in range(KT):
                            last = mm3(ps[0:TP, LB[i % 2], :], ht_hi[:, c, t * TP:(t + 1) * TP], ht_lo[:, c, t * TP:(t + 1) * TP],
                                       p_hi[:, c, :], p_lo[:, c, :], c == 0, c == KT - 1)
                        last.then_inc(u_mm, 1)
                    pe.wait_ge(u_mm, (a + 1) * NT)
                    pe.sem_inc(piece_used, 1)
                    if r == 0:
                        s, p_hi, p_lo = piece(f"root{l + 1}")
                        pe.wait_ge(split_done, s + 1)
                        pe.wait_ge((xm_ready, h_added)[l], NT)
                        for t in range(NT):
                            for c in range(KT):
                                last = mm3(ps[0:TP, AGG[t], :], ht_hi[:, c, t * TP:(t + 1) * TP], ht_lo[:, c, t * TP:(t + 1) * TP],
                                           p_hi[:, c, :], p_lo[:, c, :], c == 0, False)
                        last.then_inc(piece_used, 1)
                    pe.wait_ge(cf_ready, (a + 1) * NT)
                    pe.wait_ge(u_ready, (a + 1) * NT)

                    def apply_counts(t, close):
                        for m in range(NT):
                            for u in (u_hi[l], u_lo[l]):
                                last = pe.matmul(ps[0:TP, AGG[t], :], cf[:, m, t * TP:(t + 1) * TP], u[:, m, :], start=False,
                                                 stop=close and m == NT - 1 and u is u_lo[l])
                        return last
                    if a == 0:
                        pe.wait_ge(many_ready, 1)
                        pe.reg_mov(many, pe.value_load(many_i[0:1, 0:1], min_val=0, max_val=1))
                    with pe.If(many):
                        pe.wait_ge(rest_ready, 2 * a + 1)
                        for t in range(NT):
                            last = apply_counts(t, False)
                        last.then_inc(rest_used, 1)
                        pe.wait_ge(rest_ready, 2 * a + 2)
                    for t in range(NT):
                        last = apply_counts(t, r == REL - 1)
                        if r == REL - 1:
                            last.then_inc(agg_done, 1)
                            if l == 0 and t >= 2:
                                turn_h(t - 2)
                    if r == 0:
                        last.then_inc(rel_applied, 1)
                    else:
                        pe.wait_ge(agg_done, (l + 1) * NT)
                        pe.sem_inc(rel_applied, 1)

            def turn_h(t):
                pe.wait_ge(h_relu, t + 1)
                if t >= 2:
                    pe.wait_ge(hT_ready, NT + t - 1)
                turn_layer_input(t, row_tmp[:, t % 2, :])

            layer(0)
            turn_h(NT - 2)
            turn_h(NT - 1)
            layer(1)
            pe.wait_ge(u_ready, 4 * NT)
            for t in range(NT):
                pe.wait_ge(x1n_ready, t + 1)
                if t >= 3:
                    pe.wait_ge(x1t_ready, t - 2)
                for c in range(KT):
                    last = pe.transpose(ps[:, UB[t % 3], c * TP:(c + 1) * TP], x1n[:, t % 2, :].rearrange("p (f t) -> p t f", t=KT)[:, c],
                                        ident[0:TP, 0:TP])
                last.then_inc(x1_t, 1)
            pe.wait_ge(router_w_ready, 1)
            pe.wait_ge(x1t_ready, NT)
            for t in range(NT):
                for c in range(KT):
                    last = mm3(ps[0:TP, 4, t * 2 * E:(t + 1) * 2 * E], x1t_hi[:, c, t * TP:(t + 1) * TP], x1t_lo[:, c, t * TP:(t + 1) * TP],
                               router_hi[:, c, :], router_lo[:, c, :], t == 0 and c == 0, t == NT - 1 and c == KT - 1, skip=True)
            last.then_inc(logit_mm, 1)
            pe.wait_ge(route_ready, 1)
            for t in range(4):
                pe.transpose(ps[0:2 * E, 4, t * TP:(t + 1) * TP], route[:, t].rearrange("p b e -> p (b e)"), ident[0:TP, 0:TP])
            pe.transpose(ps[0:2 * E, 7, 0:TP], route[:, 4].rearrange("p b e -> p (b e)"), ident[0:TP, 0:TP]).then_inc(route_tr, 1)

            def hidden(e):
                pe.wait_ge(ex_split, e + 1)
                if e == 0:
                    pe.wait_ge(route_t_ready, 1)
                for h in range(2):
                    i = 2 * e + h
                    if i >= 3:
                        pe.wait_ge(hid_ready, i - 2)
                    for k in range(KT):
                        last = mm3(ps[:, UB[i % 3], 0:HALF], ex_hi[:, e % 4, 0, k * FF:(k + 1) * FF], ex_lo[:, e % 4, 0, k * FF:(k + 1) * FF],
                                   x1t_hi[:, k, h * HALF:(h + 1) * HALF], x1t_lo[:, k, h * HALF:(h + 1) * HALF], k == 0, k == KT - 1)
                    last.then_inc(hid_mm, 1)
            hidden(0)
            for e in range(NX):
                if e + 1 < NX:
                    hidden(e + 1)
                pe.wait_ge(hg_ready, 2 * e + 2)
                for t in range(NT):
                    last = mm3(ps[0:TP, AGG[t], :], hg_hi[:, e % 2, t * TP:(t + 1) * TP], hg_lo[:, e % 2, t * TP:(t + 1) * TP],
                               ex_hi[:, e % 4, 1, :], ex_lo[:, e % 4, 1, :], e == 0, False)
                last.then_inc(ex_used, 1)
            pe.wait_ge(route_split, 1)
            for t in range(NT):
                last = mm3(ps[0:TP, AGG[t], :], route_hi[:, t * TP:(t + 1) * TP], route_lo[:, t * TP:(t + 1) * TP],
                           out_b_hi[:], out_b_lo[:], False, True)
                last.then_inc(ffn_mm, 1)


_INS = ['x', 'src', 'dst', 'edge_type_2', 'L0_gnn_basis1', 'L0_gnn_att1', 'L0_gnn_gate_w1', 'L0_gnn_root1',
        'L0_gnn_bias1', 'L0_gnn_basis2', 'L0_gnn_att2', 'L0_gnn_gate_w2', 'L0_gnn_root2', 'L0_gnn_bias2',
        'L0_mix_w', 'L0_mix_Wkqv', 'L0_mix_bkqv', 'L0_mix_Wo', 'L0_mix_bo', 'L0_mix_W1', 'L0_mix_b1',
        'L0_mix_W2', 'L0_mix_b2', 'L0_mix_g1', 'L0_mix_be1', 'L0_mix_g2', 'L0_mix_be2', 'L0_ffn_Wr_sp',
        'L0_ffn_br_sp', 'L0_ffn_Wr_fq', 'L0_ffn_br_fq', 'L0_ffn_Ws1', 'L0_ffn_bs1', 'L0_ffn_Ws2',
        'L0_ffn_bs2', 'L0_ffn_W1_sp', 'L0_ffn_b1_sp', 'L0_ffn_W2_sp', 'L0_ffn_b2_sp', 'L0_ffn_W1_fq',
        'L0_ffn_b1_fq', 'L0_ffn_W2_fq', 'L0_ffn_b2_fq']
_OUTS = [((NODES, D), 'float32')]


def kernel(**inputs):
    import numpy as _np
    import concourse.bacc as _bacc
    from concourse import mybir as _mybir
    from concourse.bass_utils import run_bass_kernel_spmd as _run

    nc = _bacc.Bacc("TRN2", target_bir_lowering=False, num_devices=1)
    arrays, args = {}, []
    for name in _INS:
        a = _np.ascontiguousarray(inputs[name])
        arrays[f"in_{name}_dram"] = a
        args.append(nc.dram_tensor(f"in_{name}_dram", a.shape, _mybir.dt.from_np(a.dtype), kind="ExternalInput").ap())
    for i, (shape, dtype) in enumerate(_OUTS):
        dt = _mybir.dt.from_np(_np.dtype(dtype))
        args.append(nc.dram_tensor(f"out_{i}_dram", shape, dt, kind="ExternalOutput").ap())
    gnn_mix_ffn(nc, *args)
    r = _run(nc, [arrays], core_ids=[0])
    return r.results[0]["out_0_dram"]
```

```python
from contextlib import ExitStack

import concourse.bass as bass
from concourse import mybir

F32, F32R, F16 = mybir.dt.float32, mybir.dt.float32r, mybir.dt.float16
I32, I16 = mybir.dt.int32, mybir.dt.int16
ALU, ACT, AX = mybir.AluOpType, mybir.ActivationFunctionType, mybir.AxisListType
RMAX = bass.bass_isa.ReduceOp.max

NODES, D = 625, 512
NT, TP = 5, 125
NPAD, HALF = 628, 314
KT = D // 128
EDGES, TE = 10000, 125
ET = EDGES // TE
TB, GROUPS = 4, ET // 4
CW = 626
CB = CW // 2
REL_KEY = 1000
EXACT = 4096
REL, BASES = 2, 30
GB = 8
NG = (BASES + GB - 1) // GB
QI = 16
CHUNKS = D // QI // 4
PARTS = 2 * CHUNKS * NG
WIDE = 6 * NG
M = 256
E, FF = 8, 128
BANK = 512


def gnn_mix_ffn(nc, x, src, dst, edge_type, basis1, att1, gate_w1, root1, bias1, basis2, att2, gate_w2,
                root2, bias2, w, Wkqv, bkqv, Wo, bo, W1, b1, W2, b2, g1, be1, g2, be2, Wr_sp, br_sp,
                Wr_fq, br_fq, Ws1, bs1, Ws2, bs2, W1_sp, b1_sp, W2_sp, b2_sp, W1_fq, b1_fq, W2_fq,
                b2_fq, out):
    with ExitStack() as ctx:
        def sem(name):
            return ctx.enter_context(nc.semaphore(name))

        top = [16512]

        def region(size):
            at = top[0]
            top[0] += -(-size // 32) * 32
            assert top[0] <= 229344, top[0]
            return at

        def place(name, shape, dtype, at):
            return nc.alloc_sbuf_tensor_at(name, shape, dtype, offset=-(-at // 32) * 32)

        def own(name, shape, dtype=F32):
            n = {F32: 4, F32R: 4, I32: 4, F16: 2, I16: 2}[dtype]
            for s in shape[1:]:
                n *= s
            return place(name, shape, dtype, region(n))

        ident = own("ident", [128, 128])
        colv = own("colv", [128, 45])
        bias_row = own("bias_row", [128, 6, D])
        gate_hi = own("gate_hi", [128, 2, KT, REL], F32R)
        gate_lo = own("gate_lo", [128, 2, KT, REL], F32R)
        att_col = own("att_col", [128, 2, NG, REL])
        sel_q = own("sel_q", [128, QI])
        sel_att = own("sel_att", [128, 2, NG, REL, QI])
        gates = own("gates", [TP, NT, REL])
        bn = own("bn", [TP, NT, 6])
        stat = own("stat", [TP, NT, 2])
        veps = own("veps", [TP, NT])
        rstd = own("rstd", [TP, NT])
        neg_half_pow = own("neg_half_pow", [TP, NT])
        neg_half = own("neg_half", [128, 1])
        ones = own("ones", [128, 128])
        xd = own("xd", [TP, NT])
        d_sum = own("d_sum", [TP, NT])
        rec = own("rec", [TP, NT])
        range_i = own("range_i", [1, 3, NT], I32)
        count_acc = own("count_acc", [TP, NT * REL * 2])
        count_max = own("count_max", [TP, NT * REL * 2])
        many_i = own("many_i", [1, 1], I32)
        x1_shift = own("x1_shift", [TP, NT])

        KB628, KB512 = KT * NPAD * 4, NT * D * 4
        counts = own("counts", [TP, NT, REL * CW], I16)
        r_ring = region(4 * 8192)
        r_split = region(4 * 8192)
        stag = own("stag", [128, 2, D])
        r_wraw = region(KT * REL * D * 4)
        r_raw = region(2 * KT * D * 4)
        r_ht = region(2 * KB628)
        r_h1t = region(KB512)
        r_u = region(2 * KB512)
        r_cf = region(NT * CW * 4)
        r_extra = region(18720)

        ring = [place(f"ring{i}", [128, 4 * D], F32, r_ring + i * 8192) for i in range(8)]
        xa = place("xa", [TP, NT, D], F32, r_u)
        xn = place("xn", [TP, NT, D], F32, r_h1t)
        xn2 = place("xn2", [TP, NT, D], F32, r_extra)
        gate_rows = place("gate_rows", [REL, 2, D], F32, r_wraw)
        att_rep = place("att_rep", [REL, 2, BASES * QI], F32, r_wraw + 8448)
        att_rows = place("att_rows", [REL, 2, BASES], F32, r_wraw + 8192)
        row_vec = place("row_vec", [45, 128], F32, r_wraw + 4096)
        oh_n = place("oh_n", [TE, 2, TB, CW], F16, r_cf)
        oh_m = place("oh_m", [TE, 2, TB, REL * TE], F16, r_raw + 8192)
        zeros = place("zeros", [TE, TE], F16, r_cf + 2 * TB * CW * 2)
        xt_tmp = [place(f"xt_tmp{i}", [128, KT, TP], F32, r_raw + 12288 + i * 2016) for i in range(2)]
        o = r_u + KB512
        iota_n = place("iota_n", [TE, CW], F16, o)
        iota_m = place("iota_m", [TE, REL * TE], F16, o + 1280)
        keys = place("keys", [TE, 2, GROUPS, TB], F32, o + 2528)
        key_m = place("key_m", [TE, NT, GROUPS, TB], F32, o + 3200)
        edge_i = place("edge_i", [ET, 3, TE], I32, o + 4800)
        edge_f = place("edge_f", [ET, 3, TE], F32, o + 6304)
        key_r = place("key_r", [ET, TE], F32, o + 7808)
        o += 8320
        mnmx = place("mnmx", [ET, 2], F32, o)
        tile_id = place("tile_id", [ET, 2, NT], F32, o + 32)
        tile_ii = place("tile_ii", [ET, 2, NT], I32, o + 96)
        node_lo = place("node_lo", [ET, NT], F32, o + 160)
        in_lo = place("in_lo", [ET, NT], F32, o + 192)
        in_hi = place("in_hi", [ET, NT], F32, o + 224)
        bound = place("bound", [ET, 2, NT], F32, o + 256)
        bound_all = place("bound_all", [ET, 2, NT], F32, o + 320)
        range_f = place("range_f", [1, 3, NT], F32, o + 384)
        mean_acc = place("mean_acc", [TP, 2, NT], F32, o + 448)
        square_acc = place("square_acc", [TP, 2, NT], F32, o + 512)
        minus_mean = place("minus_mean", [TP, 2, NT], F32, o + 576)
        shift = place("shift", [TP, 2, NT], F32, o + 640)
        rstd_x = place("rstd_x", [TP, 2, NT], F32, o + 704)
        w_raw = place("w_raw", [128, KT, REL, D], F32, r_wraw)
        piece_raw = [place(f"piece_raw{i}", [128, KT, D], F32, r_raw + i * KT * D * 4) for i in range(2)]
        piece_hi = [place(f"piece_hi{i}", [128, KT, D], F32R, a) for i, a in
                    enumerate((r_split, r_split + 16384, r_wraw))]
        piece_lo = [place(f"piece_lo{i}", [128, KT, D], F32R, a + 8192) for i, a in
                    enumerate((r_split, r_split + 16384, r_wraw))]
        ht_hi = place("ht_hi", [128, KT, NPAD], F32R, r_ht)
        ht_lo = place("ht_lo", [128, KT, NPAD], F32R, r_ht + KB628)
        xt_hi = h2t_hi = x1t_hi = ht_hi
        xt_lo = h2t_lo = x1t_lo = ht_lo
        qp_hi, qp_lo = ht_hi[:, 0:2, :], ht_lo[:, 0:2, :]
        u_hi = [place(f"u_hi{l}", [TP, NT, D], F32R, a) for l, a in enumerate((r_u + KB512, r_ring))]
        u_lo = [place(f"u_lo{l}", [TP, NT, D], F32R, a) for l, a in enumerate((r_extra, r_ring + KB512))]
        cf = place("cf", [TP, NT, CW], F32R, r_cf)
        row_tmp = place("row_tmp", [TP, 2, D], F32, r_extra + 14336)
        gate_row = place("gate_row", [REL, NPAD], F32, r_extra + 10240)
        kq_hi = place("kq_hi", [128, KT, NPAD], F32R, r_u)
        kq_lo = place("kq_lo", [128, KT, NPAD], F32R, r_u + KB628)
        y = place("y", [TP, NT, D], F32, r_u)
        v = place("v", [TP, NT, D], F32, r_u + KB512)
        kp = place("kp", [TP, NT, M], F32, r_cf)
        qpt = place("qpt", [128, 2, NPAD], F32, r_cf + 5120)
        wt_hi = place("wt_hi", [128, KT, M], F32R, r_extra + 10240)
        wt_lo = place("wt_lo", [128, KT, M], F32R, r_extra + 10240 + 4096)
        w_nat = place("w_nat", [128, 2, D], F32, r_wraw + 12288)
        feat = place("feat", [TP, 2, M], F32, r_extra + 4096)
        square = place("square", [128, NPAD], F32, r_extra + 6144)
        sq_sum = place("sq_sum", [128, NPAD], F32, r_extra + 1024)
        qk = place("qk", [TP, M], F32, r_extra)
        ksum = place("ksum", [TP, M], F32, r_extra + 8672)
        kvt_hi = place("kvt_hi", [128, KT, M], F32R, r_extra + 10240)
        kvt_lo = place("kvt_lo", [128, KT, M], F32R, r_extra + 10240 + 4096)
        kvw_hi = place("kvw_hi", [128, 2, D], F32R, r_extra)
        kvw_lo = place("kvw_lo", [128, 2, D], F32R, r_extra + 4096)
        x_again = place("x_again", [TP, NT, D], F32, r_h1t)
        yn = place("yn", [TP, 2, D], F32, r_extra + 14336)
        h2_tmp = [place(f"h2_tmp{i}", [128, KT, TP], F32, r_extra + i * 2016) for i in range(2)]
        act_tmp = place("act_tmp", [128, 2, NPAD], F32, r_extra + 10240)
        act_hi = place("act_hi", [128, KT, NPAD], F32R, r_u + KB512)
        act_lo = place("act_lo", [128, KT, NPAD], F32R, r_u + KB512 + KB628)
        x1 = place("x1", [TP, NT, D], F32, r_wraw)
        x1n = place("x1n", [TP, 2, D], F32, r_extra)
        router_raw = place("router_raw", [128, KT, 2 * E], F32, r_extra + 4096)
        router_hi = place("router_hi", [128, KT, 2 * E], F32R, r_extra + 4096 + 256)
        router_lo = place("router_lo", [128, KT, 2 * E], F32R, r_extra + 4096 + 512)
        router_b = place("router_b", [2 * E, 1], F32, r_extra + 4096 + 768)
        o = r_extra + 4096 + 1024
        logit = place("logit", [TP, NT, 2, E], F32, o)
        lmax = place("lmax", [TP, NT, 2], F32, o + 320)
        shifted = place("shifted", [TP, NT, 2, E], F32, o + 384)
        expo = place("expo", [TP, NT, 2, E], F32, o + 704)
        denom = place("denom", [TP, NT, 2], F32, o + 1024)
        gate_p = place("gate_p", [TP, NT, 2], F32, o + 1088)
        rank = place("rank", [TP, NT, 2, E], F32, o + 1152)
        score = place("score", [TP, NT, 2, E], F32, o + 1472)
        best = place("best", [TP, NT, 2], F32, o + 1792)
        route = place("route", [TP, NT, 2, E], F32, o + 1856)
        o += 2208
        route_t = place("route_t", [2 * E, NPAD], F32, o)
        route_hi = place("route_hi", [2 * E, NPAD], F32R, o + 2528)
        route_lo = place("route_lo", [2 * E, NPAD], F32R, o + 2 * 2528)
        o += 3 * 2528
        assert o <= r_extra + 18720
        out_bias = place("out_bias", [2 * E, D], F32, r_raw + 4 * 4096 - 2048)
        out_b_hi = place("out_b_hi", [2 * E, D], F32R, r_wraw + KB512)
        out_b_lo = place("out_b_lo", [2 * E, D], F32R, r_wraw + KB512 + 2048)
        route_all = place("route_all", [128, 2 * E, NPAD], F32, r_h1t)
        assert r_h1t + 2 * E * NPAD * 4 <= r_extra
        XR = 3
        ex_raw = place("ex_raw", [128, XR, 2, D], F32, r_raw)
        ex_hi = place("ex_hi", [128, 4, 2, D], F32R, r_split)
        ex_lo = place("ex_lo", [128, 4, 2, D], F32R, r_split + 16384)
        o = r_ring
        hid = place("hid", [128, 6, HALF], F32, o)
        gated = place("gated", [128, 4, HALF], F32, o + 7552)
        hg_hi = place("hg_hi", [128, 2, NPAD], F32R, o + 12576)
        hg_lo = place("hg_lo", [128, 2, NPAD], F32R, o + 17600)
        logit_row = place("logit_row", [2 * E, NPAD], F32, o + 22624)
        final = place("final", [TP, 2, D], F32, r_extra)

        ps = ctx.enter_context(nc.psum_tensor("ps", [128, 8, BANK], F32))
        rel_dram = [nc.dram_tensor(f"rel_dram{l}", (KT, REL, CHUNKS, QI, D), F32, kind="Internal").ap()
                    for l in range(2)]
        route_dram = nc.dram_tensor("route_dram", (2 * E, NPAD), F32, kind="Internal").ap()

        edges_in, x_in, rows_in, smalls_in = sem("edges_in"), sem("x_in"), sem("rows_in"), sem("smalls_in")
        mean_sum, square_sum, minus_mean_ready = sem("mean_sum"), sem("square_sum"), sem("minus_mean_ready")
        att_in, att_col_ready = sem("att_in"), sem("att_col_ready")
        count_mm, count_bound, many_ready, rest_ready, rest_used = (
            sem("count_mm"), sem("count_bound"), sem("many_ready"), sem("rest_ready"), sem("rest_used"))
        basis_in = [sem(f"basis_in{i}") for i in range(8)]
        raw_in = [sem(f"raw_in{i}") for i in range(2)]
        rel_out = [sem(f"rel_out{i}") for i in range(2)]
        rel_back = [sem(f"rel_back{t}") for t in range(KT)]
        w_in, router_in, route_out, route_back = sem("w_in"), sem("router_in"), sem("route_out"), [sem(f"route_back{i}") for i in range(4)]
        x_again_in = sem("x_again_in")
        out_b_in = sem("out_b_in")
        ex_in = [sem(f"ex_in{i}") for i in range(XR)]
        stored = [sem(f"stored{i}") for i in range(2)]
        ident_ready, iotas_ready, consts_ready = (
            sem("ident_ready"), sem("iotas_ready"), sem("consts_ready"))
        key_ready, bound_ready, bound_max, keys_t, range_ready = (
            sem("key_ready"), sem("bound_ready"), sem("bound_max"), sem("keys_t"), sem("range_ready"))
        one_hot, group_used, count_ready = sem("one_hot"), sem("group_used"), sem("count_ready")
        var_ready, rstd_ready, xn_ready, xn2_ready = sem("var_ready"), sem("rstd_ready"), sem("xn_ready"), sem("xn2_ready")
        cols_ready, gate_rows_t, gate_w_hi, gate_w_ready = (
            sem("cols_ready"), sem("gate_rows_t"), sem("gate_w_hi"), sem("gate_w_ready"))
        sel_ready, att_ready = sem("sel_ready"), sem("att_ready")
        hT_t, hT_hi, hT_ready = sem("hT_t"), sem("hT_hi"), sem("hT_ready")
        basis_used, rel_sum, rel_evac = sem("basis_used"), sem("rel_sum"), sem("rel_evac")
        split_done, piece_used = sem("split_done"), sem("piece_used")
        gate_mm, gate_row_ready, gate_t, gates_ready = (
            sem("gate_mm"), sem("gate_row_ready"), sem("gate_t"), sem("gates_ready"))
        u_mm, u_hi_done, u_ready, cf_ready, rel_applied, agg_done = (
            sem("u_mm"), sem("u_hi_done"), sem("u_ready"), sem("cf_ready"), sem("rel_applied"), sem("agg_done"))
        h_added, h_relu = sem("h_added"), sem("h_relu")
        xt_t, xt_scaled, xt_hi_done, xt_ready = sem("xt_t"), sem("xt_scaled"), sem("xt_hi_done"), sem("xt_ready")
        wt_t, wt_hi_done, wt_ready = sem("wt_t"), sem("wt_hi_done"), sem("wt_ready")
        kq_mm, kq_hi_done, sq_ready, kq_ready, sq_summed, xd_mm, xd_ready = (
            sem("kq_mm"), sem("kq_hi_done"), sem("sq_ready"), sem("kq_ready"), sem("sq_summed"), sem("xd_mm"), sem("xd_ready"))
        feat_mm, feat_exp, feat_ready, qp_t, qpt_ready = (
            sem("feat_mm"), sem("feat_exp"), sem("feat_ready"), sem("qp_t"), sem("qpt_ready"))
        v_mm, v_ready, kv_mm, kv_hi_done, kv_ready, ksum_ready, kvw_mm, kvw_hi_done, kvw_ready, qp_hi_done, qp_ready, ksum_mm, d_part = (
            sem("v_mm"), sem("v_ready"), sem("kv_mm"), sem("kv_hi_done"), sem("kv_ready"), sem("ksum_ready"), sem("kvw_mm"), sem("kvw_hi_done"),
            sem("kvw_ready"), sem("qp_hi_done"), sem("qp_ready"), sem("ksum_mm"), sem("d_part"))
        wo_mm, yn_ready, h2_t, h2_scaled, h2_hi_done, h2t_ready = (
            sem("wo_mm"), sem("yn_ready"), sem("h2_t"), sem("h2_scaled"), sem("h2_hi_done"), sem("h2t_ready"))
        y_plus_b = sem("y_plus_b")
        act_mm, act_done, act_ready, w2_mm, xm_ready, xm_plus_x = (
            sem("act_mm"), sem("act_done"), sem("act_ready"), sem("w2_mm"), sem("xm_ready"), sem("xm_plus_x"))
        x1n_ready, x1_t, x1_hi_done, x1t_ready = (
            sem("x1n_ready"), sem("x1_t"), sem("x1_hi_done"), sem("x1t_ready"))
        router_w_ready, logit_mm, shift_ready, expo_ready, route_ready, route_tr, route_t_ready, route_split = (
            sem("router_w_ready"), sem("logit_mm"), sem("shift_ready"), sem("expo_ready"), sem("route_ready"),
            sem("route_tr"), sem("route_t_ready"), sem("route_split"))
        x1_plus_b, x1_shift_ready = sem("x1_plus_b"), sem("x1_shift_ready")
        logit_row_ready, logit_t, ex_hi_done = sem("logit_row_ready"), sem("logit_t"), sem("ex_hi_done")
        NX = 2 * E + 1
        HIDDEN = [(0, 0), (1, 0), (0, 1), (1, 1)] + [(e, h) for e in range(2, NX) for h in range(2)]
        HID_AT = {eh: n for n, eh in enumerate(HIDDEN)}
        HB = 6
        ex_split, ex_used, hid_mm, hid_ready, hg_ready, ffn_mm, final_ready = (
            sem("ex_split"), sem("ex_used"), sem("hid_mm"), sem("hid_ready"), sem("hg_ready"), sem("ffn_mm"), sem("final_ready"))
        dve_own, pool_own = sem("dve_own"), sem("pool_own")

        basis_rows = [b.rearrange("b (c q t) o -> c b q (t o)", q=QI, t=KT) for b in (basis1, basis2)]
        LOADED = {"k": 0, "q": 1, "v": 2, "Wo": 3, "W1": 4, "W2": 5, "root1": 6, "root2": 7}
        ORDER = ["k", "q", "v", "Wo", "W1", "W2", "rel1_0", "root1", "rel1_1", "rel2_0", "root2", "rel2_1"]
        PIECE = {name: n for n, name in enumerate(ORDER)}
        SPLIT_OF_LOAD = [PIECE[name] for name in LOADED]

        def piece(name):
            s = PIECE[name]
            return s, piece_hi[s % 2 if s else 2], piece_lo[s % 2 if s else 2]
        perm = "(p t) n -> p t n"
        nat = "(t p) n -> p t n"
        piece_src = {
            "root1": [root1.rearrange(perm, t=KT)], "root2": [root2.rearrange(perm, t=KT)],
            "k": [Wkqv[:, 0:D].rearrange(nat, p=128)], "q": [Wkqv[:, D:2 * D].rearrange(nat, p=128)],
            "v": [Wkqv[:, 2 * D:3 * D].rearrange(nat, p=128)], "Wo": [Wo.rearrange(nat, p=128)],
            "W1": [W1.rearrange(nat, p=128)], "W2": [W2.rearrange(nat, p=128)]}
        ex_w1 = [Ws1] + [W1_sp[e] for e in range(E)] + [W1_fq[e] for e in range(E)]
        ex_w2 = [Ws2] + [W2_sp[e] for e in range(E)] + [W2_fq[e] for e in range(E)]
        BACK = [(0, 1), (1, 4), (4, 8), (8, 16)]
        C_G1, C_BE1, C_G2, C_BE2, C_BK, C_B1, C_EXP = 0, 4, 8, 12, 16, 24, 28

        AGG = [0, 1, 2, 5, 6]
        UB = [7, 4, 3]
        LB = [7, 4]

        def u_bank(i):
            return LB[i % 2] if i < 2 * NT else (3, 4, 7)[(i - 2 * NT) % 3]

        COUNT_BANK = [[0, 1], [2, 7]]

        def basis_turn(i):
            if i < WIDE:
                return i % 8, i // 8 + 1
            return i % 4, (WIDE - 1 - i % 4) // 8 + 1 + (i - WIDE) // 4 + 1

        def rel_bank(ch):
            return 3 + ch % 2 if ch < 2 * CHUNKS - 2 else 3

        block = ctx.enter_context(nc.Block())

        @block.sync
        def _(sp):
            def load_part(i):
                ch, g = divmod(i, NG)
                nb = min(GB, BASES - g * GB)
                slot, _ = basis_turn(i)
                if i >= WIDE:
                    sp.wait_ge(basis_used, i - 4 + 1)
                elif i >= 8:
                    sp.wait_ge(basis_used, i - 8 + 1)
                sp.dma_start(ring[slot][0:nb * QI, :], basis_rows[ch // CHUNKS][ch % CHUNKS, g * GB:g * GB + nb]
                             ).then_inc(basis_in[slot], 16)

            def store_chunk(ch):
                sp.wait_ge(rel_evac, ch + 1)
                sp.dma_start(rel_dram[ch // CHUNKS][:, :, ch % CHUNKS].rearrange("t r q n -> (t r) q n"),
                             stag[:, ch % 2, :]).then_inc(rel_out[ch % 2], 16)

            def read_relations(l):
                for s in rel_out:
                    sp.wait_ge(s, 16 * (CHUNKS // 2) * (l + 1))
                if l == 0:
                    sp.wait_ge(piece_used, PIECE["k"] + 1)
                else:
                    sp.wait_ge(split_done, PIECE["rel1_1"] + 1)
                for t in range(KT):
                    sp.dma_start(w_raw[:, t, :, :], rel_dram[l][t].rearrange("r c q n -> (c q) r n")
                                 ).then_inc(rel_back[t], 16)

            def load_piece(name):
                n = LOADED[name]
                if n >= 2:
                    sp.wait_ge(split_done, SPLIT_OF_LOAD[n - 2] + 1)
                for s in piece_src[name]:
                    sp.dma_start(piece_raw[n % 2][:, :, :], s).then_inc(raw_in[n % 2], 16)

            for k, a in enumerate((src, dst, edge_type)):
                sp.dma_start(edge_i[:, k, :], a.rearrange("(t e) -> t e", e=TE)).then_inc(edges_in, 16)
            for l, a in enumerate((att1, att2)):
                sp.dma_start(att_rows[:, l, :], a).then_inc(att_in, 16)
            for l, gw in enumerate((gate_w1, gate_w2)):
                sp.dma_start(gate_rows[:, l, :], gw.rearrange("r i o -> r (i o)")).then_inc(rows_in, 16)
            at = 0
            for a in (g1, be1, g2, be2, bkqv[0:2 * D], b1, bs1):
                n = a.shape[0] // 128
                sp.dma_start(row_vec[at:at + n, :], a.rearrange("(t p) -> t p", p=128)).then_inc(rows_in, 16)
                at += n
            for a in (b1_sp, b1_fq):
                sp.dma_start(row_vec[at:at + E, :], a).then_inc(rows_in, 16)
                at += E
            sp.dma_start(xa[:, :, :], x.rearrange("(t p) n -> p t n", p=TP)).then_inc(x_in, 16)
            for i in range(4):
                load_part(i)
            sp.dma_start(w_nat[:, :, :], w.rearrange("(t p) n -> p t n", p=128)).then_inc(w_in, 16)
            for i in range(4, 8):
                load_part(i)
            load_piece("k")
            for n, a in enumerate((bias1, bias2, bkqv[2 * D:3 * D], bo, b2, bs2)):
                sp.dma_start(bias_row[:, n, :], a.partition_broadcast(128)).then_inc(smalls_in, 16)
            piece_after = {24: "q", 27: "v", 30: "Wo", 34: "W1", 40: "W2", 50: "root1", 62: "root2"}
            chunk = 0
            for i in range(8, PARTS):
                load_part(i)
                while chunk < 2 * CHUNKS and i >= min(NG * chunk + (12 if NG * chunk + 12 <= WIDE else 9), PARTS - 1):
                    store_chunk(chunk)
                    chunk += 1
                if i == 24:
                    sp.wait_ge(xt_ready, NT)
                    sp.wait_ge(count_ready, NT)
                if i == 39:
                    read_relations(0)
                if i in piece_after:
                    load_piece(piece_after[i])
            sp.wait_ge(hT_t, NT)
            sp.dma_start(x_again[:, :, :], x.rearrange("(t p) n -> p t n", p=TP)).then_inc(x_again_in, 16)
            read_relations(1)
            sp.wait_ge(rel_applied, 2)
            for n, a in enumerate((Wr_sp, Wr_fq)):
                sp.dma_start(router_raw[:, :, n * E:(n + 1) * E], a.rearrange("(p t) e -> p t e", p=128),
                             allow_slow_non_contiguous=True).then_inc(router_in, 16)
            for n, a in enumerate((br_sp, br_fq)):
                sp.dma_start(router_b[n * E:(n + 1) * E, :], a.rearrange("(e o) -> e o", o=1),
                             allow_slow_non_contiguous=True).then_inc(router_in, 16)

            def load_expert(e):
                if e == 0:
                    sp.wait_ge(split_done, PIECE["root2"] + 1)
                if e >= XR:
                    sp.wait_ge(ex_split, e - XR + 1)
                sp.dma_start(ex_raw[:, e % XR, 0, :].rearrange("p (t f) -> p t f", t=KT),
                             ex_w1[e].rearrange("(p t) f -> p t f", p=128)).then_inc(ex_in[e % XR], 16)
                sp.dma_start(ex_raw[:, e % XR, 1, :], ex_w2[e]).then_inc(ex_in[e % XR], 16)
            for e in range(XR):
                load_expert(e)
            for n, a in enumerate((b2_sp, b2_fq)):
                sp.dma_start(out_bias[n * E:(n + 1) * E, :], a).then_inc(out_b_in, 16)
            load_expert(XR)
            load_expert(XR + 1)
            sp.wait_ge(route_t_ready, 1)
            sp.dma_start(route_dram, route_t[:, :]).then_inc(route_out, 16)
            sp.wait_ge(route_out, 16)
            for n, (a, b) in enumerate(BACK):
                sp.dma_start(route_all[:, a:b, :], route_dram[a:b].partition_broadcast(128)).then_inc(route_back[n], 16)
                load_expert(XR + 2 + n)
            for e in range(XR + 2 + len(BACK), NX):
                load_expert(e)
            for t in range(NT):
                sp.wait_ge(final_ready, t + 1)
                sp.dma_start(out[t * TP:(t + 1) * TP, :], final[:, t % 2, :]).then_inc(stored[t % 2], 16)
            sp.wait_ge(stored[0], 16 * 3)
            sp.wait_ge(stored[1], 16 * 2)

        @block.gpsimd
        def _(pool):
            n = [0]

            def own_step(ins):
                ins.then_inc(pool_own, 1)
                n[0] += 1
                pool.wait_ge(pool_own, n[0])

            pool.memset(ident[:], 0.0).then_inc(pool_own, 1)
            n[0] += 1
            pool.iota(iota_n[:], pattern=[[1, CW]], base=0, channel_multiplier=0,
                      allow_small_or_imprecise_dtypes=True).then_inc(iotas_ready, 1)
            pool.iota(iota_m[:], pattern=[[REL_KEY, REL], [1, TE]], base=0, channel_multiplier=0,
                      allow_small_or_imprecise_dtypes=True).then_inc(iotas_ready, 1)
            pool.iota(tile_id[:], pattern=[[0, 2], [0, NT]], base=0, channel_multiplier=1,
                      allow_small_or_imprecise_dtypes=True).then_inc(iotas_ready, 1)
            pool.iota(node_lo[:], pattern=[[TP, NT]], base=0, channel_multiplier=0,
                      allow_small_or_imprecise_dtypes=True).then_inc(iotas_ready, 1)
            pool.wait_ge(pool_own, 1)
            pool.affine_select(out=ident[:], in_=ident[:], compare_op=ALU.not_equal, fill=1.0, base=0,
                               pattern=[[-1, 128]], channel_multiplier=1).then_inc(ident_ready, 1)
            pool.memset(zeros[:], 0.0).then_inc(consts_ready, 1)
            pool.memset(neg_half_pow[:], -0.5).then_inc(consts_ready, 1)
            pool.memset(neg_half[:], -0.5).then_inc(consts_ready, 1)
            pool.memset(ones[:], 1.0).then_inc(consts_ready, 1)
            pool.memset(att_col[:], 0.0).then_inc(consts_ready, 1)
            pool.wait_ge(consts_ready, 5)
            pool.wait_ge(bound_ready, 1)
            pool.partition_all_reduce(bound_all[:].rearrange("p a j -> p (a j)"),
                                      bound[:].rearrange("p a j -> p (a j)"), ET, RMAX).then_inc(bound_max, 1)
            for a in (xt_hi, xt_lo):
                pool.memset(a[:, :, NODES:NPAD].bitcast(F32), 0.0).then_inc(consts_ready, 1)
            for k in range(2):
                pool.wait_ge(mean_sum, k + 1)
                pool.tensor_scalar(minus_mean[:, k, :], mean_acc[:, k, :], -1.0 / D, None, ALU.mult).then_inc(minus_mean_ready, 1)
                pool.wait_ge(square_sum, k + 1)
                own_step(pool.tensor_scalar(rstd_x[:, k, :], square_acc[:, k, :], 1.0 / D, 1e-5, ALU.mult, ALU.add))
                own_step(pool.tensor_tensor(rstd_x[:, k, :], rstd_x[:, k, :], neg_half_pow[:], ALU.pow))
                pool.tensor_tensor(shift[:, k, :], minus_mean[:, k, :], rstd_x[:, k, :], ALU.mult).then_inc(rstd_ready, 1)

            def power(k, t):
                pool.wait_ge(var_ready, k)
                pool.tensor_tensor(rstd[:, t:t + 1], veps[:, t:t + 1], neg_half_pow[:, t:t + 1], ALU.pow).then_inc(rstd_ready, 1)

            def split(name):
                s, p_hi, p_lo = piece(name)
                if s == 0:
                    pool.wait_ge(gate_rows_t, 1)
                    pool.wait_ge(wt_t, 2)
                elif s <= 2:
                    pool.wait_ge(basis_used, WIDE)
                else:
                    pool.wait_ge(piece_used, s - 1)
                for t in range(KT):
                    if name[:3] == "rel":
                        l, r = int(name[3]) - 1, int(name[5])
                        pool.wait_ge(rel_back[t], 16 * (l + 1))
                        raw = w_raw[:, t, r, :]
                    else:
                        k = LOADED[name]
                        if t == 0:
                            pool.wait_ge(raw_in[k % 2], 16 * (k // 2 + 1))
                        raw = piece_raw[k % 2][:, t, :]
                    hi, lo = p_hi[:, t, :], p_lo[:, t, :]
                    own_step(pool.tensor_copy(hi, raw))
                    last = pool.tensor_tensor(lo, raw, hi.bitcast(F32), ALU.subtract)
                    if t < KT - 1:
                        own_step(last)
                last.then_inc(split_done, 1)
                pool.wait_ge(split_done, s + 1)
            split("k")
            for t in range(NT):
                pool.wait_ge(xt_hi_done, t + 1)
                pool.tensor_tensor(xt_lo[:, :, t * TP:(t + 1) * TP], xt_tmp[t % 2][:], xt_hi[:, :, t * TP:(t + 1) * TP].bitcast(F32),
                                   ALU.subtract).then_inc(xt_ready, 1)
            pool.wait_ge(count_ready, NT)
            pool.partition_all_reduce(count_max[:], count_acc[:], TP, RMAX).then_inc(count_bound, 1)
            pool.wait_ge(smalls_in, 16 * 6)
            own_step(pool.tensor_tensor(bias_row[:, 4, :], bias_row[:, 4, :], bias_row[:, 1, :], ALU.add))
            for name in ("q", "v", "Wo", "W1"):
                split(name)
            for t in range(NT):
                power(t + 1, t)
            for t in range(NT):
                pool.wait_ge(yn_ready, t + 1)
                pool.tensor_tensor(y[:, t, :], y[:, t, :], bias_row[0:TP, 4, :], ALU.add).then_inc(y_plus_b, 1)
            split("W2")
            split("rel1_0")
            split("root1")
            split("rel1_1")
            pool.wait_ge(x_again_in, 16)
            for t in range(NT):
                pool.wait_ge(xm_ready, t + 1)
                pool.tensor_tensor(y[:, t, :], y[:, t, :], x_again[:, t, :], ALU.add).then_inc(xm_plus_x, 1)
            split("rel2_0")
            split("root2")
            pool.wait_ge(rel_applied, 2)
            pool.iota(rank[:], pattern=[[0, 2 * NT], [-1, E]], base=E, channel_multiplier=0,
                      allow_small_or_imprecise_dtypes=True).then_inc(pool_own, 1)
            n[0] += 1
            split("rel2_1")
            pool.wait_ge(router_in, 16 * 4)
            own_step(pool.tensor_copy(router_hi[:], router_raw[:]))
            pool.tensor_tensor(router_lo[:], router_raw[:], router_hi[:].bitcast(F32), ALU.subtract).then_inc(router_w_ready, 1)

            def split_expert(e):
                pool.wait_ge(ex_hi_done, e + 1)
                raw, hi, lo = ex_raw[:, e % XR], ex_hi[:, e % 4], ex_lo[:, e % 4]
                pool.tensor_tensor(lo, raw, hi.bitcast(F32), ALU.subtract).then_inc(ex_split, 1)
            split_expert(0)
            split_expert(1)
            for t in range(NT):
                power(NT + t + 1, t)
                pool.wait_ge(rstd_ready, 2 + NT + t + 1)
                pool.tensor_scalar(x1_shift[:, t:t + 1], stat[:, t, 0:1], rstd[:, t:t + 1], -1.0, ALU.mult, ALU.mult
                                   ).then_inc(x1_shift_ready, 1)
            split_expert(2)
            split_expert(3)
            pool.wait_ge(out_b_in, 16 * 2)
            own_step(pool.tensor_copy(out_b_hi[:], out_bias[:]))
            own_step(pool.tensor_tensor(out_b_lo[:], out_bias[:], out_b_hi[:].bitcast(F32), ALU.subtract))
            pool.wait_ge(route_t_ready, 1)
            own_step(pool.tensor_copy(route_hi[:], route_t[:]))
            pool.tensor_tensor(route_lo[:], route_t[:], route_hi[:].bitcast(F32), ALU.subtract).then_inc(route_split, 1)
            for e in range(4, NX):
                split_expert(e)
                t = e - 5
                if 0 <= t < NT:
                    pool.wait_ge(x1n_ready, t + 1)
                    pool.tensor_tensor(x1[:, t, :], x1[:, t, :], bias_row[0:TP, 5, :], ALU.add).then_inc(x1_plus_b, 1)

        @block.vector
        def _(dve):
            n = [0]

            def own_step(ins):
                ins.then_inc(dve_own, 1)
                n[0] += 1
                dve.wait_ge(dve_own, n[0])


            def stats(source, t):
                own_step(dve.bn_stats(bn[:, t, :], source))
                own_step(dve.bn_aggr(stat[:, t, :], bn[:, t, :]))

            def add_eps(t):
                dve.tensor_scalar(veps[:, t:t + 1], stat[:, t, 1:2], 1e-5, None, ALU.add).then_inc(var_ready, 1)

            def normalise(target, source, t):
                return dve.tensor_scalar(target, source, stat[:, t, 0:1], rstd[:, t:t + 1], ALU.subtract, ALU.mult)

            dve.wait_ge(iotas_ready, 4)
            own_step(dve.tensor_scalar(tile_id[:], tile_id[:], 1.0 / TB, -(TB - 1.0) / (2 * TB), ALU.mult, ALU.add))
            own_step(dve.tensor_copy(tile_ii[:], tile_id[:]))
            own_step(dve.tensor_copy(tile_id[:], tile_ii[:]))
            own_step(dve.tensor_scalar(tile_id[:, 0, :], tile_id[:, 0, :], -1.0, float(GROUPS), ALU.mult, ALU.add))
            own_step(dve.tensor_scalar(tile_id[:, 1, :], tile_id[:, 1, :], 1.0, None, ALU.add))
            dve.wait_ge(edges_in, 48)
            own_step(dve.tensor_copy(edge_f[:], edge_i[:]))
            own_step(dve.tensor_scalar(key_r[:], edge_f[:, 2, :], 0.0, float(REL_KEY), ALU.not_equal, ALU.mult))
            dve.tensor_tensor(key_r[:], key_r[:], edge_f[:, 1, :], ALU.add).then_inc(key_ready, 1)
            dve.tensor_reduce(mnmx[:, 0:1], edge_f[:, 1, :], AX.X, ALU.min).then_inc(dve_own, 1)
            n[0] += 1
            own_step(dve.tensor_reduce(mnmx[:, 1:2], edge_f[:, 1, :], AX.X, ALU.max))
            own_step(dve.tensor_scalar(mnmx[:, 0:1], mnmx[:, 0:1], -(TP - 1.0), None, ALU.add))
            own_step(dve.tensor_scalar(in_hi[:], node_lo[:], mnmx[:, 1:2], None, ALU.is_le))
            own_step(dve.tensor_scalar(in_lo[:], node_lo[:], mnmx[:, 0:1], None, ALU.is_ge))
            own_step(dve.tensor_tensor(in_lo[:], in_lo[:], in_hi[:], ALU.mult))
            own_step(dve.tensor_tensor(bound[:, 0, :], tile_id[:, 0, :], in_lo[:], ALU.mult))
            dve.tensor_tensor(bound[:, 1, :], tile_id[:, 1, :], in_lo[:], ALU.mult).then_inc(bound_ready, 1)
            dve.wait_ge(keys_t, 1)
            own_step(dve.tensor_copy(keys[:].rearrange("p a g t -> p (a g t)"), ps[0:TE, 6, 0:2 * ET]))
            for j in range(NT):
                dve.tensor_scalar(key_m[:, j], keys[:, 1], float(-TP * j), None, ALU.add).then_inc(dve_own, 1)
                n[0] += 1
            dve.wait_ge(dve_own, n[0])
            dve.wait_ge(ident_ready, 1)
            dve.tensor_reduce(sel_q[:], ident[:].rearrange("p (b q) -> p q b", b=GB), AX.X, ALU.add).then_inc(dve_own, 1)
            n[0] += 1
            sel_q_made = n[0]
            dve.wait_ge(bound_max, 1)
            own_step(dve.tensor_scalar(range_f[:, 1, :], bound_all[0:1, 1, :], 1.0, None, ALU.max))
            own_step(dve.tensor_scalar(range_f[:, 0, :], bound_all[0:1, 0, :], -1.0, float(GROUPS), ALU.mult, ALU.add))
            own_step(dve.tensor_scalar(bound_all[0:1, 0, :], range_f[:, 1, :], -1.0, None, ALU.add))
            own_step(dve.tensor_tensor(range_f[:, 0, :], range_f[:, 0, :], bound_all[0:1, 0, :], ALU.min))
            own_step(dve.tensor_tensor(range_f[:, 2, :], range_f[:, 1, :], range_f[:, 0, :], ALU.subtract))
            dve.tensor_copy(range_i[:], range_f[:]).then_inc(range_ready, 1)

            dve.wait_ge(range_ready, 1)
            turn = dve.alloc_register("turn")
            dve.reg_mov(turn, 0)
            for j in range(NT):
                lo = dve.value_load(range_i[0:1, 0, j:j + 1], min_val=0, max_val=GROUPS - 1)
                hi = dve.value_load(range_i[0:1, 1, j:j + 1], min_val=1, max_val=GROUPS)
                with dve.Fori(lo, hi) as group:
                    dve.reg_add(turn, turn, 1)
                    k = dve.snap(turn)
                    dve.wait_ge(group_used, k)
                    s = k % 2
                    for h in range(TB):
                        dve.tensor_scalar(oh_n[:, bass.ds(s, 1), h, :], iota_n[:], keys[:, 0, bass.ds(group, 1), h],
                                          None, ALU.is_equal)
                        last = dve.tensor_scalar(oh_m[:, bass.ds(s, 1), h, :], iota_m[:],
                                                 key_m[:, j, bass.ds(group, 1), h], None, ALU.is_equal)
                    last.then_inc(one_hot, 1)
                if j == 0:
                    dve.wait_ge(dve_own, sel_q_made)
                    dve.wait_ge(att_col_ready, 2)
                    a = sel_att[:].rearrange("p l g r q -> p (l g r) q")
                    dve.tensor_tensor(a, att_col[:].rearrange("p l g r -> p (l g r)").unsqueeze(2).to_broadcast([128, 2 * NG * REL, QI]),
                                      sel_q[:].unsqueeze(1).to_broadcast([128, 2 * NG * REL, QI]), ALU.mult).then_inc(sel_ready, 1)
                    dve.wait_ge(gate_w_hi, 1)
                    gate_ps = ps[:, 5, 64:64 + 2 * KT * REL]
                    dve.tensor_tensor(gate_lo[:].rearrange("p l t r -> p (l t r)"), gate_ps,
                                      gate_hi[:].rearrange("p l t r -> p (l t r)").bitcast(F32), ALU.subtract).then_inc(gate_w_ready, 1)
                if j == 2:
                    for c in range(2):
                        dve.wait_ge(wt_hi_done, c + 1)
                        dve.tensor_tensor(wt_lo[:, 2 * c:2 * c + 2, :], ps[:, 5 + c, :].rearrange("p (t m) -> p t m", t=2),
                                          wt_hi[:, 2 * c:2 * c + 2, :].bitcast(F32), ALU.subtract).then_inc(wt_ready, 1)

            def halves(b):
                return ps[:, b:b + 2, 0:HALF]

            def in_halves(ap):
                return ap.rearrange("p (h m) -> p h m", h=2)

            def project(z):
                for c in range(KT):
                    i = KT * z + c
                    if z and c == 0:
                        dve.wait_ge(ksum_mm, 1)
                        dve.tensor_copy(ksum[:], ps[0:TP, 2, M:2 * M]).then_inc(ksum_ready, 1)
                    if c:
                        dve.wait_ge(sq_ready, i + 1)
                        if c >= 2:
                            dve.wait_ge(sq_summed, (KT - 1) * z + c - 1)
                        dve.tensor_tensor(sq_sum[:], sq_sum[:], square[:], ALU.add).then_inc(sq_summed, 1)
                    dve.wait_ge(kq_hi_done, i + 1)
                    dve.scalar_tensor_tensor(out=in_halves(kq_lo[:, c, :]), in0=halves((0, 5)[c % 2]),
                                             scalar=colv[:, C_BK + i:C_BK + i + 1],
                                             in1=in_halves(kq_hi[:, c, :]).bitcast(F32),
                                             op0=ALU.add, op1=ALU.subtract).then_inc(kq_ready, 1)
                dve.wait_ge(xd_mm, z + 1)
                dve.tensor_copy(xd[:], ps[0:TP, 2, 0:NT]).then_inc(xd_ready, 1)
                for t in range(NT):
                    i = NT * z + t
                    dve.wait_ge(feat_exp, i + 1)
                    if z == 0:
                        dve.tensor_scalar(kp[:, t, :], feat[:, i % 2, :], 1.0 / 16, None, ALU.mult).then_inc(feat_ready, 1)
                    else:
                        dve.tensor_scalar(feat[:, i % 2, :], feat[:, i % 2, :], 1.0 / 16, None, ALU.mult).then_inc(feat_ready, 1)
                        dve.wait_ge(feat_ready, i + 1)
                        if t == 0:
                            dve.wait_ge(ksum_ready, 1)
                        dve.tensor_tensor(qk[:], feat[:, i % 2, :], ksum[:], ALU.mult).then_inc(d_part, 1)
                        dve.wait_ge(d_part, t + 1)
                        own_step(dve.tensor_reduce(d_sum[:, t:t + 1], qk[:], AX.X, ALU.add))
                        if t == 0:
                            own_step(dve.memset(qpt[:, :, NODES:NPAD], 0.0))
                        dve.wait_ge(qp_t, t + 1)
                        dve.tensor_copy(qpt[:, :, t * TP:(t + 1) * TP],
                                        ps[:, (0, 1)[t % 2], 0:2 * TP].rearrange("p (c m) -> p c m", c=2)).then_inc(qpt_ready, 1)
            project(0)
            dve.wait_ge(count_bound, 1)
            own_step(dve.tensor_reduce(count_max[0:1, 0:1], count_max[0:1, :], AX.X, ALU.max))
            own_step(dve.tensor_scalar(count_max[0:1, 1:2], count_max[0:1, 0:1], float(EXACT), None, ALU.is_gt))
            dve.tensor_copy(many_i[:], count_max[0:1, 1:2]).then_inc(many_ready, 1)
            project(1)
            for t in range(NT):
                dve.wait_ge(v_mm, t + 1)
                dve.wait_ge(smalls_in, 16 * 6)
                dve.tensor_tensor(v[:, t, :], ps[0:TP, (6, 5)[t % 2], :], bias_row[0:TP, 2, :], ALU.add).then_inc(v_ready, 1)
            dve.wait_ge(v_ready, NT)
            dve.wait_ge(feat_mm, 2 * NT)
            for t in range(NT):
                dve.tensor_tensor(y[:, t, :], v[:, t, :], bias_row[0:TP, 3, :], ALU.add).then_inc(dve_own, 1)
                n[0] += 1
            dve.wait_ge(qp_hi_done, 1)
            dve.tensor_tensor(qp_lo, qpt[:], qp_hi.bitcast(F32), ALU.subtract).then_inc(qp_ready, 1)
            dve.wait_ge(kv_mm, 1)
            dve.wait_ge(kv_hi_done, 1)
            dve.tensor_tensor(kvt_lo[:].rearrange("p (b c) m -> p b (c m)", b=2), ps[:, 0:2, :],
                              kvt_hi[:].rearrange("p (b c) m -> p b (c m)", b=2).bitcast(F32), ALU.subtract).then_inc(kv_ready, 1)
            own_step(dve.tensor_scalar(rec[:], d_sum[:], 1e-8, None, ALU.add))
            own_step(dve.reciprocal(rec[:], rec[:]))
            dve.wait_ge(kvw_hi_done, 1)
            dve.tensor_tensor(kvw_lo[:], ps[:, 5:7, :], kvw_hi[:].bitcast(F32), ALU.subtract).then_inc(kvw_ready, 1)
            dve.wait_ge(dve_own, n[0])

            def normalise_y(t):
                dve.wait_ge(rstd_ready, 2 + t + 1)
                if t >= 2:
                    dve.wait_ge(h2_t, t - 1)
                normalise(yn[:, t % 2, :], y[:, t, :], t).then_inc(yn_ready, 1)
            for t in range(NT):
                dve.wait_ge(wo_mm, t + 1)
                own_step(dve.scalar_tensor_tensor(out=y[:, t, :], in0=ps[0:TP, AGG[t], :], scalar=rec[:, t:t + 1],
                                                  in1=y[:, t, :], op0=ALU.mult, op1=ALU.add))
                stats(y[:, t, :], t)
                add_eps(t)
                if t in (1, 2):
                    normalise_y(t - 1)
            normalise_y(2)
            normalise_y(3)
            for t in range(NT):
                dve.wait_ge(h2_hi_done, t + 1)
                dve.tensor_tensor(h2t_lo[:, :, t * TP:(t + 1) * TP], h2_tmp[t % 2][:], h2t_hi[:, :, t * TP:(t + 1) * TP].bitcast(F32),
                                  ALU.subtract).then_inc(h2t_ready, 1)
                if t == 1:
                    normalise_y(4)
            for c in range(KT):
                dve.wait_ge(act_done, c + 1)
                own_step(dve.tensor_copy(act_hi[:, c, :], act_tmp[:, c % 2, :]))
                dve.tensor_tensor(act_lo[:, c, :], act_tmp[:, c % 2, :], act_hi[:, c, :].bitcast(F32), ALU.subtract).then_inc(act_ready, 1)

            def rest_of_transposed(i, t):
                dve.wait_ge(hT_hi, i + 1)
                dve.tensor_tensor(ht_lo[:, :, t * TP:(t + 1) * TP], ps[:, LB[t % 2], 0:KT * TP].rearrange("p (t m) -> p t m", t=KT),
                                  ht_hi[:, :, t * TP:(t + 1) * TP].bitcast(F32), ALU.subtract).then_inc(hT_ready, 1)
            for t in range(NT):
                dve.wait_ge(w2_mm, t + 1)
                dve.wait_ge(y_plus_b, t + 1)
                dve.tensor_tensor(y[:, t, :], ps[0:TP, AGG[t], :], y[:, t, :], ALU.add).then_inc(xm_ready, 1)
                rest_of_transposed(t, t)

            many = dve.value_load(many_i[0:1, 0:1], min_val=0, max_val=1)

            def messages(l):
                dve.wait_ge(gates_ready, l + 1)
                for r in range(REL):
                    a = 2 * l + r
                    for t in range(NT):
                        i = a * NT + t
                        dve.wait_ge(u_hi_done, i + 1)
                        dve.scalar_tensor_tensor(out=u_lo[l][:, t, :], in0=ps[0:TP, u_bank(i), :], scalar=gates[:, t, r:r + 1],
                                                 in1=u_hi[l][:, t, :].bitcast(F32), op0=ALU.mult, op1=ALU.subtract).then_inc(u_ready, 1)
                    with dve.If(many):
                        dve.wait_ge(cf_ready, (a + 1) * NT)
                        last = dve.tensor_tensor(cf[:], counts[:, :, r * CW:(r + 1) * CW], cf[:].bitcast(F32), ALU.subtract)
                        last.then_inc(rest_ready, 1)
                        dve.wait_ge(rest_used, a + 1)
                        dve.tensor_copy(cf[:], counts[:, :, r * CW:(r + 1) * CW]).then_inc(rest_ready, 1)

            messages(0)
            for t in range(NT):
                dve.wait_ge(agg_done, t + 1)
                if t >= 2:
                    dve.wait_ge(hT_t, NT + t - 1)
                dve.tensor_tensor(row_tmp[:, t % 2, :], ps[0:TP, AGG[t], :], bias_row[0:TP, 0, :], ALU.add).then_inc(h_added, 1)
                if t >= 2:
                    rest_of_transposed(NT + t - 2, t - 2)
            for t in (NT - 2, NT - 1):
                rest_of_transposed(NT + t, t)

            messages(1)

            def x1_of(t):
                dve.wait_ge(agg_done, NT + t + 1)
                dve.wait_ge(xm_plus_x, t + 1)
                if t == 0:
                    dve.wait_ge(split_done, PIECE["rel2_1"] + 1)
                own_step(dve.tensor_tensor(x1[:, t, :], ps[0:TP, AGG[t], :], y[:, t, :], ALU.add))
                stats(x1[:, t, :], t)
                add_eps(t)

            def x1_rest(t):
                dve.wait_ge(x1_hi_done, t + 1)
                dve.tensor_tensor(x1t_lo[:, :, t * TP:(t + 1) * TP], ps[:, AGG[t], 0:KT * TP].rearrange("p (t m) -> p t m", t=KT),
                                  x1t_hi[:, :, t * TP:(t + 1) * TP].bitcast(F32), ALU.subtract).then_inc(x1t_ready, 1)
            for t in range(NT + 3):
                if t < NT:
                    x1_of(t)
                if t >= 3:
                    x1_rest(t - 3)
            hidden_done = [0]

            def gate_hidden(e, h):
                n_th = HID_AT[e, h]
                dve.wait_ge(hid_ready, n_th + 1)
                source = hid[:, n_th % HB, :]
                if e:
                    if h == 0:
                        for k, (a, b) in enumerate(BACK):
                            if e - 1 == a:
                                dve.wait_ge(route_back[k], 16)
                    target = gated[:, hidden_done[0] % 4, :]
                    own_step(dve.tensor_tensor(target, source, route_all[:, e - 1, h * HALF:(h + 1) * HALF], ALU.mult))
                    source = target
                if e >= 2 and h == 0:
                    dve.wait_ge(ex_used, e - 1)
                hi, lo = (a[:, e % 2, h * HALF:(h + 1) * HALF] for a in (hg_hi, hg_lo))
                own_step(dve.tensor_copy(hi, source))
                dve.tensor_tensor(lo, source, hi.bitcast(F32), ALU.subtract).then_inc(hg_ready, 1)
                hidden_done[0] += 1

            gate_hidden(0, 0)
            dve.wait_ge(logit_t, 1)
            own_step(dve.tensor_copy(logit[:].rearrange("p t b e -> p (t b e)"), ps[0:TP, 2, 0:NT * 2 * E]))
            lg = logit[:].rearrange("p t b e -> p (t b) e")

            def over(ap):
                return ap.rearrange("p t b -> p (t b)").unsqueeze(2).to_broadcast([TP, 2 * NT, E])

            def flat(a):
                return a[:].rearrange("p t b e -> p (t b) e")
            own_step(dve.tensor_reduce(lmax[:].rearrange("p t b -> p (t b)"), lg, AX.X, ALU.max))
            dve.tensor_tensor(flat(shifted), lg, over(lmax[:]), ALU.subtract).then_inc(shift_ready, 1)
            own_step(dve.tensor_tensor(flat(score), lg, over(lmax[:]), ALU.is_equal))
            own_step(dve.tensor_tensor(flat(score), flat(score), flat(rank), ALU.mult))
            own_step(dve.tensor_reduce(best[:].rearrange("p t b -> p (t b)"), flat(score), AX.X, ALU.max))
            own_step(dve.tensor_tensor(flat(route), flat(score), over(best[:]), ALU.is_equal))
            dve.wait_ge(expo_ready, 1)
            own_step(dve.tensor_reduce(denom[:].rearrange("p t b -> p (t b)"), flat(expo), AX.X, ALU.add))
            own_step(dve.reciprocal(gate_p[:], denom[:]))
            dve.tensor_tensor(flat(route), flat(route), over(gate_p[:]), ALU.mult).then_inc(route_ready, 1)
            own_step(dve.memset(route_t[:, NODES:NPAD], 0.0))
            dve.wait_ge(route_tr, 1)
            own_step(dve.tensor_copy(route_t[:, 0:4 * TP], ps[0:2 * E, 5, 0:4 * TP]))
            dve.tensor_copy(route_t[:, 4 * TP:NODES], ps[0:2 * E, 6, 0:TP]).then_inc(route_t_ready, 1)
            gate_hidden(0, 1)
            for e in range(1, NX):
                for h in range(2):
                    gate_hidden(e, h)
            for t in range(NT):
                dve.wait_ge(ffn_mm, t + 1)
                dve.wait_ge(x1_plus_b, t + 1)
                if t >= 2:
                    dve.wait_ge(stored[t % 2], 16 * (t // 2))
                dve.tensor_tensor(final[:, t % 2, :], ps[0:TP, AGG[t], :], x1[:, t, :], ALU.add).then_inc(final_ready, 1)

        @block.scalar
        def _(act):
            def halves(b):
                return ps[:, b:b + 2, 0:HALF]

            def in_halves(ap):
                return ap.rearrange("p (h m) -> p h m", h=2)

            def evac_relation(ch):
                act.wait_ge(rel_sum, ch + 1)
                if ch >= 2:
                    act.wait_ge(rel_out[ch % 2], 16 * (ch // 2))
                act.activation(stag[:, ch % 2, :], ps[:, rel_bank(ch), :], ACT.Copy).then_inc(rel_evac, 1)

            act.wait_ge(att_in, 32)
            for l in range(2):
                last = act.activation(att_rep[:, l, :].rearrange("r (b q) -> r b q", q=QI),
                                      att_rows[:, l, :].unsqueeze(2).to_broadcast([REL, BASES, QI]), ACT.Copy)
            last.then_inc(att_ready, 1)
            act.wait_ge(gate_rows_t, 1)
            act.wait_ge(consts_ready, 5)
            n_all = (BASES - (NG - 1) * GB) * QI
            act.activation(att_col[0:n_all].rearrange("p l g r -> p (l g r)"), ps[0:n_all, 5, 96:96 + 2 * NG * REL],
                           ACT.Copy).then_inc(att_col_ready, 1)
            act.activation(att_col[n_all:128, :, 0:NG - 1, :].rearrange("p l g r -> p l (g r)"),
                           ps[n_all:128, 5, 96:96 + 2 * NG * REL].rearrange("p (l g) -> p l g", l=2)[:, :, 0:(NG - 1) * REL],
                           ACT.Copy).then_inc(att_col_ready, 1)
            act.activation(colv[:], ps[:, 5, 0:45], ACT.Copy).then_inc(cols_ready, 1)
            act.activation(gate_hi[:].rearrange("p l t r -> p (l t r)"), ps[:, 5, 64:64 + 2 * KT * REL], ACT.Copy).then_inc(gate_w_hi, 1)
            def layer_norm(k, source, target, ready):
                for t in range(NT):
                    last = act.activation(xn2[:, t, :], source[:, t, :], ACT.Copy, accum_out=mean_acc[:, k, t:t + 1])
                last.then_inc(mean_sum, 1)
                act.wait_ge(minus_mean_ready, k + 1)
                for t in range(NT):
                    last = act.activation(xn2[:, t, :], source[:, t, :], ACT.Square, bias=minus_mean[:, k, t:t + 1],
                                          accum_out=square_acc[:, k, t:t + 1])
                last.then_inc(square_sum, 1)
                act.wait_ge(rstd_ready, k + 1)
                for t in range(NT):
                    act.activation(target[:, t, :], source[:, t, :], ACT.Identity, bias=shift[:, k, t:t + 1],
                                   scale=rstd_x[:, k, t:t + 1]).then_inc(ready, 1)

            def read_counts(j):
                act.wait_ge(count_mm, j + 1)
                for r in range(REL):
                    for h in range(2):
                        i = (j * REL + r) * 2 + h
                        last = act.activation(counts[:, j, r * CW + h * CB:r * CW + (h + 1) * CB], ps[0:TP, COUNT_BANK[r][h], 0:CB],
                                              ACT.Copy, accum_out=count_acc[:, i:i + 1])
                last.then_inc(count_ready, 1)

            def scaled(target, bank, column_g, column_b):
                for c in range(KT):
                    last = act.activation(target[:, c, :], ps[:, bank, c * TP:(c + 1) * TP], ACT.Identity,
                                          bias=colv[:, column_b + c:column_b + c + 1], scale=colv[:, column_g + c:column_g + c + 1])
                return last

            def scale_xt(t):
                act.wait_ge(xt_t, t + 1)
                if t >= 2:
                    act.wait_ge(xt_ready, t - 1)
                if t == 0:
                    act.wait_ge(cols_ready, 1)
                scaled(xt_tmp[t % 2], 5 + t % 2, C_G1, C_BE1).then_inc(xt_scaled, 1)
                act.wait_ge(xt_scaled, t + 1)
                act.activation(xt_hi[:, :, t * TP:(t + 1) * TP], xt_tmp[t % 2][:], ACT.Copy).then_inc(xt_hi_done, 1)
            act.wait_ge(x_in, 16)
            layer_norm(0, xa, xn, xn_ready)
            read_counts(0)
            evac_relation(0)
            act.wait_ge(xn_ready, NT)
            layer_norm(1, xn, xn2, xn2_ready)
            read_counts(1)
            for c in range(2):
                act.wait_ge(wt_t, c + 1)
                act.activation(wt_hi[:, 2 * c:2 * c + 2, :], ps[:, 5 + c, :].rearrange("p (t m) -> p t m", t=2),
                               ACT.Copy).then_inc(wt_hi_done, 1)
            evac_relation(1)
            read_counts(2)
            evac_relation(2)
            for t in range(2):
                scale_xt(t)
            read_counts(3)
            scale_xt(2)
            scale_xt(3)
            evac_relation(3)
            read_counts(4)
            scale_xt(4)
            evac_relation(4)
            evac_relation(5)

            def project(z):
                for c in range(KT):
                    i = KT * z + c
                    bias = colv[:, C_BK + i:C_BK + i + 1]
                    act.wait_ge(kq_mm, i + 1)
                    if c == 0:
                        target = sq_sum
                        if z:
                            act.wait_ge(xd_mm, 1)
                    else:
                        target = square
                        if z or c >= 2:
                            act.wait_ge(sq_summed, (KT - 1) * z + c - 1)
                    act.activation(in_halves(target[:]), halves((0, 5)[c % 2]), ACT.Square, bias=bias).then_inc(sq_ready, 1)
                    if z and c == 0:
                        act.wait_ge(feat_mm, NT)
                    act.activation(in_halves(kq_hi[:, c, :]), halves((0, 5)[c % 2]), ACT.Identity, bias=bias).then_inc(kq_hi_done, 1)
                evac_relation(6 + z)
                act.wait_ge(xd_ready, z + 1)
                for t in range(NT):
                    i = NT * z + t
                    act.wait_ge(feat_mm, i + 1)
                    if i >= 2:
                        if i >= NT + 2:
                            act.wait_ge(qp_t, i - NT - 1)
                            act.wait_ge(d_part, i - NT - 1)
                        else:
                            act.wait_ge(feat_ready, i - 1)
                    act.activation(feat[:, i % 2, :], ps[0:TP, (5, 6)[t % 2], 0:M], ACT.Exp, bias=xd[:, t:t + 1]).then_inc(feat_exp, 1)
            project(0)
            project(1)
            evac_relation(8)
            evac_relation(9)
            act.wait_ge(v_mm, NT)
            act.wait_ge(qpt_ready, NT)
            act.activation(qp_hi, qpt[:], ACT.Copy).then_inc(qp_hi_done, 1)
            act.wait_ge(kv_mm, 1)
            act.activation(kvt_hi[:].rearrange("p (b c) m -> p b (c m)", b=2), ps[:, 0:2, :], ACT.Copy).then_inc(kv_hi_done, 1)
            evac_relation(10)
            act.wait_ge(kvw_mm, 1)
            act.activation(kvw_hi[:], ps[:, 5:7, :], ACT.Copy).then_inc(kvw_hi_done, 1)
            evac_relation(11)
            for t in range(NT):
                act.wait_ge(h2_t, t + 1)
                if t >= 2:
                    act.wait_ge(h2t_ready, t - 1)
                if t == 0:
                    act.wait_ge(wo_mm, NT)
                scaled(h2_tmp[t % 2], (7, 2)[t % 2], C_G2, C_BE2).then_inc(h2_scaled, 1)
                act.wait_ge(h2_scaled, t + 1)
                act.activation(h2t_hi[:, :, t * TP:(t + 1) * TP], h2_tmp[t % 2][:], ACT.Copy).then_inc(h2_hi_done, 1)
            evac_relation(12)
            for c in range(KT):
                act.wait_ge(act_mm, c + 1)
                if c >= 2:
                    act.wait_ge(act_ready, c - 1)
                act.activation(in_halves(act_tmp[:, c % 2, :]), halves((0, 5)[c % 2]), ACT.Gelu,
                               bias=colv[:, C_B1 + c:C_B1 + c + 1]).then_inc(act_done, 1)
            evac_relation(13)

            def split_transposed(i, t):
                act.wait_ge(hT_t, i + 1)
                act.activation(ht_hi[:, :, t * TP:(t + 1) * TP], ps[:, LB[t % 2], 0:KT * TP].rearrange("p (t m) -> p t m", t=KT),
                               ACT.Copy).then_inc(hT_hi, 1)
            for t in range(NT):
                if t == 2:
                    evac_relation(14)
                split_transposed(t, t)

            def messages(l):
                act.wait_ge(gate_mm, l + 1)
                act.activation(in_halves(gate_row[:]), ps[0:REL, 0:2, 0:HALF], ACT.Sigmoid).then_inc(gate_row_ready, 1)
                act.wait_ge(gate_t, l + 1)
                act.activation(gates[:].rearrange("p t r -> p (t r)"), ps[0:TP, 2, 0:NT * REL], ACT.Copy).then_inc(gates_ready, 1)
                act.wait_ge(gates_ready, l + 1)
                for r in range(REL):
                    a = 2 * l + r
                    for t in range(NT):
                        if t == 0 and a == 0:
                            act.wait_ge(w2_mm, NT)
                            act.wait_ge(count_ready, NT)
                        elif t == 0:
                            act.wait_ge(rel_applied, a)
                        i = a * NT + t
                        act.activation(cf[:, t, :], counts[:, t, r * CW:(r + 1) * CW], ACT.Copy).then_inc(cf_ready, 1)
                        act.wait_ge(u_mm, i + 1)
                        act.activation(u_hi[l][:, t, :], ps[0:TP, u_bank(i), :], ACT.Copy, scale=gates[:, t, r:r + 1]).then_inc(u_hi_done, 1)
                    if a == 0:
                        evac_relation(15)

            messages(0)
            for t in range(NT):
                act.wait_ge(h_added, t + 1)
                act.activation(row_tmp[:, t % 2, :], row_tmp[:, t % 2, :], ACT.Relu).then_inc(h_relu, 1)
                if t >= 2:
                    split_transposed(NT + t - 2, t - 2)
            for t in (NT - 2, NT - 1):
                split_transposed(NT + t, t)
            messages(1)

            def expert_hi(e):
                act.wait_ge(ex_in[e % XR], 32 * (e // XR + 1))
                if e < 4:
                    act.wait_ge(piece_used, len(ORDER))
                else:
                    act.wait_ge(ex_used, e - 3)
                act.activation(ex_hi[:, e % 4], ex_raw[:, e % XR], ACT.Copy).then_inc(ex_hi_done, 1)

            def normalise_x1(t):
                act.wait_ge(x1_shift_ready, t + 1)
                if t >= 2:
                    act.wait_ge(x1_t, t - 1)
                act.activation(x1n[:, t % 2, :], x1[:, t, :], ACT.Identity, bias=x1_shift[:, t:t + 1],
                               scale=rstd[:, t:t + 1]).then_inc(x1n_ready, 1)

            def split_x1t(t):
                act.wait_ge(x1_t, t + 1)
                if t == 0:
                    act.wait_ge(u_mm, 4 * NT)
                act.activation(x1t_hi[:, :, t * TP:(t + 1) * TP], ps[:, AGG[t], 0:KT * TP].rearrange("p (t m) -> p t m", t=KT),
                               ACT.Copy).then_inc(x1_hi_done, 1)

            def gelu(n_th):
                e, _ = HIDDEN[n_th]
                act.wait_ge(hid_mm, n_th + 1)
                if n_th >= HB:
                    before_e, before_h = HIDDEN[n_th - HB]
                    act.wait_ge(hg_ready, 2 * before_e + before_h + 1)
                act.activation(hid[:, n_th % HB, :], ps[:, UB[n_th % 3], 0:HALF], ACT.Gelu,
                               bias=colv[:, C_EXP + e:C_EXP + e + 1]).then_inc(hid_ready, 1)
            for e in range(3):
                expert_hi(e)
            for t in range(NT):
                normalise_x1(t)
                if t:
                    split_x1t(t - 1)
            gelu(0)
            split_x1t(NT - 1)
            gelu(1)
            act.wait_ge(router_in, 16 * 4)
            act.wait_ge(logit_mm, 1)
            act.activation(in_halves(logit_row[:]), ps[0:2 * E, 0:2, 0:HALF], ACT.Identity, bias=router_b[:, 0:1]
                           ).then_inc(logit_row_ready, 1)
            gelu(2)
            expert_hi(3)
            act.wait_ge(shift_ready, 1)
            act.activation(expo[:].rearrange("p t b e -> p (t b e)"), shifted[:].rearrange("p t b e -> p (t b e)"),
                           ACT.Exp).then_inc(expo_ready, 1)
            gelu(3)
            for e in range(2, NX):
                gelu(2 * e)
                gelu(2 * e + 1)
                if e + 2 < NX:
                    expert_hi(e + 2)

        @block.tensor
        def _(pe):
            def mm3(target, a_hi, a_lo, b_hi, b_lo, first, last, skip=False):
                pe.matmul(target, a_hi, b_hi, start=first, stop=False, skip_group_check=skip)
                pe.matmul(target, a_hi, b_lo, start=False, stop=False, skip_group_check=skip)
                return pe.matmul(target, a_lo, b_hi, start=False, stop=last, skip_group_check=skip)

            part = [0]

            def relation_parts(count):
                for i in range(part[0], part[0] + count):
                    ch, g = divmod(i, NG)
                    nb = min(GB, BASES - g * GB)
                    slot, turn_ = basis_turn(i)
                    pe.wait_ge(basis_in[slot], 16 * turn_)
                    if g == 0 and ch >= 2:
                        pe.wait_ge(rel_evac, ch - 1 if ch < 2 * CHUNKS - 1 else ch)
                    for c in range(4):
                        last = pe.matmul(ps[32 * c:32 * c + 32, rel_bank(ch), :],
                                         sel_att[0:nb * QI, ch // CHUNKS, g].rearrange("p r q -> p (r q)"),
                                         ring[slot][0:nb * QI, c * D:(c + 1) * D], start=(g == 0), stop=(g == NG - 1))
                    last.then_inc(basis_used, 1)
                    if g == NG - 1:
                        pe.wait_ge(basis_used, i + 1)
                        pe.sem_inc(rel_sum, 1)
                part[0] += count

            pe.wait_ge(ident_ready, 1)
            pe.wait_ge(key_ready, 1)
            pe.transpose(ps[0:TE, 6, 0:ET], edge_f[:, 0, :], ident[0:ET, 0:ET])
            pe.transpose(ps[0:TE, 6, ET:2 * ET], key_r[:], ident[0:ET, 0:ET]).then_inc(keys_t, 1)
            pe.wait_ge(att_ready, 1)
            for l in range(2):
                for g in range(NG):
                    nb = min(GB, BASES - g * GB)
                    o = 96 + (l * NG + g) * REL
                    pe.transpose(ps[0:nb * QI, 5, o:o + REL],
                                 att_rep[:, l, g * GB * QI:(g * GB + nb) * QI],
                                 ident[0:REL, 0:REL])
            pe.wait_ge(rows_in, 16 * 11)
            pe.transpose(ps[:, 5, 0:45], row_vec[:], ident[0:45, 0:45])
            for l in range(2):
                for t in range(KT):
                    o = 64 + (l * KT + t) * REL
                    last = pe.transpose(ps[:, 5, o:o + REL], gate_rows[:, l, :].rearrange("r (i t) -> r t i", t=KT)[:, t],
                                        ident[0:REL, 0:REL])
            last.then_inc(gate_rows_t, 1)

            def turn_xt(t):
                pe.wait_ge(xn2_ready, t + 1)
                if t >= 2:
                    pe.wait_ge(xt_scaled, t - 1)
                else:
                    pe.wait_ge(wt_ready, t + 1)
                for c in range(KT):
                    last = pe.transpose(ps[:, 5 + t % 2, c * TP:(c + 1) * TP], xn2[:, t, c * 128:(c + 1) * 128], ident[0:TP, 0:TP])
                last.then_inc(xt_t, 1)

            pe.wait_ge(range_ready, 1)
            pe.wait_ge(consts_ready, 5)
            turn, all_used = pe.alloc_register("turn"), pe.alloc_register("all_used")
            pe.reg_mov(turn, 0)
            pe.sem_inc(group_used, 2)
            for j in range(NT):
                groups = pe.value_load(range_i[0:1, 2, j:j + 1], min_val=1, max_val=GROUPS)
                if j:
                    pe.wait_ge(count_ready, j)
                for b in COUNT_BANK[0] + COUNT_BANK[1]:
                    pe.matmul(ps[0:TP, b, 0:2], zeros[:], iota_n[:, 0:2], start=True, stop=False, skip_group_check=True)
                with pe.Fori(0, groups) as _group:
                    pe.reg_add(turn, turn, 1)
                    k = pe.snap(turn)
                    pe.wait_ge(one_hot, k)
                    s = k % 2
                    for u in range(TB):
                        for r in range(REL):
                            for h in range(2):
                                last = pe.matmul(ps[0:TP, COUNT_BANK[r][h], 0:CB],
                                                 oh_m[:, bass.ds(s, 1), u, r * TE:(r + 1) * TE],
                                                 oh_n[:, bass.ds(s, 1), u, CB * h:CB * (h + 1)],
                                                 start=False, stop=False, skip_group_check=True)
                    last.then_inc(group_used, 1)
                pe.reg_add(all_used, turn, 2)
                pe.wait_ge(group_used, pe.snap(all_used))
                pe.sem_inc(count_mm, 1)
                if j == 0:
                    pe.wait_ge(sel_ready, 1)
                if j == 1:
                    pe.wait_ge(w_in, 16)
                    pe.wait_ge(gate_w_ready, 1)
                    pe.wait_ge(cols_ready, 1)
                    for c in range(2):
                        for t in range(2):
                            for m in range(2):
                                o = t * M + m * 128
                                last = pe.transpose(ps[:, 5 + c, o:o + 128], w_nat[:, m, (2 * c + t) * 128:(2 * c + t + 1) * 128], ident[:])
                        last.then_inc(wt_t, 1)
                if j == 3:
                    turn_xt(2)
                    relation_parts(2)
                    turn_xt(3)
                    relation_parts(3)
                elif j == 4:
                    turn_xt(4)
                    relation_parts(NG + 1)
                else:
                    relation_parts(NG + (j > 0))
                    if j == 2:
                        turn_xt(0)
                        turn_xt(1)

            def project(z):
                s, p_hi, p_lo = piece("kq"[z])
                pe.wait_ge(split_done, s + 1)
                pe.wait_ge(xt_ready, NT)
                pe.wait_ge(consts_ready, 7)
                for c in range(KT):
                    i = KT * z + c
                    b = (0, 5)[c % 2]
                    if c >= 2:
                        pe.wait_ge(kq_ready, i - 1)
                    elif z == 0:
                        pe.wait_ge(count_ready, NT)
                        pe.wait_ge(wt_ready, 2)
                        pe.wait_ge(xt_scaled, NT)
                    elif c == 0:
                        pe.wait_ge(kq_ready, KT)
                    else:
                        pe.wait_ge(feat_exp, NT)
                    for k in range(KT):
                        for h in range(2):
                            last = mm3(ps[:, b + h, 0:HALF], p_hi[:, k, c * 128:(c + 1) * 128],
                                       p_lo[:, k, c * 128:(c + 1) * 128], xt_hi[:, k, h * HALF:(h + 1) * HALF],
                                       xt_lo[:, k, h * HALF:(h + 1) * HALF], k == 0, k == KT - 1)
                    last.then_inc(kq_mm, 1)
                    if z and c == 0:
                        pe.wait_ge(feat_ready, NT)
                        pe.wait_ge(xd_ready, 1)
                        for t in range(NT):
                            last = pe.matmul(ps[0:TP, 2, M:2 * M], ones[0:TP, 0:TP], kp[:, t, :], start=(t == 0), stop=(t == NT - 1))
                        last.then_inc(ksum_mm, 1)
                    if c:
                        relation_parts(1)
                pe.wait_ge(kq_mm, KT * (z + 1))
                pe.sem_inc(piece_used, 1)
                relation_parts(1)
                pe.wait_ge(kq_ready, KT * (z + 1))
                for t in range(NT):
                    i = NT * z + t
                    if t >= 2:
                        pe.wait_ge(feat_exp, i - 1)
                    for k in range(KT):
                        last = mm3(ps[0:TP, (5, 6)[t % 2], 0:M], kq_hi[:, k, t * TP:(t + 1) * TP], kq_lo[:, k, t * TP:(t + 1) * TP],
                                   wt_hi[:, k, :], wt_lo[:, k, :], k == 0, k == KT - 1)
                    last.then_inc(feat_mm, 1)
                    if t == 0:
                        half_norms(z)
                    if t in ((1, 3), (0, 1, 2, 4))[z]:
                        relation_parts(1)
                    if z and t:
                        turn_features(t - 1)

            def half_norms(z):
                pe.wait_ge(sq_summed, (KT - 1) * (z + 1))
                if z:
                    pe.wait_ge(xd_ready, 1)
                    pe.wait_ge(ksum_ready, 1)
                for t in range(NT):
                    last = pe.matmul(ps[0:TP, 2, t:t + 1], sq_sum[:, t * TP:(t + 1) * TP], neg_half[:], start=(t == 0),
                                     stop=(t == NT - 1), skip_group_check=True)
                last.then_inc(xd_mm, 1)

            def turn_features(t):
                pe.wait_ge(feat_ready, NT + t + 1)
                if t >= 2:
                    pe.wait_ge(qpt_ready, t - 1)
                for m in range(2):
                    last = pe.transpose(ps[:, (0, 1)[t % 2], m * TP:(m + 1) * TP], feat[:, (NT + t) % 2, m * 128:(m + 1) * 128],
                                        ident[0:TP, 0:TP])
                last.then_inc(qp_t, 1)

            project(0)
            project(1)
            s, p_hi, p_lo = piece("v")
            pe.wait_ge(split_done, s + 1)
            pe.wait_ge(feat_exp, 2 * NT)
            for t in range(NT):
                if t >= 2:
                    pe.wait_ge(v_ready, t - 1)
                for k in range(KT):
                    last = mm3(ps[0:TP, (6, 5)[t % 2], :], xt_hi[:, k, t * TP:(t + 1) * TP], xt_lo[:, k, t * TP:(t + 1) * TP],
                               p_hi[:, k, :], p_lo[:, k, :], k == 0, k == KT - 1)
                last.then_inc(v_mm, 1)
                if t == 0:
                    turn_features(NT - 1)
                relation_parts(1)
            pe.wait_ge(v_mm, NT)
            pe.sem_inc(piece_used, 1)
            pe.wait_ge(v_ready, NT)
            pe.wait_ge(qpt_ready, NT)
            pe.wait_ge(feat_ready, NT)
            pe.wait_ge(xd_ready, 2)
            for c in range(KT):
                for t in range(NT):
                    last = pe.matmul(ps[:, c // 2, c % 2 * M:(c % 2 + 1) * M], v[:, t, c * 128:(c + 1) * 128], kp[:, t, :],
                                     start=(t == 0), stop=(t == NT - 1))
                if c == 1:
                    relation_parts(1)
            last.then_inc(kv_mm, 1)
            relation_parts(2)
            s, p_hi, p_lo = piece("Wo")
            pe.wait_ge(split_done, s + 1)
            pe.wait_ge(kv_ready, 1)
            for m in range(2):
                for k in range(KT):
                    last = mm3(ps[:, 5 + m, :], kvt_hi[:, k, m * 128:(m + 1) * 128], kvt_lo[:, k, m * 128:(m + 1) * 128],
                               p_hi[:, k, :], p_lo[:, k, :], k == 0, k == KT - 1)
            last.then_inc(kvw_mm, 1)
            pe.wait_ge(kvw_mm, 1)
            pe.sem_inc(piece_used, 1)
            relation_parts(3)
            pe.wait_ge(kvw_ready, 1)
            pe.wait_ge(qp_ready, 1)
            for t in range(NT):
                for m in range(2):
                    last = mm3(ps[0:TP, AGG[t], :], qp_hi[:, m, t * TP:(t + 1) * TP], qp_lo[:, m, t * TP:(t + 1) * TP],
                               kvw_hi[:, m, :], kvw_lo[:, m, :], m == 0, m == 1)
                last.then_inc(wo_mm, 1)
                if t in (0, 2):
                    relation_parts(1)
            relation_parts(1)
            for t in range(NT):
                pe.wait_ge(yn_ready, t + 1)
                if t == 0:
                    pe.wait_ge(count_ready, NT)
                if t >= 2:
                    pe.wait_ge(h2_scaled, t - 1)
                for c in range(KT):
                    last = pe.transpose(ps[:, (7, 2)[t % 2], c * TP:(c + 1) * TP], yn[:, t % 2, c * 128:(c + 1) * 128], ident[0:TP, 0:TP])
                last.then_inc(h2_t, 1)
                relation_parts((0, 1, 0, 0, 1)[t])
            s, p_hi, p_lo = piece("W1")
            pe.wait_ge(split_done, s + 1)
            for c, h in ((0, 0), (1, 0), (0, 1), (1, 1), (2, 0), (2, 1), (3, 0), (3, 1)):
                if c >= 2:
                    pe.wait_ge(act_done, c - 1)
                pe.wait_ge(h2t_ready, (3, NT)[h])
                for k in range(KT):
                    last = mm3(ps[:, (0, 5)[c % 2] + h, 0:HALF], p_hi[:, k, c * 128:(c + 1) * 128],
                               p_lo[:, k, c * 128:(c + 1) * 128], h2t_hi[:, k, h * HALF:(h + 1) * HALF],
                               h2t_lo[:, k, h * HALF:(h + 1) * HALF], k == 0, k == KT - 1)
                if h:
                    last.then_inc(act_mm, 1)
                    relation_parts((1, 1, 1, 0)[c])
            pe.wait_ge(act_mm, KT)
            pe.sem_inc(piece_used, 1)

            def turn_layer_input(t, rows):
                for c in range(KT):
                    last = pe.transpose(ps[:, LB[t % 2], c * TP:(c + 1) * TP], rows.rearrange("p (i t) -> p t i", t=KT)[:, c],
                                        ident[0:TP, 0:TP])
                last.then_inc(hT_t, 1)

            def turn_xn(t):
                if t >= 2:
                    pe.wait_ge(hT_ready, t - 1)
                elif t == 0:
                    pe.wait_ge(xn_ready, NT)
                    pe.wait_ge(h2_scaled, NT)
                else:
                    pe.wait_ge(rel_evac, 2 * CHUNKS - 2)
                turn_layer_input(t, xn[:, t, :])
            turn_xn(0)
            relation_parts(1)
            s, p_hi, p_lo = piece("W2")
            pe.wait_ge(split_done, s + 1)
            pe.wait_ge(act_ready, KT)
            for t in range(NT):
                for k in range(KT):
                    last = mm3(ps[0:TP, AGG[t], :], act_hi[:, k, t * TP:(t + 1) * TP], act_lo[:, k, t * TP:(t + 1) * TP],
                               p_hi[:, k, :], p_lo[:, k, :], k == 0, k == KT - 1)
                last.then_inc(w2_mm, 1)
                if t + 1 < NT:
                    turn_xn(t + 1)
                relation_parts(1)
            pe.wait_ge(w2_mm, NT)
            pe.sem_inc(piece_used, 1)
            many = pe.alloc_register("many")

            def layer(l):
                def messages_tile(r, t, p_hi, p_lo):
                    i = (2 * l + r) * NT + t
                    if l == 0 and i >= 2:
                        pe.wait_ge(u_ready, i - 1)
                    if l == 1 and i >= 2 * NT + 3:
                        pe.wait_ge(u_ready, i - 2)
                    for c in range(KT):
                        last = mm3(ps[0:TP, u_bank(i), :], ht_hi[:, c, t * TP:(t + 1) * TP], ht_lo[:, c, t * TP:(t + 1) * TP],
                                   p_hi[:, c, :], p_lo[:, c, :], c == 0, c == KT - 1)
                    last.then_inc(u_mm, 1)

                if l == 0:
                    relation_parts(PARTS - part[0])
                    pe.wait_ge(xm_ready, 3)
                else:
                    s, p_hi, p_lo = piece("rel2_0")
                    pe.wait_ge(split_done, s + 1)
                    pe.wait_ge(rel_evac, 2 * CHUNKS)
                    messages_tile(0, 0, p_hi, p_lo)
                    turn_h(NT - 1)
                    pe.wait_ge(h_added, 3)
                    pe.wait_ge(hT_ready, 2 * NT - 1)
                if l == 0:
                    pe.wait_ge(hT_ready, NT)
                for h in range(2):
                    if h:
                        pe.wait_ge(hT_ready, NT * (l + 1))
                    for c in range(KT):
                        last = mm3(ps[0:REL, h, 0:HALF], gate_hi[:, l, c, :], gate_lo[:, l, c, :], ht_hi[:, c, h * HALF:(h + 1) * HALF],
                                   ht_lo[:, c, h * HALF:(h + 1) * HALF], c == 0, c == KT - 1)
                last.then_inc(gate_mm, 1)
                if l == 1:
                    messages_tile(0, 1, p_hi, p_lo)

                def turn_gates():
                    pe.wait_ge(gate_row_ready, l + 1)
                    for t in range(NT):
                        last = pe.transpose(ps[0:TP, 2, t * REL:(t + 1) * REL], gate_row[:, t * TP:(t + 1) * TP], ident[0:REL, 0:REL])
                    last.then_inc(gate_t, 1)
                for r in range(REL):
                    a = 2 * l + r
                    s, p_hi, p_lo = piece(f"rel{l + 1}_{r}")
                    pe.wait_ge(split_done, s + 1)
                    for t in range(NT):
                        if a != 2 or t >= 2:
                            messages_tile(r, t, p_hi, p_lo)
                        if r == 0 and t == (0, 1)[l]:
                            turn_gates()
                    pe.wait_ge(u_mm, (a + 1) * NT)
                    pe.sem_inc(piece_used, 1)
                    if r == 0:
                        s, p_hi, p_lo = piece(f"root{l + 1}")
                        pe.wait_ge(split_done, s + 1)
                        pe.wait_ge(gates_ready, l + 1)
                        pe.wait_ge((xm_ready, h_added)[l], NT)
                        for t in range(NT):
                            for c in range(KT):
                                last = mm3(ps[0:TP, AGG[t], :], ht_hi[:, c, t * TP:(t + 1) * TP], ht_lo[:, c, t * TP:(t + 1) * TP],
                                           p_hi[:, c, :], p_lo[:, c, :], c == 0, False)
                        last.then_inc(piece_used, 1)
                    def apply_counts(t, tiles, close):
                        last = None
                        for m in tiles:
                            for u in (u_hi[l], u_lo[l]):
                                last = pe.matmul(ps[0:TP, AGG[t], :], cf[:, m, t * TP:(t + 1) * TP], u[:, m, :], start=False,
                                                 stop=close and m == NT - 1 and u is u_lo[l])
                        return last
                    if a == 0:
                        pe.wait_ge(many_ready, 1)
                        pe.reg_mov(many, pe.value_load(many_i[0:1, 0:1], min_val=0, max_val=1))
                    with pe.If(many):
                        pe.wait_ge(rest_ready, 2 * a + 1)
                        for t in range(NT):
                            last = apply_counts(t, range(NT), False)
                        last.then_inc(rest_used, 1)
                        pe.wait_ge(rest_ready, 2 * a + 2)
                    pe.wait_ge(cf_ready, (a + 1) * NT - 1)
                    pe.wait_ge(u_ready, (a + 1) * NT - 1)
                    early = (NT - 1, 2, 0, 0, 0)
                    for t in range(NT):
                        apply_counts(t, range(early[t]), False)
                    pe.wait_ge(cf_ready, (a + 1) * NT)
                    pe.wait_ge(u_ready, (a + 1) * NT)
                    for t in range(NT):
                        last = apply_counts(t, range(early[t], NT), r == REL - 1)
                        if r == REL - 1:
                            last.then_inc(agg_done, 1)
                            if l == 0 and t >= 2:
                                turn_h(t - 2)
                            if l == 1 and t >= 3:
                                turn_x1(t - 3)
                    if r == 0:
                        last.then_inc(rel_applied, 1)
                    else:
                        pe.wait_ge(agg_done, (l + 1) * NT)
                        pe.sem_inc(rel_applied, 1)

            def turn_h(t):
                pe.wait_ge(h_relu, t + 1)
                if t >= 2:
                    pe.wait_ge(hT_ready, NT + t - 1)
                turn_layer_input(t, row_tmp[:, t % 2, :])

            def turn_x1(t):
                pe.wait_ge(x1n_ready, t + 1)
                for c in range(KT):
                    last = pe.transpose(ps[:, AGG[t], c * TP:(c + 1) * TP], x1n[:, t % 2, :].rearrange("p (f t) -> p t f", t=KT)[:, c],
                                        ident[0:TP, 0:TP])
                last.then_inc(x1_t, 1)

            layer(0)
            turn_h(NT - 2)
            layer(1)

            def router(h):
                pe.wait_ge(router_w_ready, 1)
                pe.wait_ge(x1t_ready, (3, NT)[h])
                for c in range(KT):
                    last = mm3(ps[0:2 * E, h, 0:HALF], router_hi[:, c, :], router_lo[:, c, :], x1t_hi[:, c, h * HALF:(h + 1) * HALF],
                               x1t_lo[:, c, h * HALF:(h + 1) * HALF], c == 0, c == KT - 1)
                return last

            def hidden(n_th):
                e, h = HIDDEN[n_th]
                pe.wait_ge(ex_split, e + 1)
                if n_th >= 3:
                    pe.wait_ge(hid_ready, n_th - 2)
                else:
                    pe.wait_ge(u_ready, 4 * NT)
                for k in range(KT):
                    last = mm3(ps[:, UB[n_th % 3], 0:HALF], ex_hi[:, e % 4, 0, k * FF:(k + 1) * FF], ex_lo[:, e % 4, 0, k * FF:(k + 1) * FF],
                               x1t_hi[:, k, h * HALF:(h + 1) * HALF], x1t_lo[:, k, h * HALF:(h + 1) * HALF], k == 0, k == KT - 1)
                last.then_inc(hid_mm, 1)
            turn_x1(2)
            turn_x1(3)
            router(0)
            hidden(0)
            turn_x1(4)
            hidden(1)
            router(1).then_inc(logit_mm, 1)
            hidden(2)
            pe.wait_ge(logit_row_ready, 1)
            for t in range(NT):
                last = pe.transpose(ps[0:TP, 2, t * 2 * E:(t + 1) * 2 * E], logit_row[:, t * TP:(t + 1) * TP], ident[0:2 * E, 0:2 * E])
            last.then_inc(logit_t, 1)
            hidden(3)
            hidden(4)
            pe.wait_ge(route_ready, 1)
            for t in range(4):
                pe.transpose(ps[0:2 * E, 5, t * TP:(t + 1) * TP], route[:, t].rearrange("p b e -> p (b e)"), ident[0:TP, 0:TP])
            pe.transpose(ps[0:2 * E, 6, 0:TP], route[:, 4].rearrange("p b e -> p (b e)"), ident[0:TP, 0:TP]).then_inc(route_tr, 1)
            hidden(5)
            pe.wait_ge(route_t_ready, 1)
            for e in range(NX):
                if e and e + 2 < NX:
                    hidden(2 * (e + 2))
                    hidden(2 * (e + 2) + 1)
                pe.wait_ge(hg_ready, 2 * e + 2)
                for t in range(NT):
                    last = mm3(ps[0:TP, AGG[t], :], hg_hi[:, e % 2, t * TP:(t + 1) * TP], hg_lo[:, e % 2, t * TP:(t + 1) * TP],
                               ex_hi[:, e % 4, 1, :], ex_lo[:, e % 4, 1, :], e == 0, False)
                last.then_inc(ex_used, 1)
            pe.wait_ge(route_split, 1)
            for t in range(NT):
                last = mm3(ps[0:TP, AGG[t], :], route_hi[:, t * TP:(t + 1) * TP], route_lo[:, t * TP:(t + 1) * TP],
                           out_b_hi[:], out_b_lo[:], False, True)
                last.then_inc(ffn_mm, 1)


_INS = ['x', 'src', 'dst', 'edge_type_2', 'L0_gnn_basis1', 'L0_gnn_att1', 'L0_gnn_gate_w1', 'L0_gnn_root1',
        'L0_gnn_bias1', 'L0_gnn_basis2', 'L0_gnn_att2', 'L0_gnn_gate_w2', 'L0_gnn_root2', 'L0_gnn_bias2',
        'L0_mix_w', 'L0_mix_Wkqv', 'L0_mix_bkqv', 'L0_mix_Wo', 'L0_mix_bo', 'L0_mix_W1', 'L0_mix_b1',
        'L0_mix_W2', 'L0_mix_b2', 'L0_mix_g1', 'L0_mix_be1', 'L0_mix_g2', 'L0_mix_be2', 'L0_ffn_Wr_sp',
        'L0_ffn_br_sp', 'L0_ffn_Wr_fq', 'L0_ffn_br_fq', 'L0_ffn_Ws1', 'L0_ffn_bs1', 'L0_ffn_Ws2',
        'L0_ffn_bs2', 'L0_ffn_W1_sp', 'L0_ffn_b1_sp', 'L0_ffn_W2_sp', 'L0_ffn_b2_sp', 'L0_ffn_W1_fq',
        'L0_ffn_b1_fq', 'L0_ffn_W2_fq', 'L0_ffn_b2_fq']
_OUTS = [((NODES, D), 'float32')]


def kernel(**inputs):
    import numpy as _np
    import concourse.bacc as _bacc
    from concourse import mybir as _mybir
    from concourse.bass_utils import run_bass_kernel_spmd as _run

    nc = _bacc.Bacc("TRN2", target_bir_lowering=False, num_devices=1)
    arrays, args = {}, []
    for name in _INS:
        a = _np.ascontiguousarray(inputs[name])
        arrays[f"in_{name}_dram"] = a
        args.append(nc.dram_tensor(f"in_{name}_dram", a.shape, _mybir.dt.from_np(a.dtype), kind="ExternalInput").ap())
    for i, (shape, dtype) in enumerate(_OUTS):
        dt = _mybir.dt.from_np(_np.dtype(dtype))
        args.append(nc.dram_tensor(f"out_{i}_dram", shape, dt, kind="ExternalOutput").ap())
    gnn_mix_ffn(nc, *args)
    r = _run(nc, [arrays], core_ids=[0])
    return r.results[0]["out_0_dram"]
```
